# Optimizing a Trainium2 kernel written in Bass

```python
import numpy as np
import jax
import jax.numpy as jnp

def _softmax(x, axis=-1):
    return jax.nn.softmax(x, axis=axis)

def _gelu(x):
    return jax.nn.gelu(x, approximate=True)

def _silu(x):
    return jax.nn.silu(x)

def _sigmoid(x):
    return jax.nn.sigmoid(x)

def _layernorm(x, axis=-1, eps=1e-05):
    m = jnp.mean(x, axis=axis, keepdims=True)
    v = jnp.var(x, axis=axis, keepdims=True)
    return (x - m) / jnp.sqrt(v + eps)

def _scatter_add(tgt, idx, src, axis=0):
    return tgt.at[idx].add(src)

def _segment_sum(src, seg, n):
    return jax.ops.segment_sum(src, seg, n)
kernel_name = 'mk_gnn_ffn_d1_gnn_r8_3fff4c'

def setup_inputs(seed: int=0):
    np.random.seed(seed)
    _w = jnp.asarray

    def _rec_inputs():
        import jax
        import jax.numpy as jnp
        _gk = jax.random.key(seed)
        x = -0.0003713 + 1 * jax.random.normal(jax.random.fold_in(_gk, 1), (12500, 256), jnp.float32)
        _s = jax.random.randint(jax.random.fold_in(_gk, 2), (100000,), 0, 12500, jnp.int32)
        _d = jax.random.randint(jax.random.fold_in(_gk, 3), (100000,), 0, 12500, jnp.int32)
        _loop = jnp.arange(12500, dtype=jnp.int32)
        src = jnp.concatenate([_s, _d, _loop])
        dst = jnp.concatenate([_d, _s, _loop])
        _o = jnp.argsort(dst, stable=True)
        src = src[_o]
        dst = dst[_o]
        edge_type_8 = jax.random.randint(jax.random.fold_in(_gk, 12), (212500,), 0, 8, jnp.int32)
        return (x, src, dst, edge_type_8)
    x, src, dst, edge_type_8 = _rec_inputs()

    def _L0_gnn_setup():
        import jax, jax.numpy as jnp
        import numpy as np
        N = 6250
        E = 100000
        DIN = 256
        DOUT = 256
        R = 8
        key = jax.random.key(seed)
        k1, k2, k3, k4, k5, k6 = jax.random.split(key, 6)
        h = jax.random.normal(k1, (N, DIN), dtype=jnp.float32)
        weight = jax.random.normal(k2, (R, DIN, DOUT), dtype=jnp.float32) * (1.0 / np.sqrt(DIN))
        sl_w = jax.random.normal(k3, (DOUT, DIN), dtype=jnp.float32) * (1.0 / np.sqrt(DIN))
        sl_b = jax.random.normal(k4, (DOUT,), dtype=jnp.float32) * 0.01
        edge_index = jax.random.randint(k5, (2, E), 0, N, dtype=jnp.int32)
        edge_type = jax.random.randint(k6, (E,), 0, R, dtype=jnp.int32)
        return {'h': h, 'weight': weight, 'sl_w': sl_w, 'sl_b': sl_b, 'edge_index': edge_index, 'edge_type': edge_type, 'num_nodes': N}
    _L0_gnn_all = _L0_gnn_setup()
    _L0_gnn_in = {k: v for k, v in _L0_gnn_all.items() if k in ('weight', 'sl_w', 'sl_b')}
    del _L0_gnn_all

    def _L0_ffn_setup():
        import jax, jax.numpy as jnp
        import numpy as np
        DIM = 256
        H = 8
        D = 64
        G = 64
        INNER = H * D
        SCALE = D ** (-0.5)
        key = jax.random.key(seed)
        ks = jax.random.split(key, 12)
        B, N = (4, 2048)
        x = jax.random.normal(ks[0], (B, N, DIM), dtype=jnp.float32)
        s = lambda fan_in: 1.0 / np.sqrt(fan_in)
        W_fx = jax.random.normal(ks[1], (DIM, INNER), dtype=jnp.float32) * s(DIM)
        b_fx = jnp.zeros((INNER,), dtype=jnp.float32)
        W_x = jax.random.normal(ks[2], (DIM, INNER), dtype=jnp.float32) * s(DIM)
        b_x = jnp.zeros((INNER,), dtype=jnp.float32)
        A = jax.random.normal(ks[3], (G, D), dtype=jnp.float32)
        Q, _ = jnp.linalg.qr(A.T)
        W_slice = Q[:, :G].astype(jnp.float32)
        b_slice = jnp.zeros((G,), dtype=jnp.float32)
        W_q = jax.random.normal(ks[4], (D, D), dtype=jnp.float32) * s(D)
        W_k = jax.random.normal(ks[5], (D, D), dtype=jnp.float32) * s(D)
        W_v = jax.random.normal(ks[6], (D, D), dtype=jnp.float32) * s(D)
        W_out = jax.random.normal(ks[7], (INNER, DIM), dtype=jnp.float32) * s(INNER)
        b_out = jnp.zeros((DIM,), dtype=jnp.float32)
        temperature = jnp.ones((1, H, 1, 1), dtype=jnp.float32) * 0.5
        return {'x': x, 'W_fx': W_fx, 'b_fx': b_fx, 'W_x': W_x, 'b_x': b_x, 'W_slice': W_slice, 'b_slice': b_slice, 'W_q': W_q, 'W_k': W_k, 'W_v': W_v, 'W_out': W_out, 'b_out': b_out, 'temperature': temperature}
    _L0_ffn_all = _L0_ffn_setup()
    _L0_ffn_in = {k: v for k, v in _L0_ffn_all.items() if k in ('W_fx', 'b_fx', 'W_x', 'b_x', 'W_slice', 'b_slice', 'W_q', 'W_k', 'W_v', 'W_out', 'b_out', 'temperature')}
    del _L0_ffn_all
    return {'x': x, 'src': src, 'dst': dst, 'edge_type_8': edge_type_8, 'L0_gnn_weight': _L0_gnn_in['weight'], 'L0_gnn_sl_w': _L0_gnn_in['sl_w'], 'L0_gnn_sl_b': _L0_gnn_in['sl_b'], 'L0_ffn_W_fx': _L0_ffn_in['W_fx'], 'L0_ffn_b_fx': _L0_ffn_in['b_fx'], 'L0_ffn_W_x': _L0_ffn_in['W_x'], 'L0_ffn_b_x': _L0_ffn_in['b_x'], 'L0_ffn_W_slice': _L0_ffn_in['W_slice'], 'L0_ffn_b_slice': _L0_ffn_in['b_slice'], 'L0_ffn_W_q': _L0_ffn_in['W_q'], 'L0_ffn_W_k': _L0_ffn_in['W_k'], 'L0_ffn_W_v': _L0_ffn_in['W_v'], 'L0_ffn_W_out': _L0_ffn_in['W_out'], 'L0_ffn_b_out': _L0_ffn_in['b_out'], 'L0_ffn_temperature': _L0_ffn_in['temperature']}

def reference(x, src, dst, edge_type_8, L0_gnn_weight, L0_gnn_sl_w, L0_gnn_sl_b, L0_ffn_W_fx, L0_ffn_b_fx, L0_ffn_W_x, L0_ffn_b_x, L0_ffn_W_slice, L0_ffn_b_slice, L0_ffn_W_q, L0_ffn_W_k, L0_ffn_W_v, L0_ffn_W_out, L0_ffn_b_out, L0_ffn_temperature):
    import jax
    import jax.numpy as jnp

    def _L0_gnn_ref(h, weight, sl_w, sl_b, edge_index, edge_type, num_nodes):
        import jax, jax.numpy as jnp
        import numpy as np
        N = 6250
        E = 100000
        DIN = 256
        DOUT = 256
        R = 8
        src, dst = (edge_index[0], edge_index[1])
        hW = jnp.einsum('nd,rde->rne', h, weight)
        msg = hW[edge_type, src]
        m = jax.ops.segment_sum(msg, dst, num_segments=num_nodes)
        deg = jax.ops.segment_sum(jnp.ones_like(dst, dtype=h.dtype), dst, num_segments=num_nodes)
        deg = jnp.maximum(deg, 1.0)[:, None]
        return h @ sl_w.T + sl_b + m / deg

    def _L0_ffn_ref(x, W_fx, b_fx, W_x, b_x, W_slice, b_slice, W_q, W_k, W_v, W_out, b_out, temperature):
        import jax, jax.numpy as jnp
        import numpy as np
        DIM = 256
        H = 8
        D = 64
        G = 64
        INNER = H * D
        SCALE = D ** (-0.5)
        B, N, _ = x.shape
        fx_mid = (x @ W_fx + b_fx).reshape(B, N, H, D).transpose(0, 2, 1, 3)
        x_mid = (x @ W_x + b_x).reshape(B, N, H, D).transpose(0, 2, 1, 3)
        temp = jnp.clip(temperature, 0.1, 5.0)
        slice_weights = jax.nn.softmax((x_mid @ W_slice + b_slice) / temp, axis=-1)
        slice_norm = slice_weights.sum(axis=2)
        slice_token = jnp.einsum('bhnc,bhng->bhgc', fx_mid, slice_weights)
        slice_token = slice_token / (slice_norm[..., None] + 1e-05)
        q = slice_token @ W_q
        k = slice_token @ W_k
        v = slice_token @ W_v
        attn = jax.nn.softmax(jnp.einsum('bhgc,bhkc->bhgk', q, k) * SCALE, axis=-1)
        out_slice = jnp.einsum('bhgk,bhkc->bhgc', attn, v)
        out_x = jnp.einsum('bhgc,bhng->bhnc', out_slice, slice_weights)
        out_x = out_x.transpose(0, 2, 1, 3).reshape(B, N, INNER)
        return out_x @ W_out + b_out
    edge_index = jnp.stack([src, dst])
    x = x + _L0_gnn_ref(_layernorm(x, axis=-1), L0_gnn_weight, L0_gnn_sl_w, L0_gnn_sl_b, edge_index, edge_type_8, 12500)
    x = x + _L0_ffn_ref(_layernorm(x, axis=-1)[None], L0_ffn_W_fx, L0_ffn_b_fx, L0_ffn_W_x, L0_ffn_b_x, L0_ffn_W_slice, L0_ffn_b_slice, L0_ffn_W_q, L0_ffn_W_k, L0_ffn_W_v, L0_ffn_W_out, L0_ffn_b_out, L0_ffn_temperature)[0]
    return x

_drawn_inputs = setup_inputs


def setup_inputs(seed=0):
    import zlib

    import numpy as np

    out = dict(_drawn_inputs(seed))
    spreads = {'L0_ffn_b_fx': (0.0, 0.1),
     'L0_ffn_b_x': (0.0, 0.8),
     'L0_ffn_b_slice': (0.0, 0.8),
     'L0_ffn_b_out': (0.0, 0.1),
     'L0_ffn_temperature': (0.5, 0.6)}
    factors = {'L0_gnn_sl_b': 7.265,
     'L0_ffn_W_fx': 7.117,
     'L0_ffn_W_x': 8.0,
     'L0_ffn_W_slice': 8.0,
     'L0_ffn_W_q': 8.0,
     'L0_ffn_W_k': 8.0}
    for name, (base, spread) in spreads.items():
        noise = np.random.default_rng([zlib.crc32(name.encode()), seed]).standard_normal(out[name].shape)
        drawn = base * np.exp(spread * noise) if base else spread * noise
        out[name] = jnp.asarray(drawn.astype(out[name].dtype))
    for name, factor in factors.items():
        out[name] = (out[name] * factor).astype(out[name].dtype)
    return out
```

```python
from contextlib import ExitStack

import numpy as np
import concourse.bass as bass
from concourse import mybir

ALU = mybir.AluOpType
ACT = mybir.ActivationFunctionType
AX_X = mybir.AxisListType.X
F32 = mybir.dt.float32
BF16 = mybir.dt.bfloat16
I32 = mybir.dt.int32
U32 = mybir.dt.uint32
ENG = mybir.EngineType

P = 128
N, D, R, E = 12500, 256, 8, 212500
DH = D // P
EPS = 1e-5

TILES = -(-N // P)
NP = TILES * P
CH = 15
WIN = P
LOC = P // R
GROUP = CH * P
MG = 8
MC = MG * CH
GROUPS = -(-E // (GROUP * MG)) * MG
CHUNKS = GROUPS * CH
PREPS = GROUPS // MG
EP = GROUPS * GROUP
TPB = TILES // PREPS
assert TPB * PREPS == TILES and GROUPS % 2 == 0
PAD_TYPE = 64
MROWS = NP + 2 * P
TRASH = NP + P
MW = D + 1
MP = 264

H, C, G = 8, 64, 64
HG = H * G


def several(eng, n, body):
    body(0, True, False)
    with eng.Fori(1, n - 1) as i:
        body(i, False, False)
    body(n - 1, False, True)


def reused(turn, k, ring, per):
    if k >= ring:
        return turn * per + k - ring + 1
    return (turn - 1) * per + k + ring * ((per - 1 - k) // ring) + 1


def program(nc, x, src, dst, typ, w_rel, sl_w, sl_b, w_fx, b_fx, w_x, b_x, w_slice, b_slice,
            w_q, w_k, w_v, w_out, b_out, temp, out):
    table = nc.dram_tensor("table", (NP, D), F32, kind="Internal").ap()
    base = nc.dram_tensor("base", (NP, D), F32, kind="Internal").ap()
    sums = nc.dram_tensor("sums", (MROWS, MP), F32, kind="Internal").ap()
    starts = nc.dram_tensor("starts", (2, CHUNKS), I32, kind="Internal").ap()
    slices = nc.dram_tensor("slices", (NP, HG), F32, kind="Internal").ap()

    with ExitStack() as whole:
        def sb(scope, name, shape, dt=F32):
            return scope.enter_context(nc.sbuf_tensor(name, shape, dt))

        def ps(scope, name, shape, dt=F32):
            return scope.enter_context(nc.psum_tensor(name, shape, dt))

        live = []

        def sem(name):
            live.append(nc.alloc_semaphore(name=name))
            return live[-1]

        def release():
            nc.clear_and_free_semaphores(live)
            live.clear()
            nc.all_engine_barrier()

        passed = nc.alloc_semaphore(name="passed")

        ident = sb(whole, "ident", [P, P])
        ones = sb(whole, "ones", [P, P])
        with ExitStack() as graph:
            meta = sb(graph, "meta", [P, 5, CHUNKS])
            w_sb = sb(graph, "w_sb", [P, DH, R, D])
            start_row = sb(graph, "start_row", [1, 2, CHUNKS], I32)
            flag = sb(graph, "flag", [1, 1], I32)
            with ExitStack() as scope:
                prepare(nc, scope, sb, ps, sem, passed, x, src, dst, typ, w_rel, sl_w, sl_b, table, base,
                        sums, starts, ident, ones, meta, w_sb, start_row, flag)
            with ExitStack() as scope:
                aggregate(nc, scope, sb, ps, sem, passed, table, sums, ident, ones, meta, w_sb,
                          start_row, flag)
            release()
        x1 = sb(whole, "x1", [P, TILES, D])
        mean = sb(whole, "mean", [P, TILES])
        rstd = sb(whole, "rstd", [P, TILES])
        tok = sb(whole, "tok", [P, 4, D + 1])
        mix = sb(whole, "mix", [P, 4, D])
        with ExitStack() as scope:
            front_pass(nc, scope, sb, ps, sem, passed, base, sums, x1, mean, rstd)
        with ExitStack() as scope:
            slice_pass(nc, scope, sb, ps, sem, passed, w_x, b_x, w_slice, b_slice, b_out, temp, slices, ident, ones,
                       x1, mean, rstd, tok)
        with ExitStack() as scope:
            token_stage(nc, scope, sb, ps, sem, passed, w_fx, b_fx, w_q, w_k, w_v, w_out, ident, tok, mix)
        with ExitStack() as scope:
            output_pass(nc, scope, sb, ps, sem, passed, slices, out, ident, x1, mix)


def prepare(nc, scope, sb, ps, sem, passed, x, src, dst, typ, w_rel, sl_w, sl_b, table, base, sums, starts,
            ident, ones, meta, w_sb, start_row, flag):
    x_t = sb(scope, "p_x", [P, TPB, D])
    hn = sb(scope, "p_hn", [P, TPB, D])
    xb = sb(scope, "p_xb", [P, TPB, D])
    own = sb(scope, "p_own", [P, TPB, D])
    hT = sb(scope, "p_hT", [P, 2, DH, P])
    stats = sb(scope, "p_stats", [P, TPB, 6])
    mv = sb(scope, "p_mv", [P, TPB, 2])
    var = sb(scope, "p_var", [P, TPB])
    std = sb(scope, "p_std", [P, TPB])
    rstd = sb(scope, "p_rstd", [P, TPB])
    slw = sb(scope, "p_slw", [P, DH, D])
    slT = sb(scope, "p_slT", [P, DH, D])
    slb = sb(scope, "p_slb", [P, D])
    zero = sb(scope, "p_zero", [P, 2640])
    raw = sb(scope, "p_raw", [MC, 4, P], I32)
    rows = sb(scope, "p_rows", [MC, 4, P])
    key = sb(scope, "p_key", [MC, 2, P])
    junk = sb(scope, "p_junk", [MC, P])
    ow = sb(scope, "p_ow", [MC, 4])
    oi = sb(scope, "p_oi", [MC, 2], I32)
    over = sb(scope, "p_over", [MC, 3])
    bad = sb(scope, "p_bad", [MC, 3])
    bad_sum = sb(scope, "p_bad_sum", [MC, 3])
    bad_row = sb(scope, "p_bad_row", [MC, 1])
    first_of = sb(scope, "p_first_of", [MC, MG, CH])
    p_hT = ps(scope, "pp_hT", [P, 2, 512])
    p_own = ps(scope, "pp_own", [P, 2, 512])
    p_cols = ps(scope, "pp_cols", [P, 2, 512])
    p_small = ps(scope, "pp_small", [P, 512])

    const_ok = sem("const_ok")
    masks_ok = sem("masks_ok")
    weights_in = sem("weights_in")
    sl_turned = sem("sl_turned")
    sl_ready = sem("sl_ready")
    zero_ok = sem("zero_ok")
    zero_out = sem("zero_out")
    x_in = [sem(f"x_in{k}") for k in range(TPB)]
    stats_ok = sem("stats_ok")
    mv_ok = sem("mv_ok")
    var_ok = sem("var_ok")
    std_ok = sem("std_ok")
    rstd_ok = sem("rstd_ok")
    hn_ok = sem("hn_ok")
    xb_ok = sem("xb_ok")
    hT_ps = sem("hT_ps")
    hT_ok = sem("hT_ok")
    own_ps = sem("own_ps")
    own_ok = sem("own_ok")
    stored = [sem(f"stored{k}") for k in range(TPB)]
    raw_in = sem("raw_in")
    rows_ok = sem("rows_ok")
    base_ps = sem("base_ps")
    base_ok = sem("base_ok")
    w_ok = sem("w_ok")
    off_ok = sem("off_ok")
    key_half = sem("key_half")
    planes_ok = sem("planes_ok")
    bad_ok = sem("bad_ok")
    bad_added = sem("bad_added")
    cols_ps = sem("cols_ps")
    cols_ok = sem("cols_ok")
    starts_out = sem("starts_out")
    row_in = sem("row_in")
    bad_rowed = sem("bad_rowed")
    bad_ps = sem("bad_ps")
    flag_ok = sem("flag_ok")

    def edges(a, turn, shift=0):
        return a[bass.ds(turn * (MC * P) + shift, MC * P)].rearrange("(c p) -> c p", p=P)

    def tile(a, turn, k):
        return a[bass.ds(turn * (TPB * P) + k * P, P), :]

    with nc.Block() as block:
        @block.sync
        def _(sp):
            def load_x(turn, k):
                sp.dma_start(x_t[:, k, :], tile(x, turn, k)).then_inc(x_in[k], 16)

            def load_edges(turn):
                for n, (a, shift) in enumerate(((dst, 0), (typ, 0), (src, 0), (dst, 1))):
                    sp.dma_start(raw[:, n, :], edges(a, turn, shift)).then_inc(raw_in, 16)

            load_edges(0)
            for k in range(TPB):
                load_x(0, k)
            for h in range(DH):
                sp.dma_start(slw[:, h, :], sl_w[h * P:(h + 1) * P, :]).then_inc(weights_in, 16)
            sp.dma_start(slb[:, :], sl_b.rearrange("(a n) -> a n", a=1).to_broadcast((P, D))).then_inc(weights_in, 16)
            for h in range(DH):
                sp.dma_start(w_sb[:, h, :, :], w_rel[:, h * P:(h + 1) * P, :].rearrange("r p n -> p r n")).then_inc(weights_in, 16)
            sp.wait_ge(zero_ok, 1)
            flat = sums.rearrange("(p a) w -> p (a w)", p=P)
            for n in range(10):
                sp.dma_start(flat[:, n * 2640:(n + 1) * 2640], zero[:, :]).then_inc(zero_out, 16)

            def turn(i, first, last):
                sp.wait_ge(rows_ok, i + 1)
                if not last:
                    load_edges(i + 1)
                for k in range(TPB):
                    sp.wait_ge(hn_ok, i * TPB + k + 1)
                    sp.dma_start(tile(table, i, k), hn[:, k, :]).then_inc(stored[k], 16)
                    if not last:
                        sp.wait_ge(xb_ok, i * TPB + k + 1)
                        load_x(i + 1, k)
                sp.wait_ge(off_ok, i * 2 + 2)
                for n in range(2):
                    sp.dma_start(starts[n, bass.ds(i * MC, MC)].rearrange("(c a) -> c a", a=1), oi[:, n:n + 1]).then_inc(starts_out, 16)
                for k in range(TPB):
                    sp.wait_ge(own_ok, i * TPB + k + 1)
                    sp.dma_start(tile(base, i, k), own[:, k, :]).then_inc(stored[k], 16)

            several(sp, PREPS, turn)
            sp.wait_ge(starts_out, 32 * PREPS)
            sp.dma_start(start_row[0:1, :, :], starts.rearrange("(o a) c -> o a c", o=1)).then_inc(row_in, 16)
            sp.wait_ge(row_in, 16)
            sp.wait_ge(zero_out, 160)
            for k in range(TPB):
                sp.wait_ge(stored[k], 32 * PREPS)

        @block.gpsimd
        def _(pool):
            nc.gpsimd.memset(ident[:, :], 0.0)
            nc.gpsimd.memset(first_of[:, :, :], 0.0)
            nc.gpsimd.memset(ones[:, :], 1.0).then_inc(const_ok, 1)
            pool.wait_ge(const_ok, 1)
            nc.gpsimd.affine_select(out=ident[:, :], in_=ident[:, :], compare_op=ALU.not_equal, fill=1.0,
                                    base=0, pattern=[[-1, P]], channel_multiplier=1).then_inc(masks_ok, 1)
            nc.gpsimd.affine_select(out=first_of[:, :, :], in_=first_of[:, :, :], compare_op=ALU.not_equal, fill=1.0,
                                    base=0, pattern=[[-CH, MG], [0, CH]], channel_multiplier=1).then_inc(masks_ok, 1)
            nc.gpsimd.memset(zero[:, :], 0.0).then_inc(zero_ok, 1)
            pool.wait_ge(weights_in, 16 * (2 * DH + 1))

            def turn(i, first, last):
                for k in range(TPB):
                    pool.wait_ge(x_in[k], i * 16 + 16)
                    if not first:
                        pool.wait_ge(own_ok, (i - 1) * TPB + k + 1)
                    nc.gpsimd.tensor_tensor(xb[:, k, :], x_t[:, k, :], slb[:, :], ALU.add).then_inc(xb_ok, 1)

            several(pool, PREPS, turn)

        @block.vector
        def _(dve):
            nc.vector.memset(bad_sum[:, :], 0.0).then_inc(bad_added, 1)
            for h in range(DH):
                dve.wait_ge(sl_turned, h + 1)
                nc.vector.tensor_copy(slT[:, h, :], p_own[:, h, 0:D]).then_inc(sl_ready, 1)

            def convert(i, first):
                dve.wait_ge(raw_in, i * 64 + 64)
                if not first:
                    dve.wait_ge(cols_ps, i)
                    dve.wait_ge(planes_ok, i * 2)
                nc.vector.tensor_copy(rows[:, :, :], raw[:, :, :]).then_inc(rows_ok, 1)

            def order(i, first):
                dve.wait_ge(rows_ok, i + 1)
                if not first:
                    dve.wait_ge(bad_added, i + 1)
                dve.sem_inc(passed, 1)
                nc.vector.tensor_tensor_reduce(junk[:, :], rows[:, 0, :], rows[:, 3, :], 1.0, 0.0, ALU.subtract,
                                               ALU.max, over[:, 0:1]).then_inc(bad_ok, 1)

            def window(i, first):
                dve.wait_ge(base_ps, i + 1)
                if not first:
                    dve.wait_ge(off_ok, i * 2)
                nc.vector.tensor_copy(ow[:, 1:2], p_small[0:MC, 0:1]).then_inc(base_ok, 1)
                dve.wait_ge(base_ok, i + 1)
                nc.vector.tensor_scalar(ow[:, 2:3], ow[:, 1:2], float(WIN - LOC), rows[:, 0, 0:1], ALU.add, ALU.min).then_inc(w_ok, 1)

            def half_key(i):
                nc.vector.scalar_tensor_tensor(out=key[:, 0, :], in0=rows[:, 1, :], scalar=float(LOC), in1=rows[:, 0, :],
                                               op0=ALU.mult, op1=ALU.add).then_inc(key_half, 1)
                nc.vector.tensor_scalar(key[:, 1, :], rows[:, 0, :], ow[:, 1:2], None, ALU.subtract).then_inc(planes_ok, 1)

            def offsets(i, first):
                dve.wait_ge(w_ok, i + 1)
                nc.vector.tensor_scalar(ow[:, 0:1], ow[:, 2:3], ow[:, 1:2], None, ALU.subtract).then_inc(off_ok, 1)
                dve.wait_ge(off_ok, i * 2 + 1)
                if not first:
                    dve.wait_ge(starts_out, i * 32)
                nc.vector.tensor_copy(oi[:, :], ow[:, 0:2]).then_inc(off_ok, 1)

            def full_key(i):
                dve.wait_ge(key_half, i + 1)
                nc.vector.tensor_scalar(key[:, 0, :], key[:, 0, :], ow[:, 2:3], None, ALU.subtract).then_inc(planes_ok, 1)

            def spans(i):
                for n, (start, width) in enumerate(((rows[:, 0, 0:1], LOC), (ow[:, 1:2], WIN))):
                    nc.vector.tensor_scalar(over[:, n + 1:n + 2], rows[:, 0, P - 1:P], float(N - 1), start,
                                            ALU.min, ALU.subtract).then_inc(bad_ok, 1)
                dve.wait_ge(bad_ok, i * 6 + 3)
                for n, most in enumerate((0, LOC - 1, WIN - 1)):
                    nc.vector.tensor_scalar(bad[:, n:n + 1], over[:, n:n + 1], most + 0.5, None, ALU.is_gt).then_inc(bad_ok, 1)
                dve.wait_ge(bad_ok, i * 6 + 6)
                dve.wait_ge(bad_added, i + 1)
                nc.vector.tensor_tensor(bad_sum[:, :], bad_sum[:, :], bad[:, :], ALU.add).then_inc(bad_added, 1)

            def turn(i, first, last):
                n0 = i * TPB
                convert(i, first)
                if not first:
                    dve.wait_ge(hn_ok, n0)
                for k in range(TPB):
                    dve.wait_ge(x_in[k], i * 16 + 16)
                    nc.vector.bn_stats(stats[:, k, :], x_t[:, k, :]).then_inc(stats_ok, 1)
                order(i, first)
                for k in range(TPB):
                    if k == 0:
                        dve.wait_ge(stats_ok, n0 + TPB)
                        dve.sem_inc(passed, 1)
                    nc.vector.bn_aggr(mv[:, k, :], stats[:, k, :]).then_inc(mv_ok, 1)
                dve.wait_ge(mv_ok, n0 + TPB)
                nc.vector.tensor_scalar(var[:, :], mv[:, :, 1], EPS, None, ALU.add).then_inc(var_ok, 1)
                window(i, first)
                dve.wait_ge(base_ok, i + 1)
                half_key(i)
                offsets(i, first)
                full_key(i)
                dve.wait_ge(std_ok, i + 1)
                nc.vector.reciprocal(rstd[:, :], std[:, :]).then_inc(rstd_ok, 1)
                dve.wait_ge(rstd_ok, i + 1)
                for k in range(TPB):
                    if not first:
                        dve.wait_ge(stored[k], i * 32)
                        dve.wait_ge(hT_ps, (i - 1) * TPB + k + 1)
                    nc.vector.tensor_scalar(hn[:, k, :], x_t[:, k, :], mv[:, k, 0:1], rstd[:, k:k + 1],
                                            ALU.subtract, ALU.mult).then_inc(hn_ok, 1)
                spans(i)
                for k in range(TPB):
                    dve.wait_ge(own_ps, n0 + k + 1)
                    dve.wait_ge(xb_ok, n0 + k + 1)
                    nc.vector.tensor_tensor(own[:, k, :], p_own[:, k % 2, 0:D], xb[:, k, :], ALU.add).then_inc(own_ok, 1)

            several(dve, PREPS, turn)
            dve.wait_ge(bad_added, PREPS + 1)
            nc.vector.reduce_sum(bad_row[:, :], bad_sum[:, :], AX_X).then_inc(bad_rowed, 1)
            dve.wait_ge(bad_ps, 1)
            nc.vector.tensor_scalar(flag[:, :], p_small[0:1, 0:1], 0.5, None, ALU.is_gt).then_inc(flag_ok, 1)

        @block.scalar
        def _(act):
            def turn(i, first, last):
                act.wait_ge(var_ok, i + 1)
                if not first:
                    act.wait_ge(rstd_ok, i)
                nc.scalar.activation(std[:, :], var[:, :], ACT.Sqrt).then_inc(std_ok, 1)
                for k in range(TPB):
                    n = i * TPB + k
                    act.wait_ge(hT_ps, n + 1)
                    if not (first and k < 2):
                        act.wait_ge(own_ps, reused(i, k, 2, TPB))
                    nc.scalar.activation(hT[:, k % 2, :, :], p_hT[:, k % 2, 0:D].rearrange("p (h n) -> p h n", h=DH), ACT.Copy).then_inc(hT_ok, 1)
                act.wait_ge(cols_ps, i + 1)
                act.sem_inc(passed, 1)
                nc.scalar.activation(meta[:, 0:4, bass.ds(i * MC, MC)], p_cols[:, 0, :].rearrange("p (a c) -> p a c", a=4)[:, :, 0:MC], ACT.Copy)
                nc.scalar.activation(meta[:, 4, bass.ds(i * MC, MC)], p_cols[:, 1, 0:MC], ACT.Copy).then_inc(cols_ok, 1)

            several(act, PREPS, turn)

        @block.tensor
        def _(pe):
            pe.wait_ge(masks_ok, 2)
            pe.wait_ge(weights_in, 16 * (2 * DH + 1))
            for h in range(DH):
                for g in range(DH):
                    last = nc.tensor.transpose(p_own[:, h, g * P:(g + 1) * P], slw[:, g, h * P:(h + 1) * P], ident[:, :])
                last.then_inc(sl_turned, 1)
            pe.wait_ge(sl_ready, DH)

            def own_product(i, k, first):
                n = i * TPB + k
                pe.wait_ge(hT_ok, n + 1)
                if not (first and k < 2):
                    pe.wait_ge(own_ok, reused(i, k, 2, TPB))
                for h in range(DH):
                    last = nc.tensor.matmul(p_own[:, k % 2, 0:D], hT[:, k % 2, h, :], slT[:, h, :], start=(h == 0), stop=(h == DH - 1))
                last.then_inc(own_ps, 1)

            def turn(i, first, last):
                pe.wait_ge(rows_ok, i + 1)
                if not first:
                    pe.wait_ge(base_ok, i)
                nc.tensor.matmul(p_small[0:MC, 0:1], first_of[:, :, :].rearrange("p g c -> p (g c)"), rows[:, 0, 0:1],
                                 start=True, stop=True).then_inc(base_ps, 1)
                for k in range(TPB):
                    n = i * TPB + k
                    pe.wait_ge(hn_ok, n + 1)
                    if not (first and k < 2):
                        pe.wait_ge(hT_ok, reused(i, k, 2, TPB))
                    for h in range(DH):
                        t = nc.tensor.transpose(p_hT[:, k % 2, h * P:(h + 1) * P], hn[:, k, h * P:(h + 1) * P], ident[:, :])
                    t.then_inc(hT_ps, 1)
                    if k:
                        own_product(i, k - 1, first)
                own_product(i, TPB - 1, first)
                pe.wait_ge(planes_ok, i * 2 + 2)
                if not first:
                    pe.wait_ge(cols_ok, i)
                for n, plane in enumerate((rows[:, 2, :], key[:, 0, :], key[:, 1, :], rows[:, 0, :], rows[:, 1, :])):
                    t = nc.tensor.transpose(p_cols[:, n // 4, (n % 4) * P:(n % 4) * P + MC], plane, ident[0:MC, 0:MC])
                t.then_inc(cols_ps, 1)

            several(pe, PREPS, turn)
            pe.wait_ge(bad_rowed, 1)
            nc.tensor.matmul(p_small[0:1, 0:1], bad_row[:, :], ones[0:MC, 0:1], start=True, stop=True).then_inc(bad_ps, 1)


def aggregate(nc, scope, sb, ps, sem, passed, table, sums, ident, ones, meta, w_sb, start_row, flag):
    SR, CR = 5, 3
    rows = sb(scope, "a_rows", [P, 2, CH, D])
    idx = sb(scope, "a_idx", [P, 2, CH], U32)
    kd = sb(scope, "a_kd", [P, 2, 2, CH])
    spot = sb(scope, "a_spot", [P, SR, P])
    hits = sb(scope, "a_hits", [P, SR, P], BF16)
    acc = sb(scope, "a_acc", [P, 2, DH * R, WIN])
    res = sb(scope, "a_res", [P, 2, MW])
    count = sb(scope, "a_count", [P, P])
    zeros = sb(scope, "a_zeros", [P, DH * R * WIN])
    ones_bf = sb(scope, "a_ones_bf", [P, 1], BF16)
    p_chunk = ps(scope, "ap_chunk", [P, CR, 512])
    p_deg = ps(scope, "ap_deg", [P, 2, 512])
    p_msg = ps(scope, "ap_msg", [P, 2, 512])
    one_idx = sb(scope, "g_idx", [P, 1], U32)
    row_idx = sb(scope, "g_row_idx", [P, 1], U32)
    dt = sb(scope, "g_dt", [P, 2])
    mask = sb(scope, "g_mask", [P, R])
    diag = sb(scope, "g_diag", [P, P])
    same = sb(scope, "g_same", [P, P])
    below = sb(scope, "g_below", [P, P])
    spill = sb(scope, "g_spill", [P, P])
    trash = sb(scope, "g_trash", [P, 1])
    pick = sb(scope, "g_pick", [P, 4])
    gT = sb(scope, "g_gT", [P, DH, P])
    msg = sb(scope, "g_msg", [P, MW])
    wide = sb(scope, "g_wide", [P, MP])

    consts = sem("a_consts")
    idx_ok = sem("a_idx_ok")
    kd_ok = sem("a_kd_ok")
    acc_zero = sem("a_acc_zero")
    gathered = [[sem(f"a_gathered{b}_{c}") for c in range(CH)] for b in range(2)]
    built = sem("a_built")
    summed = sem("a_summed")
    added = sem("a_added")
    msg_ok = sem("a_msg_ok")
    res_ok = sem("a_res_ok")
    accumulated = sem("a_accumulated")

    g_idx_ok = sem("g_idx_ok")
    g_rows_in = sem("g_rows_in")
    g_dt_ok = sem("g_dt_ok")
    g_mask_ok = sem("g_mask_ok")
    g_diag_ok = sem("g_diag_ok")
    g_dst_ps = sem("g_dst_ps")
    g_same_ok = sem("g_same_ok")
    g_before_ok = sem("g_before_ok")
    g_pick_ok = sem("g_pick_ok")
    g_row_idx_ok = sem("g_row_idx_ok")
    g_turned = sem("g_turned")
    g_gT_ok = sem("g_gT_ok")
    g_part_ps = sem("g_part_ps")
    g_msg_ok = sem("g_msg_ok")
    g_comb_ps = sem("g_comb_ps")
    g_wide_ok = sem("g_wide_ok")
    g_scattered = sem("g_scattered")

    def general_pool(pool):
        nc.gpsimd.iota(trash[:, :], pattern=[[0, 1]], base=TRASH, channel_multiplier=1,
                       allow_small_or_imprecise_dtypes=True).then_inc(consts, 1)
        nc.gpsimd.memset(wide[:, :], 0.0).then_inc(consts, 1)
        nc.gpsimd.memset(below[:, :], 1.0).then_inc(consts, 1)
        pool.wait_ge(consts, 6)
        nc.gpsimd.affine_select(out=below[:, :], in_=below[:, :], compare_op=ALU.is_gt, fill=0.0, base=0,
                                pattern=[[-1, P]], channel_multiplier=1).then_inc(consts, 1)

        def turn(j, first, last):
            pool.wait_ge(g_idx_ok, j + 1)
            pool.sem_inc(passed, 1)
            pool.indirect_dma_start(out=rows[:, 0, 0, :], out_offset=None, in_=table,
                                    in_offset=bass.IndirectOffsetOnAxis(ap=one_idx[:, 0:1], axis=0)).then_inc(g_rows_in, 16)
            pool.wait_ge(g_wide_ok, j + 1)
            pool.sem_inc(passed, 1)
            pool.wait_ge(g_row_idx_ok, j + 1)
            pool.sem_inc(passed, 1)
            pool.indirect_dma_start(out=sums, out_offset=bass.IndirectOffsetOnAxis(ap=row_idx[:, 0:1], axis=0),
                                    in_=wide[:, :], in_offset=None, compute_op=ALU.add).then_inc(g_scattered, 16)
            pool.wait_ge(g_scattered, j * 16 + 16)
            pool.sem_inc(passed, 1)

        several(pool, CHUNKS, turn)

    def general_act(act):
        def turn(j, first, last):
            if not first:
                act.wait_ge(g_rows_in, j * 16)
                act.sem_inc(passed, 1)
            nc.scalar.activation(one_idx[:, 0:1], meta[:, 0, bass.ds(j, 1)], ACT.Copy).then_inc(g_idx_ok, 1)
            act.wait_ge(g_turned, j + 1)
            if not first:
                act.wait_ge(g_part_ps, j * R)
            nc.scalar.activation(gT[:, :, :], p_chunk[:, 1, 0:D].rearrange("p (h n) -> p h n", h=DH), ACT.Copy).then_inc(g_gT_ok, 1)
            act.wait_ge(g_comb_ps, j + 1)
            if not first:
                act.wait_ge(g_scattered, j * 16)
            nc.scalar.activation(wide[:, 0:MW], p_chunk[:, 0, 0:MW], ACT.Copy).then_inc(g_wide_ok, 1)

        act.wait_ge(consts, 7)
        several(act, CHUNKS, turn)

    def general_dve(dve):
        dve.wait_ge(consts, 7)
        nc.vector.memset(msg[:, D:MW], 1.0).then_inc(g_before_ok, 1)

        def turn(j, first, last):
            if not first:
                dve.wait_ge(g_row_idx_ok, j)
                dve.wait_ge(g_mask_ok, j)
                dve.sem_inc(passed, 1)
            nc.vector.tensor_copy(dt[:, :], meta[:, 3:5, bass.ds(j, 1)].rearrange("p a c -> p (a c)")).then_inc(g_dt_ok, 1)
            dve.wait_ge(g_dt_ok, j + 1)
            if not first:
                dve.wait_ge(g_msg_ok, j * R)
            nc.vector.tensor_scalar(mask[:, :], count[:, 0:R], dt[:, 1:2], None, ALU.is_equal).then_inc(g_mask_ok, 1)
            if not first:
                dve.wait_ge(g_dst_ps, j)
            nc.vector.tensor_scalar(diag[:, :], ident[:, :], dt[:, 0:1], None, ALU.mult).then_inc(g_diag_ok, 1)
            dve.wait_ge(g_dst_ps, j + 1)
            if not first:
                dve.wait_ge(g_comb_ps, j)
            nc.vector.tensor_scalar(same[:, :], p_deg[:, 0, 0:P], dt[:, 0:1], None, ALU.is_equal).then_inc(g_same_ok, 1)
            dve.wait_ge(g_same_ok, j + 1)
            dve.wait_ge(g_before_ok, j + 1)
            nc.vector.tensor_tensor_reduce(spill[:, :], same[:, :], below[:, :], 1.0, 0.0, ALU.mult, ALU.add,
                                           pick[:, 0:1]).then_inc(g_before_ok, 1)
            dve.wait_ge(g_before_ok, j + 2)
            nc.vector.tensor_scalar(pick[:, 1:2], pick[:, 0:1], 0.5, None, ALU.is_lt).then_inc(g_pick_ok, 1)
            nc.vector.tensor_tensor(pick[:, 2:3], dt[:, 0:1], trash[:, :], ALU.subtract).then_inc(g_pick_ok, 1)
            dve.wait_ge(g_pick_ok, j * 3 + 2)
            nc.vector.tensor_tensor(pick[:, 3:4], pick[:, 2:3], pick[:, 1:2], ALU.mult).then_inc(g_pick_ok, 1)
            dve.wait_ge(g_pick_ok, j * 3 + 3)
            if not first:
                dve.wait_ge(g_scattered, j * 16)
            nc.vector.tensor_tensor(row_idx[:, :], pick[:, 3:4], trash[:, :], ALU.add).then_inc(g_row_idx_ok, 1)
            dve.wait_ge(g_mask_ok, j + 1)
            for r in range(R):
                dve.wait_ge(g_part_ps, j * R + r + 1)
                if r == 0:
                    if not first:
                        dve.wait_ge(g_comb_ps, j)
                    nc.vector.tensor_scalar(msg[:, 0:D], p_msg[:, 0, 0:D], mask[:, 0:1], None, ALU.mult).then_inc(g_msg_ok, 1)
                    continue
                dve.wait_ge(g_msg_ok, j * R + r)
                nc.vector.scalar_tensor_tensor(out=msg[:, 0:D], in0=p_msg[:, r % 2, 0:D], scalar=mask[:, r:r + 1],
                                               in1=msg[:, 0:D], op0=ALU.mult, op1=ALU.add).then_inc(g_msg_ok, 1)

        several(dve, CHUNKS, turn)

    def general_pe(pe):
        pe.wait_ge(consts, 7)

        def turn(j, first, last):
            pe.wait_ge(g_diag_ok, j + 1)
            if not first:
                pe.wait_ge(g_same_ok, j)
            nc.tensor.matmul(p_deg[:, 0, 0:P], ones[:, :], diag[:, :], start=True, stop=True).then_inc(g_dst_ps, 1)
            pe.wait_ge(g_rows_in, j * 16 + 16)
            if not first:
                pe.wait_ge(g_gT_ok, j)
            for h in range(DH):
                t = nc.tensor.transpose(p_chunk[:, 1, h * P:(h + 1) * P], rows[:, 0, 0, h * P:(h + 1) * P], ident[:, :])
            t.then_inc(g_turned, 1)
            pe.wait_ge(g_gT_ok, j + 1)
            for r in range(R):
                if not first or r >= 2:
                    pe.wait_ge(g_msg_ok, j * R + r - 1)
                for h in range(DH):
                    m = nc.tensor.matmul(p_msg[:, r % 2, 0:D], gT[:, h, :], w_sb[:, h, r, :], start=(h == 0), stop=(h == DH - 1))
                m.then_inc(g_part_ps, 1)
            pe.wait_ge(g_msg_ok, j * R + R)
            if not first:
                pe.wait_ge(g_wide_ok, j)
            nc.tensor.matmul(p_chunk[:, 0, 0:MW], same[:, :], msg[:, :], start=True, stop=True).then_inc(g_comb_ps, 1)

        several(pe, CHUNKS, turn)

    with nc.Block() as block:
        @block.gpsimd
        def _(pool):
            nc.gpsimd.iota(count[:, :], pattern=[[1, P]], base=0, channel_multiplier=0,
                           allow_small_or_imprecise_dtypes=True).then_inc(consts, 1)
            nc.gpsimd.memset(zeros[:, :], 0.0).then_inc(consts, 1)
            nc.gpsimd.memset(ones_bf[:, :], 1.0).then_inc(consts, 1)
            general = pool.value_load(flag[0:1, 0:1], min_val=0, max_val=1)
            with pool.If(general == 0):
                def accumulate(g, b):
                    row = pool.value_load(start_row[0:1, 1, bass.ds(g * CH, 1)], min_val=0, max_val=NP)
                    pool.wait_ge(res_ok, g + 1)
                    pool.sem_inc(passed, 1)
                    pool.dma_start(sums[bass.ds(row, WIN), 0:MW], res[:, b, :], accum_op=ALU.add).then_inc(accumulated, 16)

                def turn(i, first, last):
                    for b in range(2):
                        g = i * 2 + b
                        pool.wait_ge(idx_ok, g + 1)
                        pool.sem_inc(passed, 1)
                        for c in range(CH):
                            if not first:
                                pool.wait_ge(summed, (g - 2) * CH + c + 1)
                                pool.sem_inc(passed, 1)
                                if c == 5:
                                    accumulate(g - 2, b)
                                if c == CH - 1:
                                    pool.wait_ge(accumulated, (g - 1) * 16)
                                    pool.sem_inc(passed, 1)
                            pool.indirect_dma_start(
                                out=rows[:, b, c, :], out_offset=None, in_=table,
                                in_offset=bass.IndirectOffsetOnAxis(ap=idx[:, b, c:c + 1], axis=0),
                            ).then_inc(gathered[b][c], 16)

                several(pool, GROUPS // 2, turn)
                for g in (GROUPS - 2, GROUPS - 1):
                    accumulate(g, g % 2)
                    pool.wait_ge(accumulated, 16 * (g + 1))
            with pool.Else():
                general_pool(pool)

        @block.scalar
        def _(act):
            act.wait_ge(consts, 3)
            general = act.value_load(flag[0:1, 0:1], min_val=0, max_val=1)
            with act.If(general == 0):
                def lists(g, b):
                    act.sem_inc(passed, 1)
                    nc.scalar.activation(idx[:, b, :], meta[:, 0, bass.ds(g * CH, CH)], ACT.Copy).then_inc(idx_ok, 1)
                    nc.scalar.activation(kd[:, b, :, :], meta[:, 1:3, bass.ds(g * CH, CH)], ACT.Copy).then_inc(kd_ok, 1)

                def clear(g, b):
                    nc.scalar.activation(acc[:, b, :, :].rearrange("p a n -> p (a n)"), zeros[:, :], ACT.Copy).then_inc(acc_zero, 1)

                def turn(i, first, last):
                    for b in range(2):
                        g = i * 2 + b
                        if first and b == 0:
                            for n in range(2):
                                lists(n, n)
                                clear(n, n)
                            continue
                        act.wait_ge(summed, g * CH)
                        if not (last and b):
                            act.sem_inc(passed, 1)
                            if not first or b:
                                lists(g + 1, 1 - b)
                        act.wait_ge(msg_ok, g)
                        if not (last and b):
                            clear(g + 1, 1 - b)
                        collect(g - 1, 1 - b, first)

                def collect(g, b, early):
                    if not early:
                        act.wait_ge(accumulated, (g - 1) * 16)
                    act.wait_ge(msg_ok, g + 1)
                    nc.scalar.activation(res[:, b, 0:D], p_msg[:, b, 0:D], ACT.Copy)
                    nc.scalar.activation(res[:, b, D:MW], p_deg[:, b, 0:1], ACT.Copy).then_inc(res_ok, 1)

                several(act, GROUPS // 2, turn)
                collect(GROUPS - 1, 1, False)
            with act.Else():
                general_act(act)

        @block.vector
        def _(dve):
            dve.wait_ge(consts, 3)
            general = dve.value_load(flag[0:1, 0:1], min_val=0, max_val=1)
            with dve.If(general == 0):
                def build(g, b, c, fresh):
                    q = g * CH + c
                    if c == 0:
                        dve.wait_ge(kd_ok, g + 1)
                    if not fresh:
                        dve.wait_ge(summed, q - SR + 1)
                    nc.vector.tensor_scalar(spot[:, c % SR, :], count[:, :], kd[:, b, 0, c:c + 1], None, ALU.is_equal)
                    nc.vector.tensor_scalar(hits[:, c % SR, :], count[:, :], kd[:, b, 1, c:c + 1], None, ALU.is_equal).then_inc(built, 1)

                def add(g, b, c, at, early):
                    q = g * CH + c
                    if c == 0:
                        dve.wait_ge(acc_zero, g + 1)
                    if not (early and c == 0):
                        dve.wait_ge(added, q)
                    dve.wait_ge(summed, q + 1)
                    a = acc[:, b, :, bass.ds(at, LOC)]
                    nc.vector.tensor_tensor(a, a, p_chunk[:, c % CR, 0:D].rearrange("p (a l) -> p a l", l=LOC), ALU.add).then_inc(added, 1)

                def turn(i, first, last):
                    for b in range(2):
                        g = i * 2 + b
                        early = first and b == 0
                        if early:
                            build(g, b, 0, True)
                            build(g, b, 1, True)
                        _, at = nc.values_load_multi_w_load_instructions(
                            start_row[0:1, 0, bass.ds(g * CH, CH)], engines=(ENG.DVE,), min_val=0, max_val=WIN - LOC,
                            skip_runtime_bounds_check_because="the offsets are clamped, and the flag is clear")
                        for c in range(2, CH):
                            build(g, b, c, early and c < SR)
                            add(g, b, c - 2, at[c - 2], early)
                        for c in range(2):
                            if not (last and b):
                                build(g + 1, 1 - b, c, False)
                            add(g, b, CH - 2 + c, at[CH - 2 + c], False)

                several(dve, GROUPS // 2, turn)
            with dve.Else():
                general_dve(dve)

        @block.tensor
        def _(pe):
            pe.wait_ge(consts, 3)
            general = pe.value_load(flag[0:1, 0:1], min_val=0, max_val=1)
            with pe.If(general == 0):
                def messages(g, b, early):
                    pe.wait_ge(added, (g + 1) * CH)
                    if not early:
                        pe.wait_ge(res_ok, g - 1)
                    for n in range(DH * R):
                        m = nc.tensor.matmul(p_msg[:, b, 0:D], acc[:, b, n, :], w_sb[:, n // R, n % R, :],
                                             start=(n == 0), stop=(n == DH * R - 1))
                    m.then_inc(msg_ok, 1)

                def turn(i, first, last):
                    for b in range(2):
                        g = i * 2 + b
                        for c in range(CH):
                            q = g * CH + c
                            pe.wait_ge(built, q + 1)
                            pe.wait_ge(gathered[b][c], i * 16 + 16)
                            if not (first and b == 0 and c < CR):
                                pe.wait_ge(added, q - CR + 1)
                            if c == 0 and not first:
                                pe.wait_ge(res_ok, g - 1)
                            for h in range(DH):
                                nc.tensor.matmul(p_chunk[:, c % CR, h * P:(h + 1) * P], rows[:, b, c, h * P:(h + 1) * P],
                                                 spot[:, c % SR, :], start=True, stop=True)
                            nc.tensor.matmul(p_deg[:, b, 0:1], hits[:, c % SR, :], ones_bf[:, :],
                                             start=(c == 0), stop=(c == CH - 1)).then_inc(summed, 1)
                            if c == 2 and not (first and b == 0):
                                messages(g - 1, 1 - b, first)

                several(pe, GROUPS // 2, turn)
                messages(GROUPS - 1, 1, False)
            with pe.Else():
                general_pe(pe)


def front_pass(nc, scope, sb, ps, sem, passed, base, sums, x1, mean, rstd):
    U = TPB
    m = sb(scope, "f_m", [P, U, MW])
    bs = sb(scope, "f_bs", [P, U, D])
    deg = sb(scope, "f_deg", [P, 2, U])
    stats = sb(scope, "f_stats", [P, U, 6])
    mv = sb(scope, "f_mv", [P, U, 2])
    var = sb(scope, "f_var", [P, TILES])
    std = sb(scope, "f_std", [P, TILES])
    m_in = [sem(f"f_m_in{k}") for k in range(U)]
    deg_ok = sem("f_deg_ok")
    x1_ok = sem("f_x1_ok")
    stats_ok = sem("f_stats_ok")
    mv_ok = sem("f_mv_ok")
    mv_kept = sem("f_mv_kept")
    std_ok = sem("f_std_ok")
    rstd_ok = sem("f_rstd_ok")

    with nc.Block() as block:
        @block.sync
        def _(sp):
            def turn(i, first, last):
                for k in range(U):
                    t = i * U + k
                    if not first:
                        sp.wait_ge(x1_ok, t - U + 1)
                    sp.dma_start(m[:, k, :], sums[bass.ds(t * P, P), 0:MW]).then_inc(m_in[k], 16)
                    sp.dma_start(bs[:, k, :], base[bass.ds(t * P, P), :]).then_inc(m_in[k], 16)

            several(sp, TILES // U, turn)

        @block.vector
        def _(dve):
            def turn(i, first, last):
                for k in range(U):
                    t = i * U + k
                    dve.wait_ge(m_in[k], i * 32 + 32)
                    if not first:
                        dve.wait_ge(x1_ok, t - U + 1)
                    nc.vector.tensor_scalar(deg[:, 0, k:k + 1], m[:, k, D:MW], 1.0, None, ALU.max).then_inc(deg_ok, 1)
                    dve.wait_ge(deg_ok, t * 2 + 1)
                    nc.vector.reciprocal(deg[:, 1, k:k + 1], deg[:, 0, k:k + 1]).then_inc(deg_ok, 1)
                    dve.wait_ge(deg_ok, t * 2 + 2)
                    nc.vector.scalar_tensor_tensor(out=x1[:, bass.ds(t, 1), :].rearrange("p a d -> p (a d)"), in0=m[:, k, 0:D],
                                                   scalar=deg[:, 1, k:k + 1], in1=bs[:, k, :], op0=ALU.mult, op1=ALU.add).then_inc(x1_ok, 1)
                if not first:
                    dve.wait_ge(mv_ok, i * U)
                for k in range(U):
                    t = i * U + k
                    dve.wait_ge(x1_ok, t + 1)
                    dve.sem_inc(passed, 1)
                    nc.vector.bn_stats(stats[:, k, :], x1[:, bass.ds(t, 1), :].rearrange("p a d -> p (a d)")).then_inc(stats_ok, 1)
                dve.wait_ge(stats_ok, i * U + U)
                if not first:
                    dve.wait_ge(mv_kept, i * 2)
                dve.sem_inc(passed, 1)
                for k in range(U):
                    nc.vector.bn_aggr(mv[:, k, :], stats[:, k, :]).then_inc(mv_ok, 1)
                dve.wait_ge(mv_ok, i * U + U)
                dve.sem_inc(passed, 1)
                nc.vector.tensor_copy(mean[:, bass.ds(i * U, U)], mv[:, :, 0]).then_inc(mv_kept, 1)
                nc.vector.tensor_scalar(var[:, bass.ds(i * U, U)], mv[:, :, 1], EPS, None, ALU.add).then_inc(mv_kept, 1)

            several(dve, TILES // U, turn)
            dve.wait_ge(std_ok, 1)
            nc.vector.reciprocal(rstd[:, :], std[:, :]).then_inc(rstd_ok, 1)
            dve.wait_ge(rstd_ok, 1)

        @block.scalar
        def _(act):
            act.wait_ge(mv_kept, 2 * (TILES // U))
            nc.scalar.activation(std[:, :], var[:, :], ACT.Sqrt).then_inc(std_ok, 1)


def slice_pass(nc, scope, sb, ps, sem, passed, w_x, b_x, w_slice, b_slice, b_out, temp, slices, ident,
               ones, x1, mean, rstd, tok):
    wx = sb(scope, "s_wx", [P, DH, HG])
    wxT = sb(scope, "s_wxT", [C, DH, H, P])
    ws = sb(scope, "s_ws", [C, G])
    bxT = sb(scope, "s_bxT", [C, H])
    bsl = sb(scope, "s_bsl", [1, G])
    brow = sb(scope, "s_brow", [1, HG])
    bfull = sb(scope, "s_bfull", [P, HG])
    wxs = sb(scope, "s_wxs", [P, DH, HG])
    tmp = sb(scope, "s_tmp", [P, H])
    rtmp = sb(scope, "s_rtmp", [P, H])
    bo = sb(scope, "s_bo", [P, D])
    real = sb(scope, "s_real", [P, TILES])
    xn = sb(scope, "s_xn", [P, 2, D + 1])
    xT = sb(scope, "s_xT", [P, 2, DH, P])
    lg = sb(scope, "s_lg", [P, 2, HG])
    top = sb(scope, "s_top", [P, 2, H])
    ntop = sb(scope, "s_ntop", [P, 2, H])
    ex = sb(scope, "s_ex", [P, 2, HG])
    tot = sb(scope, "s_tot", [P, 2, H])
    inv = sb(scope, "s_inv", [P, 2, H])
    invr = sb(scope, "s_invr", [P, 2, H])
    sw = sb(scope, "s_sw", [P, 2, HG])
    p_xT = ps(scope, "sp_xT", [P, 2, 512])
    p_lg = ps(scope, "sp_lg", [P, 2, 512])
    p_tok = ps(scope, "sp_tok", [P, 4, 512])

    w_in = sem("s_w_in")
    cst = sem("s_cst")
    tmp_ok = sem("s_tmp_ok")
    wx_ps = sem("s_wx_ps")
    wx_ok = sem("s_wx_ok")
    kept = sem("s_kept")
    xn_ok = sem("s_xn_ok")
    xT_ps = sem("s_xT_ps")
    xT_ok = sem("s_xT_ok")
    lg_ps = sem("s_lg_ps")
    lg_ok = sem("s_lg_ok")
    top_ok = sem("s_top_ok")
    ntop_ok = sem("s_ntop_ok")
    ex_ok = sem("s_ex_ok")
    inv_ok = sem("s_inv_ok")
    invr_ok = sem("s_invr_ok")
    sw_ok = sem("s_sw_ok")
    tok_ps = sem("s_tok_ps")
    tok_ok = sem("s_tok_ok")
    sw_out = [sem(f"s_sw_out{b}") for b in range(2)]

    def row(a):
        return a.rearrange("(a n) -> a n", a=1)

    with nc.Block() as block:
        @block.sync
        def _(sp):
            for h in range(DH):
                sp.dma_start(wx[:, h, :], w_x[h * P:(h + 1) * P, :]).then_inc(w_in, 16)
            sp.dma_start(ws[:, :], w_slice).then_inc(w_in, 16)
            for h in range(H):
                sp.dma_start(bxT[:, h:h + 1], b_x[h * C:(h + 1) * C].rearrange("(c a) -> c a", a=1)).then_inc(w_in, 16)
            sp.dma_start(bsl[:, :], row(b_slice)).then_inc(w_in, 16)
            sp.dma_start(tmp[:, :], temp.rearrange("a h b c -> (a b c) h").to_broadcast((P, H))).then_inc(w_in, 16)
            sp.dma_start(bo[:, :], row(b_out).to_broadcast((P, D))).then_inc(w_in, 16)

            def turn(i, first, last):
                for b in range(2):
                    t = i * 2 + b
                    if not first:
                        sp.wait_ge(sw_ok, t - 1)
                        sp.dma_start(slices[bass.ds((t - 2) * P, P), :], sw[:, b, :]).then_inc(sw_out[b], 16)

            several(sp, TILES // 2, turn)
            for b in range(2):
                t = TILES - 2 + b
                sp.wait_ge(sw_ok, t + 1)
                sp.dma_start(slices[t * P:(t + 1) * P, :], sw[:, b, :]).then_inc(sw_out[b], 16)
            for b in range(2):
                sp.wait_ge(sw_out[b], 16 * (TILES // 2))

        @block.gpsimd
        def _(pool):
            nc.gpsimd.memset(real[:, :], 1.0).then_inc(cst, 1)
            pool.wait_ge(cst, 1)
            nc.gpsimd.affine_select(out=real[:, :], in_=real[:, :], compare_op=ALU.is_gt, fill=0.0, base=N,
                                    pattern=[[-P, TILES]], channel_multiplier=-1).then_inc(cst, 1)
            pool.wait_ge(w_in, 16 * (DH + H + 4))

            def turn(i, first, last):
                for b in range(2):
                    t = i * 2 + b
                    pool.wait_ge(xn_ok, t + 1)
                    pool.sem_inc(passed, 1)
                    own = x1[:, bass.ds(t, 1), :].rearrange("p a d -> p (a d)")
                    nc.gpsimd.tensor_tensor(own, own, bo[:, :], ALU.add).then_inc(kept, 1)
                    pool.wait_ge(invr_ok, t + 1)
                    pool.wait_ge(ex_ok, t + 1)
                    if not first:
                        pool.wait_ge(sw_out[b], i * 16)
                        pool.wait_ge(tok_ps, t - 1)
                    nc.gpsimd.tensor_tensor(sw[:, b, :].rearrange("p (h g) -> p h g", h=H),
                                            ex[:, b, :].rearrange("p (h g) -> p h g", h=H),
                                            invr[:, b, :].rearrange("p (h a) -> p h a", a=1).to_broadcast((P, H, G)),
                                            ALU.mult).then_inc(sw_ok, 1)

            several(pool, TILES // 2, turn)

        @block.vector
        def _(dve):
            nc.vector.memset(xn[:, :, D:D + 1], 1.0).then_inc(tmp_ok, 1)
            dve.wait_ge(w_in, 16 * (DH + H + 4))
            dve.wait_ge(tmp_ok, 1)
            dve.wait_ge(cst, 2)
            nc.vector.tensor_scalar(tmp[:, :], tmp[:, :], 0.1, 5.0, ALU.max, ALU.min).then_inc(tmp_ok, 1)
            dve.wait_ge(tmp_ok, 2)
            nc.vector.reciprocal(rtmp[:, :], tmp[:, :]).then_inc(tmp_ok, 1)
            dve.wait_ge(tmp_ok, 3)
            per_head = rtmp[:, :].rearrange("p (h a) -> p h a", a=1).to_broadcast((P, H, G))
            for h in range(DH):
                dve.wait_ge(wx_ps, h + 1)
                nc.vector.tensor_copy(wxT[:, h, :, :], p_tok[0:C, 2 * h:2 * h + 2, :].rearrange("p a (b n) -> p (a b) n", n=P)).then_inc(wx_ok, 1)
            for h in range(DH):
                dve.wait_ge(wx_ps, DH + h + 1)
                nc.vector.tensor_tensor(wxs[:, h, :].rearrange("p (h g) -> p h g", h=H),
                                        p_lg[:, h, :].rearrange("p (h g) -> p h g", h=H), per_head, ALU.mult).then_inc(wx_ok, 1)
            dve.wait_ge(wx_ps, 2 * DH + 1)
            nc.vector.tensor_tensor(brow[:, :].rearrange("p (h g) -> p h g", h=H),
                                    p_xT[0:1, 0, :].rearrange("p (h g) -> p h g", h=H), per_head[0:1], ALU.mult).then_inc(wx_ok, 1)
            dve.wait_ge(wx_ps, 2 * DH + 2)
            nc.vector.tensor_copy(bfull[:, :], p_xT[:, 1, :]).then_inc(wx_ok, 1)
            dve.wait_ge(wx_ok, 2 * DH + 2)

            def norm(t, b, first):
                if not first:
                    dve.wait_ge(tok_ps, t - 1)
                dve.sem_inc(passed, 1)
                nc.vector.tensor_scalar(xn[:, b, 0:D], x1[:, bass.ds(t, 1), :].rearrange("p a d -> p (a d)"), mean[:, bass.ds(t, 1)],
                                        rstd[:, bass.ds(t, 1)], ALU.subtract, ALU.mult).then_inc(xn_ok, 1)

            def tops(t, b, first):
                dve.wait_ge(lg_ps, t + 1)
                if not first:
                    dve.wait_ge(ex_ok, t - 1)
                nc.vector.tensor_tensor(lg[:, b, :], p_lg[:, b, :], bfull[:, :], ALU.add).then_inc(lg_ok, 1)
                dve.wait_ge(lg_ok, t + 1)
                nc.vector.reduce_max(top[:, b, :], lg[:, b, :].rearrange("p (h g) -> p h g", h=H), AX_X).then_inc(top_ok, 1)
                dve.wait_ge(top_ok, t + 1)
                nc.vector.tensor_scalar(ntop[:, b, :], top[:, b, :], -1.0, None, ALU.mult).then_inc(ntop_ok, 1)

            def invert(t, b, first):
                dve.wait_ge(ex_ok, t + 1)
                if not first:
                    dve.wait_ge(sw_ok, t - 1)
                nc.vector.reciprocal(inv[:, b, :], tot[:, b, :]).then_inc(inv_ok, 1)
                dve.wait_ge(inv_ok, t + 1)
                nc.vector.tensor_scalar(invr[:, b, :], inv[:, b, :], real[:, bass.ds(t, 1)], None, ALU.mult).then_inc(invr_ok, 1)

            def turn(i, first, last):
                for b in range(2):
                    t = i * 2 + b
                    if not first:
                        invert(t - 2, b, isinstance(i, int) and i == 1)
                    norm(t, b, first)
                    if not (first and b == 0):
                        tops(t - 1, 1 - b, first)

            turn(0, True, False)
            turn(1, False, False)
            with dve.Fori(2, TILES // 2) as i:
                turn(i, False, False)
            tops(TILES - 1, 1, False)
            invert(TILES - 2, 0, False)
            invert(TILES - 1, 1, False)
            for j in range(4):
                dve.wait_ge(tok_ps, TILES)
                nc.vector.tensor_copy(tok[:, j, :], p_tok[:, j, 0:D + 1]).then_inc(tok_ok, 1)

        @block.scalar
        def _(act):
            def copy_xT(t, b, first):
                act.wait_ge(xT_ps, t + 1)
                if not first:
                    act.wait_ge(lg_ps, t - 1)
                nc.scalar.activation(xT[:, b, :, :], p_xT[:, b, 0:D].rearrange("p (h n) -> p h n", h=DH), ACT.Copy).then_inc(xT_ok, 1)

            def exps(t, b, first):
                act.wait_ge(ntop_ok, t + 1)
                if not first:
                    act.wait_ge(sw_ok, t - 1)
                for h in range(H):
                    e = nc.scalar.activation(ex[:, b, h * G:(h + 1) * G], lg[:, b, h * G:(h + 1) * G], ACT.Exp,
                                             bias=ntop[:, b, h:h + 1], accum_out=tot[:, b, h:h + 1])
                e.then_inc(ex_ok, 1)

            def turn(i, first, last):
                for b in range(2):
                    t = i * 2 + b
                    copy_xT(t, b, first)
                    if not (first and b == 0):
                        exps(t - 1, 1 - b, first or (isinstance(i, int) and i == 1 and b == 0))

            turn(0, True, False)
            turn(1, False, False)
            with act.Fori(2, TILES // 2) as i:
                turn(i, False, False)
            exps(TILES - 1, 1, False)

        @block.tensor
        def _(pe):
            pe.wait_ge(w_in, 16 * (DH + H + 4))
            for h in range(DH):
                for n in range(H):
                    t = nc.tensor.transpose(p_tok[0:C, 2 * h + n // 4, (n % 4) * P:(n % 4 + 1) * P], wx[:, h, n * C:(n + 1) * C], ident[:, :])
                t.then_inc(wx_ps, 1)
            for h in range(DH):
                pe.wait_ge(wx_ok, h + 1)
                for n in range(H):
                    t = nc.tensor.matmul(p_lg[:, h, n * G:(n + 1) * G], wxT[:, h, n, :], ws[:, :], start=True, stop=True)
                t.then_inc(wx_ps, 1)
            for n in range(H):
                nc.tensor.matmul(p_xT[0:1, 0, n * G:(n + 1) * G], bxT[:, n:n + 1], ws[:, :], start=True, stop=False)
                t = nc.tensor.matmul(p_xT[0:1, 0, n * G:(n + 1) * G], ones[0:1, 0:1], bsl[:, :], start=False, stop=True)
            t.then_inc(wx_ps, 1)
            pe.wait_ge(wx_ok, 2 * DH + 1)
            nc.tensor.matmul(p_xT[:, 1, :], ones[0:1, :], brow[:, :], start=True, stop=True).then_inc(wx_ps, 1)
            pe.wait_ge(wx_ok, 2 * DH + 2)

            def logits(t, b, first):
                pe.wait_ge(xn_ok, t + 1)
                if not first:
                    pe.wait_ge(xT_ok, t - 1)
                for h in range(DH):
                    m = nc.tensor.transpose(p_xT[:, b, h * P:(h + 1) * P], xn[:, b, h * P:(h + 1) * P], ident[:, :])
                m.then_inc(xT_ps, 1)
                pe.wait_ge(xT_ok, t + 1)
                if not first:
                    pe.wait_ge(lg_ok, t - 1)
                for h in range(DH):
                    m = nc.tensor.matmul(p_lg[:, b, :], xT[:, b, h, :], wxs[:, h, :], start=(h == 0), stop=(h == DH - 1))
                m.then_inc(lg_ps, 1)

            def tokens(t, b, start, stop):
                pe.wait_ge(sw_ok, t + 1)
                for j in range(4):
                    m = nc.tensor.matmul(p_tok[:, j, 0:D + 1], sw[:, b, j * P:(j + 1) * P], xn[:, b, :], start=start, stop=stop)
                m.then_inc(tok_ps, 1)

            def turn(i, first, last):
                for b in range(2):
                    t = i * 2 + b
                    logits(t, b, first)
                    if not (first and b == 0):
                        tokens(t - 1, 1 - b, first, False)

            several(pe, TILES // 2, turn)
            tokens(TILES - 1, 1, False, True)


def token_stage(nc, scope, sb, ps, sem, passed, w_fx, b_fx, w_q, w_k, w_v, w_out, ident, tok, mix):
    wfx = sb(scope, "t_wfx", [P, DH, HG])
    bfx = sb(scope, "t_bfx", [1, HG])
    wqkv = sb(scope, "t_wqkv", [C, 3, C])
    wo = sb(scope, "t_wo", [C, H, D])
    den = sb(scope, "t_den", [P, 2, 4])
    tn = sb(scope, "t_tn", [P, 4, D + 1])
    tT = sb(scope, "t_tT", [P, DH, HG])
    nrow = sb(scope, "t_nrow", [1, HG])
    tokT = sb(scope, "t_tokT", [C, HG])
    qkv = sb(scope, "t_qkv", [C, 3, HG])
    sc = sb(scope, "t_sc", [G, H, G])
    sm = sb(scope, "t_sm", [G, 3, H])
    aT = sb(scope, "t_aT", [G, H, G])
    vw = sb(scope, "t_vw", [G, H, D])
    p_a = ps(scope, "tp_a", [P, 2, 512])
    p_b = ps(scope, "tp_b", [P, 512])
    p_c = ps(scope, "tp_c", [P, 512])
    p_vw = ps(scope, "tp_vw", [P, 4, 512])
    w_in = sem("t_w_in")
    mm = sem("t_products")
    el = sem("t_elementwise")
    exped = sem("t_exped")

    def per_head(a):
        return a.rearrange("p (h a) -> p h a", a=1).to_broadcast((G, H, G))

    with nc.Block() as block:
        @block.sync
        def _(sp):
            for h in range(DH):
                sp.dma_start(wfx[:, h, :], w_fx[h * P:(h + 1) * P, :]).then_inc(w_in, 16)
            sp.dma_start(bfx[:, :], b_fx.rearrange("(a n) -> a n", a=1)).then_inc(w_in, 16)
            for n, w in enumerate((w_q, w_k, w_v)):
                sp.dma_start(wqkv[:, n, :], w).then_inc(w_in, 16)
            sp.dma_start(wo[:, :, :], w_out.rearrange("(h c) d -> c h d", c=C)).then_inc(w_in, 16)

        @block.vector
        def _(dve):
            nc.vector.tensor_scalar(den[:, 0, :], tok[:, :, D], 1e-5, None, ALU.add).then_inc(el, 1)
            dve.wait_ge(el, 1)
            nc.vector.reciprocal(den[:, 1, :], den[:, 0, :]).then_inc(el, 1)
            dve.wait_ge(el, 2)
            nc.vector.tensor_tensor(tn[:, :, :], tok[:, :, :], den[:, 1, :].rearrange("p (j a) -> p j a", a=1).to_broadcast((P, 4, D + 1)),
                                    ALU.mult).then_inc(el, 1)
            dve.wait_ge(mm, 1)
            nc.vector.tensor_copy(tT[:, :, :], p_a[:, :, :])
            nc.vector.tensor_copy(nrow[:, :], p_b[0:1, :]).then_inc(el, 1)
            dve.wait_ge(mm, 2)
            nc.vector.tensor_copy(tokT[:, :], p_c[0:C, :]).then_inc(el, 1)
            dve.wait_ge(mm, 3)
            nc.vector.tensor_copy(qkv[:, 0:2, :], p_a[0:C, :, :])
            nc.vector.tensor_copy(qkv[:, 2, :], p_b[0:C, :]).then_inc(el, 1)
            dve.wait_ge(mm, 4)
            nc.vector.tensor_scalar(sc[:, :, :], p_c[0:G, :].rearrange("p (h k) -> p h k", h=H), C ** -0.5, None, ALU.mult).then_inc(el, 1)
            dve.wait_ge(el, 7)
            nc.vector.reduce_max(sm[:, 0, :], sc[:, :, :], AX_X).then_inc(el, 1)
            dve.wait_ge(el, 8)
            nc.vector.tensor_tensor(sc[:, :, :], sc[:, :, :], per_head(sm[:, 0, :]), ALU.subtract).then_inc(el, 1)
            dve.wait_ge(exped, 1)
            nc.vector.reduce_sum(sm[:, 1, :], sc[:, :, :], AX_X).then_inc(el, 1)
            dve.wait_ge(el, 10)
            nc.vector.reciprocal(sm[:, 2, :], sm[:, 1, :]).then_inc(el, 1)
            dve.wait_ge(el, 11)
            nc.vector.tensor_tensor(sc[:, :, :], sc[:, :, :], per_head(sm[:, 2, :]), ALU.mult).then_inc(el, 1)
            dve.wait_ge(mm, 5)
            nc.vector.tensor_copy(vw[:, :, :], p_vw[0:G, :, :].rearrange("p a (b d) -> p (a b) d", d=D)).then_inc(el, 1)
            dve.wait_ge(mm, 6)
            nc.vector.tensor_copy(aT[:, :, :], p_a[0:G, 0, :].rearrange("p (h g) -> p h g", h=H)).then_inc(el, 1)
            dve.wait_ge(mm, 7)
            nc.vector.tensor_copy(mix[:, :, :], p_vw[:, 0:2, :].rearrange("p a (b d) -> p (a b) d", d=D)).then_inc(el, 1)
            dve.wait_ge(el, 15)

        @block.scalar
        def _(act):
            act.wait_ge(el, 9)
            nc.scalar.activation(sc[:, :, :], sc[:, :, :], ACT.Exp).then_inc(exped, 1)

        @block.tensor
        def _(pe):
            pe.wait_ge(el, 3)
            for j in range(4):
                for h in range(DH):
                    nc.tensor.transpose(p_a[:, h, j * P:(j + 1) * P], tn[:, j, h * P:(h + 1) * P], ident[:, :])
                m = nc.tensor.matmul(p_b[0:1, j * P:(j + 1) * P], tn[:, j, D:D + 1], ident[:, :], start=True, stop=True)
            m.then_inc(mm, 1)
            pe.wait_ge(w_in, 16 * (DH + 5))
            pe.wait_ge(el, 4)
            for n in range(H):
                own = slice(n * C, (n + 1) * C)
                for h in range(DH):
                    nc.tensor.matmul(p_c[0:C, own], wfx[:, h, own], tT[:, h, own], start=(h == 0), stop=False)
                m = nc.tensor.matmul(p_c[0:C, own], bfx[:, own], nrow[:, own], start=False, stop=True)
            m.then_inc(mm, 1)
            pe.wait_ge(el, 5)
            for n in range(3):
                m = nc.tensor.matmul(p_a[0:C, n, :] if n < 2 else p_b[0:C, :], wqkv[:, n, :], tokT[:, :], start=True, stop=True)
            m.then_inc(mm, 1)
            pe.wait_ge(el, 6)
            for n in range(H):
                own = slice(n * C, (n + 1) * C)
                m = nc.tensor.matmul(p_c[0:G, own], qkv[:, 0, own], qkv[:, 1, own], start=True, stop=True)
            m.then_inc(mm, 1)
            for n in range(H):
                m = nc.tensor.matmul(p_vw[0:G, n // 2, (n % 2) * D:(n % 2 + 1) * D], qkv[:, 2, n * C:(n + 1) * C], wo[:, n, :], start=True, stop=True)
            m.then_inc(mm, 1)
            pe.wait_ge(el, 12)
            for n in range(H):
                m = nc.tensor.transpose(p_a[0:G, 0, n * G:(n + 1) * G], sc[:, n, :], ident[0:G, 0:G])
            m.then_inc(mm, 1)
            pe.wait_ge(el, 14)
            for n in range(H):
                m = nc.tensor.matmul(p_vw[(n % 2) * G:(n % 2 + 1) * G, n // 4, (n // 2 % 2) * D:(n // 2 % 2 + 1) * D], aT[:, n, :], vw[:, n, :],
                                     start=True, stop=True)
            m.then_inc(mm, 1)


def output_pass(nc, scope, sb, ps, sem, passed, slices, out, ident, x1, mix):
    U = 7
    sl = sb(scope, "o_sl", [P, U, HG])
    sT = sb(scope, "o_sT", [P, U, 4, P])
    ot = sb(scope, "o_ot", [P, U, D])
    p_T = ps(scope, "op_T", [P, 3, 512])
    p_o = ps(scope, "op_o", [P, 3, 512])
    sl_in = [sem(f"o_sl_in{k}") for k in range(U)]
    turned = sem("o_turned")
    sT_ok = sem("o_sT_ok")
    o_ps = sem("o_ps")
    ot_ok = sem("o_ot_ok")
    out_out = [sem(f"o_out{k}") for k in range(U)]

    with nc.Block() as block:
        @block.sync
        def _(sp):
            for k in range(U):
                sp.dma_start(sl[:, k, :], slices[k * P:(k + 1) * P, :]).then_inc(sl_in[k], 16)

            def turn(i, first, last):
                for k in range(U):
                    t = i * U + k
                    if not last:
                        sp.wait_ge(turned, t + 1)
                        sp.dma_start(sl[:, k, :], slices[bass.ds((t + U) * P, P), :]).then_inc(sl_in[k], 16)
                    sp.wait_ge(ot_ok, t + 1)
                    sp.dma_start(out[bass.ds(t * P, P), :], ot[:, k, :]).then_inc(out_out[k], 16)

            several(sp, TILES // U, turn)
            for k in range(U):
                sp.wait_ge(out_out[k], 16 * (TILES // U))

        @block.tensor
        def _(pe):
            def turn_slices(i, k, first):
                t = i * U + k
                pe.wait_ge(sl_in[k], i * 16 + 16)
                if not (first and k < 3):
                    pe.wait_ge(sT_ok, reused(i, k, 3, U))
                for j in range(4):
                    m = nc.tensor.transpose(p_T[:, k % 3, j * P:(j + 1) * P], sl[:, k, j * P:(j + 1) * P], ident[:, :])
                m.then_inc(turned, 1)

            def blend(i, k, first):
                t = i * U + k
                pe.wait_ge(sT_ok, t + 1)
                if not (first and k < 3):
                    pe.wait_ge(ot_ok, reused(i, k, 3, U))
                for j in range(4):
                    m = nc.tensor.matmul(p_o[:, k % 3, 0:D], sT[:, k, j, :], mix[:, j, :], start=(j == 0), stop=(j == 3))
                m.then_inc(o_ps, 1)

            def turn(i, first, last):
                for k in range(U):
                    turn_slices(i, k, first)
                    if k:
                        blend(i, k - 1, first)
                blend(i, U - 1, first)

            several(pe, TILES // U, turn)

        @block.scalar
        def _(act):
            def turn(i, first, last):
                for k in range(U):
                    t = i * U + k
                    act.wait_ge(turned, t + 1)
                    if not first:
                        act.wait_ge(o_ps, t - U + 1)
                    nc.scalar.activation(sT[:, k, :, :], p_T[:, k % 3, :].rearrange("p (j n) -> p j n", j=4), ACT.Copy).then_inc(sT_ok, 1)

            several(act, TILES // U, turn)

        @block.vector
        def _(dve):
            def turn(i, first, last):
                for k in range(U):
                    t = i * U + k
                    if not first:
                        dve.wait_ge(out_out[k], i * 16)
                    dve.wait_ge(o_ps, t + 1)
                    nc.vector.tensor_tensor(ot[:, k, :], p_o[:, k % 3, 0:D], x1[:, bass.ds(t, 1), :].rearrange("p a d -> p (a d)"), ALU.add).then_inc(ot_ok, 1)

            several(dve, TILES // U, turn)


def kernel(x, src, dst, edge_type_8, L0_gnn_weight, L0_gnn_sl_w, L0_gnn_sl_b, L0_ffn_W_fx, L0_ffn_b_fx,
           L0_ffn_W_x, L0_ffn_b_x, L0_ffn_W_slice, L0_ffn_b_slice, L0_ffn_W_q, L0_ffn_W_k, L0_ffn_W_v,
           L0_ffn_W_out, L0_ffn_b_out, L0_ffn_temperature):
    import concourse.bacc as bacc
    from concourse.bass_utils import run_bass_kernel_spmd

    def filled(a, rows, value):
        a = np.ascontiguousarray(a)
        full = np.full((rows,) + a.shape[1:], value, a.dtype)
        full[:a.shape[0]] = a
        return full

    arrays = {
        "x": filled(x, NP, 0),
        "src": filled(src, EP + P, 0),
        "dst": filled(dst, EP + P, NP),
        "typ": filled(edge_type_8, EP + P, PAD_TYPE),
        "w_rel": L0_gnn_weight, "sl_w": L0_gnn_sl_w, "sl_b": L0_gnn_sl_b,
        "w_fx": L0_ffn_W_fx, "b_fx": L0_ffn_b_fx, "w_x": L0_ffn_W_x, "b_x": L0_ffn_b_x,
        "w_slice": L0_ffn_W_slice, "b_slice": L0_ffn_b_slice, "w_q": L0_ffn_W_q, "w_k": L0_ffn_W_k,
        "w_v": L0_ffn_W_v, "w_out": L0_ffn_W_out, "b_out": L0_ffn_b_out, "temp": L0_ffn_temperature,
    }
    nc = bacc.Bacc("TRN2", target_bir_lowering=False, num_devices=1)
    feed, aps = {}, {}
    for name, a in arrays.items():
        a = np.ascontiguousarray(a)
        feed[f"in_{name}"] = a
        aps[name] = nc.dram_tensor(f"in_{name}", a.shape, mybir.dt.from_np(a.dtype), kind="ExternalInput").ap()
    aps["out"] = nc.dram_tensor("out_0", (NP, D), F32, kind="ExternalOutput").ap()
    program(nc, **aps)
    r = run_bass_kernel_spmd(nc, [feed], core_ids=[0])
    return r.results[0]["out_0"][:N]
```

```python
from contextlib import ExitStack

import numpy as np
import concourse.bass as bass
from concourse import mybir

ALU = mybir.AluOpType
ACT = mybir.ActivationFunctionType
AX_X = mybir.AxisListType.X
F32 = mybir.dt.float32
BF16 = mybir.dt.bfloat16
I32 = mybir.dt.int32
U32 = mybir.dt.uint32
ENG = mybir.EngineType

P = 128
N, D, R, E = 12500, 256, 8, 212500
DH = D // P
EPS = 1e-5

TILES = -(-N // P)
NP = TILES * P
CH = 15
WIN = P
LOC = P // R
GROUP = CH * P
MG = 8
MC = MG * CH
GROUPS = -(-E // (GROUP * MG)) * MG
CHUNKS = GROUPS * CH
PREPS = GROUPS // MG
EP = GROUPS * GROUP
TPB = TILES // PREPS
LAG = 5
assert TPB * PREPS == TILES and MG % 2 == 0 and MG == TPB + 1 and MC % 2 == 0
PAD_TYPE = 64
MROWS = NP + 2 * P
TRASH = NP + P
MW = D + 1
MP = 264

H, C, G = 8, 64, 64
HG = H * G


def several(eng, n, body):
    body(0, True, False)
    with eng.Fori(1, n - 1) as i:
        body(i, False, False)
    body(n - 1, False, True)


def reused(turn, k, ring, per):
    if k >= ring:
        return turn * per + k - ring + 1
    return (turn - 1) * per + k + ring * ((per - 1 - k) // ring) + 1


def program(nc, x, src, dst, typ, w_rel, sl_w, sl_b, w_fx, b_fx, w_x, b_x, w_slice, b_slice,
            w_q, w_k, w_v, w_out, b_out, temp, out):
    table = nc.dram_tensor("table", (NP, D), F32, kind="Internal").ap()
    base = nc.dram_tensor("base", (NP, D), F32, kind="Internal").ap()
    sums = nc.dram_tensor("sums", (MROWS, MP), F32, kind="Internal").ap()
    starts = nc.dram_tensor("starts", (2, CHUNKS), I32, kind="Internal").ap()
    x1 = nc.dram_tensor("x1", (NP, D), F32, kind="Internal").ap()
    slices = nc.dram_tensor("slices", (NP, HG), F32, kind="Internal").ap()

    with ExitStack() as whole:
        def sb(scope, name, shape, dt=F32):
            return scope.enter_context(nc.sbuf_tensor(name, shape, dt))

        def ps(scope, name, shape, dt=F32):
            return scope.enter_context(nc.psum_tensor(name, shape, dt))

        live = []

        def sem(name):
            live.append(nc.alloc_semaphore(name=name))
            return live[-1]

        def release():
            nc.clear_and_free_semaphores(live)
            live.clear()
            nc.all_engine_barrier()

        passed = nc.alloc_semaphore(name="passed")

        ident = sb(whole, "ident", [P, P])
        ones = sb(whole, "ones", [P, P])
        tok = sb(whole, "tok", [P, 4, D])
        tok_sum = sb(whole, "tok_sum", [P, 4])
        mix = sb(whole, "mix", [P, 4, D])
        with ExitStack() as graph:
            meta = sb(graph, "meta", [P, 5, CHUNKS])
            w_sb = sb(graph, "w_sb", [P, DH, R, D])
            start_row = sb(graph, "start_row", [1, 2, CHUNKS], I32)
            flag = sb(graph, "flag", [1, 1], I32)
            with ExitStack() as scope:
                prepare(nc, scope, sb, ps, sem, passed, x, src, dst, typ, w_rel, sl_w, sl_b, table, base,
                        sums, starts, ident, ones, meta, w_sb, start_row, flag)
            release()
            with ExitStack() as scope:
                main_pass(nc, scope, sb, ps, sem, passed, table, base, sums, x1, slices, w_x, b_x, w_slice,
                          b_slice, temp, ident, ones, meta, w_sb, start_row, flag, tok, tok_sum)
            release()
        with ExitStack() as scope:
            token_stage(nc, scope, sb, ps, sem, w_fx, b_fx, w_q, w_k, w_v, w_out, ident, tok, tok_sum, mix)
        with ExitStack() as scope:
            output_pass(nc, scope, sb, ps, sem, b_out, x1, slices, out, ident, mix)


def prepare(nc, scope, sb, ps, sem, passed, x, src, dst, typ, w_rel, sl_w, sl_b, table, base, sums, starts,
            ident, ones, meta, w_sb, start_row, flag):
    x_t = sb(scope, "p_x", [P, TPB, D])
    hn = sb(scope, "p_hn", [P, TPB, D])
    xb = sb(scope, "p_xb", [P, TPB, D])
    own = sb(scope, "p_own", [P, TPB, D])
    hT = sb(scope, "p_hT", [P, 2, DH, P])
    stats = sb(scope, "p_stats", [P, TPB, 6])
    mv = sb(scope, "p_mv", [P, TPB, 2])
    var = sb(scope, "p_var", [P, TPB])
    std = sb(scope, "p_std", [P, TPB])
    rstd = sb(scope, "p_rstd", [P, TPB])
    slw = sb(scope, "p_slw", [P, DH, D])
    slT = sb(scope, "p_slT", [P, DH, D])
    slb = sb(scope, "p_slb", [P, D])
    zero = sb(scope, "p_zero", [P, 2640])
    raw = sb(scope, "p_raw", [MC, 4, P], I32)
    rows = sb(scope, "p_rows", [MC, 4, P])
    key = sb(scope, "p_key", [MC, 2, P])
    junk = sb(scope, "p_junk", [MC, P])
    ow = sb(scope, "p_ow", [MC, 4])
    oi = sb(scope, "p_oi", [MC, 2], I32)
    over = sb(scope, "p_over", [MC, 4])
    bad = sb(scope, "p_bad", [MC, 4])
    bad_sum = sb(scope, "p_bad_sum", [MC, 4])
    due = sb(scope, "p_due", [MC, 1])
    bad_row = sb(scope, "p_bad_row", [MC, 1])
    first_of = sb(scope, "p_first_of", [MC, MG, CH])
    p_hT = ps(scope, "pp_hT", [P, 2, 512])
    p_own = ps(scope, "pp_own", [P, 2, 512])
    p_cols = ps(scope, "pp_cols", [P, 2, 512])
    p_small = ps(scope, "pp_small", [P, 512])

    const_ok = sem("const_ok")
    masks_ok = sem("masks_ok")
    weights_in = sem("weights_in")
    sl_turned = sem("sl_turned")
    sl_ready = sem("sl_ready")
    zero_ok = sem("zero_ok")
    due_ok = sem("due_ok")
    zero_out = sem("zero_out")
    x_in = [sem(f"x_in{k}") for k in range(TPB)]
    stats_ok = sem("stats_ok")
    mv_ok = sem("mv_ok")
    var_ok = sem("var_ok")
    std_ok = sem("std_ok")
    rstd_ok = sem("rstd_ok")
    hn_ok = sem("hn_ok")
    xb_ok = sem("xb_ok")
    hT_ps = sem("hT_ps")
    hT_ok = sem("hT_ok")
    own_ps = sem("own_ps")
    own_ok = sem("own_ok")
    stored = [sem(f"stored{k}") for k in range(TPB)]
    raw_in = sem("raw_in")
    rows_ok = sem("rows_ok")
    base_ps = sem("base_ps")
    base_ok = sem("base_ok")
    w_ok = sem("w_ok")
    off_ok = sem("off_ok")
    key_half = sem("key_half")
    planes_ok = sem("planes_ok")
    bad_ok = sem("bad_ok")
    bad_added = sem("bad_added")
    cols_ps = sem("cols_ps")
    cols_ok = sem("cols_ok")
    starts_out = sem("starts_out")
    row_in = sem("row_in")
    bad_rowed = sem("bad_rowed")
    bad_ps = sem("bad_ps")
    flag_ok = sem("flag_ok")

    def edges(a, turn, shift=0):
        return a[bass.ds(turn * (MC * P) + shift, MC * P)].rearrange("(c p) -> c p", p=P)

    def tile(a, turn, k):
        return a[bass.ds(turn * (TPB * P) + k * P, P), :]

    with nc.Block() as block:
        @block.sync
        def _(sp):
            def load_x(turn, k):
                sp.dma_start(x_t[:, k, :], tile(x, turn, k)).then_inc(x_in[k], 16)

            def load_edges(turn):
                for n, (a, shift) in enumerate(((dst, 0), (typ, 0), (src, 0), (dst, 1))):
                    sp.dma_start(raw[:, n, :], edges(a, turn, shift)).then_inc(raw_in, 16)

            load_edges(0)
            for k in range(TPB):
                load_x(0, k)
            for h in range(DH):
                sp.dma_start(slw[:, h, :], sl_w[h * P:(h + 1) * P, :]).then_inc(weights_in, 16)
            sp.dma_start(slb[:, :], sl_b.rearrange("(a n) -> a n", a=1).to_broadcast((P, D))).then_inc(weights_in, 16)
            for h in range(DH):
                sp.dma_start(w_sb[:, h, :, :], w_rel[:, h * P:(h + 1) * P, :].rearrange("r p n -> p r n")).then_inc(weights_in, 16)
            sp.wait_ge(zero_ok, 1)
            flat = sums.rearrange("(p a) w -> p (a w)", p=P)
            for n in range(10):
                sp.dma_start(flat[:, n * 2640:(n + 1) * 2640], zero[:, :]).then_inc(zero_out, 16)

            def turn(i, first, last):
                sp.wait_ge(rows_ok, i + 1)
                if not last:
                    load_edges(i + 1)
                for k in range(TPB):
                    sp.wait_ge(hn_ok, i * TPB + k + 1)
                    sp.dma_start(tile(table, i, k), hn[:, k, :]).then_inc(stored[k], 16)
                    if not last:
                        sp.wait_ge(xb_ok, i * TPB + k + 1)
                        load_x(i + 1, k)
                sp.wait_ge(off_ok, i * 2 + 2)
                for n in range(2):
                    sp.dma_start(starts[n, bass.ds(i * MC, MC)].rearrange("(c a) -> c a", a=1), oi[:, n:n + 1]).then_inc(starts_out, 16)
                for k in range(TPB):
                    sp.wait_ge(own_ok, i * TPB + k + 1)
                    sp.dma_start(tile(base, i, k), own[:, k, :]).then_inc(stored[k], 16)

            several(sp, PREPS, turn)
            sp.wait_ge(starts_out, 32 * PREPS)
            sp.dma_start(start_row[0:1, :, :], starts.rearrange("(o a) c -> o a c", o=1)).then_inc(row_in, 16)
            sp.wait_ge(row_in, 16)
            sp.wait_ge(zero_out, 160)
            for k in range(TPB):
                sp.wait_ge(stored[k], 32 * PREPS)

        @block.gpsimd
        def _(pool):
            nc.gpsimd.memset(ident[:, :], 0.0)
            nc.gpsimd.memset(first_of[:, :, :], 0.0)
            nc.gpsimd.memset(ones[:, :], 1.0).then_inc(const_ok, 1)
            pool.wait_ge(const_ok, 1)
            nc.gpsimd.affine_select(out=ident[:, :], in_=ident[:, :], compare_op=ALU.not_equal, fill=1.0,
                                    base=0, pattern=[[-1, P]], channel_multiplier=1).then_inc(masks_ok, 1)
            nc.gpsimd.affine_select(out=first_of[:, :, :], in_=first_of[:, :, :], compare_op=ALU.not_equal, fill=1.0,
                                    base=0, pattern=[[-CH, MG], [0, CH]], channel_multiplier=1).then_inc(masks_ok, 1)
            nc.gpsimd.memset(due[:, :], float(-NP)).then_inc(due_ok, 1)
            for n in range(MG):
                for k in range(TPB):
                    turns, g = divmod(k + LAG - 2, MG)
                    if g == n:
                        pool.wait_ge(due_ok, n + 1 - (n > (LAG - 3) % MG))
                        nc.gpsimd.affine_select(out=due[:, :], in_=due[:, :], compare_op=ALU.not_equal,
                                                fill=float(P * (k + 1) - turns * TPB * P), base=-n * CH,
                                                pattern=[[0, 1]], channel_multiplier=1).then_inc(due_ok, 1)
            nc.gpsimd.memset(zero[:, :], 0.0).then_inc(zero_ok, 1)
            pool.wait_ge(weights_in, 16 * (2 * DH + 1))

            def turn(i, first, last):
                for k in range(TPB):
                    pool.wait_ge(x_in[k], i * 16 + 16)
                    if not first:
                        pool.wait_ge(own_ok, (i - 1) * TPB + k + 1)
                    nc.gpsimd.tensor_tensor(xb[:, k, :], x_t[:, k, :], slb[:, :], ALU.add).then_inc(xb_ok, 1)

            several(pool, PREPS, turn)

        @block.vector
        def _(dve):
            nc.vector.memset(bad_sum[:, :], 0.0).then_inc(bad_added, 1)
            dve.wait_ge(due_ok, TPB + 1)
            for h in range(DH):
                dve.wait_ge(sl_turned, h + 1)
                nc.vector.tensor_copy(slT[:, h, :], p_own[:, h, 0:D]).then_inc(sl_ready, 1)

            def convert(i, first):
                dve.wait_ge(raw_in, i * 64 + 64)
                if not first:
                    dve.wait_ge(cols_ps, i)
                    dve.wait_ge(planes_ok, i * 2)
                nc.vector.tensor_copy(rows[:, :, :], raw[:, :, :]).then_inc(rows_ok, 1)

            def order(i, first):
                dve.wait_ge(rows_ok, i + 1)
                if not first:
                    dve.wait_ge(bad_added, i + 1)
                dve.sem_inc(passed, 1)
                nc.vector.tensor_tensor_reduce(junk[:, :], rows[:, 0, :], rows[:, 3, :], 1.0, 0.0, ALU.subtract,
                                               ALU.max, over[:, 0:1]).then_inc(bad_ok, 1)

            def window(i, first):
                dve.wait_ge(base_ps, i + 1)
                if not first:
                    dve.wait_ge(off_ok, i * 2)
                nc.vector.tensor_copy(ow[:, 1:2], p_small[0:MC, 0:1]).then_inc(base_ok, 1)
                dve.wait_ge(base_ok, i + 1)
                nc.vector.tensor_scalar(ow[:, 2:3], ow[:, 1:2], float(WIN - LOC), rows[:, 0, 0:1], ALU.add, ALU.min).then_inc(w_ok, 1)

            def half_key(i):
                nc.vector.scalar_tensor_tensor(out=key[:, 0, :], in0=rows[:, 1, :], scalar=float(LOC), in1=rows[:, 0, :],
                                               op0=ALU.mult, op1=ALU.add).then_inc(key_half, 1)
                nc.vector.tensor_scalar(key[:, 1, :], rows[:, 0, :], ow[:, 1:2], None, ALU.subtract).then_inc(planes_ok, 1)

            def offsets(i, first):
                dve.wait_ge(w_ok, i + 1)
                nc.vector.tensor_scalar(ow[:, 0:1], ow[:, 2:3], ow[:, 1:2], None, ALU.subtract).then_inc(off_ok, 1)
                dve.wait_ge(off_ok, i * 2 + 1)
                if not first:
                    dve.wait_ge(starts_out, i * 32)
                nc.vector.tensor_copy(oi[:, :], ow[:, 0:2]).then_inc(off_ok, 1)

            def full_key(i):
                dve.wait_ge(key_half, i + 1)
                nc.vector.tensor_scalar(key[:, 0, :], key[:, 0, :], ow[:, 2:3], None, ALU.subtract).then_inc(planes_ok, 1)

            def spans(i):
                for n, (start, width) in enumerate(((rows[:, 0, 0:1], LOC), (ow[:, 1:2], WIN))):
                    nc.vector.tensor_scalar(over[:, n + 1:n + 2], rows[:, 0, P - 1:P], float(N - 1), start,
                                            ALU.min, ALU.subtract).then_inc(bad_ok, 1)
                nc.vector.tensor_scalar(over[:, 3:4], due[:, :], ow[:, 1:2], None, ALU.subtract).then_inc(bad_ok, 1)
                dve.wait_ge(bad_ok, i * 9 + 4)
                nc.vector.tensor_scalar(due[:, :], due[:, :], float(TPB * P), None, ALU.add).then_inc(bad_ok, 1)
                for n, most in enumerate((0, LOC - 1, WIN - 1, 0)):
                    nc.vector.tensor_scalar(bad[:, n:n + 1], over[:, n:n + 1], most + 0.5, None, ALU.is_gt).then_inc(bad_ok, 1)
                dve.wait_ge(bad_ok, i * 9 + 9)
                dve.wait_ge(bad_added, i + 1)
                nc.vector.tensor_tensor(bad_sum[:, :], bad_sum[:, :], bad[:, :], ALU.add).then_inc(bad_added, 1)

            def turn(i, first, last):
                n0 = i * TPB
                convert(i, first)
                if not first:
                    dve.wait_ge(hn_ok, n0)
                for k in range(TPB):
                    dve.wait_ge(x_in[k], i * 16 + 16)
                    nc.vector.bn_stats(stats[:, k, :], x_t[:, k, :]).then_inc(stats_ok, 1)
                order(i, first)
                for k in range(TPB):
                    if k == 0:
                        dve.wait_ge(stats_ok, n0 + TPB)
                        dve.sem_inc(passed, 1)
                    nc.vector.bn_aggr(mv[:, k, :], stats[:, k, :]).then_inc(mv_ok, 1)
                dve.wait_ge(mv_ok, n0 + TPB)
                nc.vector.tensor_scalar(var[:, :], mv[:, :, 1], EPS, None, ALU.add).then_inc(var_ok, 1)
                window(i, first)
                dve.wait_ge(base_ok, i + 1)
                half_key(i)
                offsets(i, first)
                full_key(i)
                dve.wait_ge(std_ok, i + 1)
                nc.vector.reciprocal(rstd[:, :], std[:, :]).then_inc(rstd_ok, 1)
                dve.wait_ge(rstd_ok, i + 1)
                for k in range(TPB):
                    if not first:
                        dve.wait_ge(stored[k], i * 32)
                        dve.wait_ge(hT_ps, (i - 1) * TPB + k + 1)
                    nc.vector.tensor_scalar(hn[:, k, :], x_t[:, k, :], mv[:, k, 0:1], rstd[:, k:k + 1],
                                            ALU.subtract, ALU.mult).then_inc(hn_ok, 1)
                spans(i)
                for k in range(TPB):
                    dve.wait_ge(own_ps, n0 + k + 1)
                    dve.wait_ge(xb_ok, n0 + k + 1)
                    nc.vector.tensor_tensor(own[:, k, :], p_own[:, k % 2, 0:D], xb[:, k, :], ALU.add).then_inc(own_ok, 1)

            several(dve, PREPS, turn)
            dve.wait_ge(bad_added, PREPS + 1)
            nc.vector.reduce_sum(bad_row[:, :], bad_sum[:, :], AX_X).then_inc(bad_rowed, 1)
            dve.wait_ge(bad_ps, 1)
            nc.vector.tensor_scalar(flag[:, :], p_small[0:1, 0:1], 0.5, None, ALU.is_gt).then_inc(flag_ok, 1)

        @block.scalar
        def _(act):
            def turn(i, first, last):
                act.wait_ge(var_ok, i + 1)
                if not first:
                    act.wait_ge(rstd_ok, i)
                nc.scalar.activation(std[:, :], var[:, :], ACT.Sqrt).then_inc(std_ok, 1)
                for k in range(TPB):
                    n = i * TPB + k
                    act.wait_ge(hT_ps, n + 1)
                    if not (first and k < 2):
                        act.wait_ge(own_ps, reused(i, k, 2, TPB))
                    nc.scalar.activation(hT[:, k % 2, :, :], p_hT[:, k % 2, 0:D].rearrange("p (h n) -> p h n", h=DH), ACT.Copy).then_inc(hT_ok, 1)
                act.wait_ge(cols_ps, i + 1)
                act.sem_inc(passed, 1)
                nc.scalar.activation(meta[:, 0:4, bass.ds(i * MC, MC)], p_cols[:, 0, :].rearrange("p (a c) -> p a c", a=4)[:, :, 0:MC], ACT.Copy)
                nc.scalar.activation(meta[:, 4, bass.ds(i * MC, MC)], p_cols[:, 1, 0:MC], ACT.Copy).then_inc(cols_ok, 1)

            several(act, PREPS, turn)

        @block.tensor
        def _(pe):
            pe.wait_ge(masks_ok, 2)
            pe.wait_ge(weights_in, 16 * (2 * DH + 1))
            for h in range(DH):
                for g in range(DH):
                    last = nc.tensor.transpose(p_own[:, h, g * P:(g + 1) * P], slw[:, g, h * P:(h + 1) * P], ident[:, :])
                last.then_inc(sl_turned, 1)
            pe.wait_ge(sl_ready, DH)

            def own_product(i, k, first):
                n = i * TPB + k
                pe.wait_ge(hT_ok, n + 1)
                if not (first and k < 2):
                    pe.wait_ge(own_ok, reused(i, k, 2, TPB))
                for h in range(DH):
                    last = nc.tensor.matmul(p_own[:, k % 2, 0:D], hT[:, k % 2, h, :], slT[:, h, :], start=(h == 0), stop=(h == DH - 1))
                last.then_inc(own_ps, 1)

            def turn(i, first, last):
                pe.wait_ge(rows_ok, i + 1)
                if not first:
                    pe.wait_ge(base_ok, i)
                nc.tensor.matmul(p_small[0:MC, 0:1], first_of[:, :, :].rearrange("p g c -> p (g c)"), rows[:, 0, 0:1],
                                 start=True, stop=True).then_inc(base_ps, 1)
                for k in range(TPB):
                    n = i * TPB + k
                    pe.wait_ge(hn_ok, n + 1)
                    if not (first and k < 2):
                        pe.wait_ge(hT_ok, reused(i, k, 2, TPB))
                    for h in range(DH):
                        t = nc.tensor.transpose(p_hT[:, k % 2, h * P:(h + 1) * P], hn[:, k, h * P:(h + 1) * P], ident[:, :])
                    t.then_inc(hT_ps, 1)
                    if k:
                        own_product(i, k - 1, first)
                own_product(i, TPB - 1, first)
                pe.wait_ge(planes_ok, i * 2 + 2)
                if not first:
                    pe.wait_ge(cols_ok, i)
                for n, plane in enumerate((rows[:, 2, :], key[:, 0, :], key[:, 1, :], rows[:, 0, :], rows[:, 1, :])):
                    t = nc.tensor.transpose(p_cols[:, n // 4, (n % 4) * P:(n % 4) * P + MC], plane, ident[0:MC, 0:MC])
                t.then_inc(cols_ps, 1)

            several(pe, PREPS, turn)
            pe.wait_ge(bad_rowed, 1)
            nc.tensor.matmul(p_small[0:1, 0:1], bad_row[:, :], ones[0:MC, 0:1], start=True, stop=True).then_inc(bad_ps, 1)


def main_pass(nc, scope, sb, ps, sem, passed, table, base, sums, x1, slices, w_x, b_x, w_slice, b_slice, temp,
              ident, ones, meta, w_sb, start_row, flag, tok, tok_sum):
    SR, CR = 5, 2
    rows = sb(scope, "a_rows", [P, 2, CH, D])
    idx = sb(scope, "a_idx", [P, 2, CH], U32)
    kd = sb(scope, "a_kd", [P, 2, 2, CH])
    spot = sb(scope, "a_spot", [P, SR, P])
    hits = sb(scope, "a_hits", [P, SR, P], BF16)
    acc = sb(scope, "a_acc", [P, 2, DH * R, WIN])
    res = sb(scope, "a_res", [P, 2, MW])
    count = sb(scope, "a_count", [P, P])
    zeros = sb(scope, "a_zeros", [P, DH * R * WIN])
    ones_bf = sb(scope, "a_ones_bf", [P, 1], BF16)
    p_chunk = ps(scope, "ap_chunk", [P, CR, 512])
    p_acc = ps(scope, "ap_acc", [P, 2, 512])
    p_tok = ps(scope, "sp_tok", [P, 4, D])
    p_lg = ps(scope, "sp_lg", [P, HG])
    p_x = ps(scope, "sp_x", [P, 512])
    p_sum = p_x[:, D:D + 4]
    wx = sb(scope, "s_wx", [P, DH, HG])
    wxT = sb(scope, "s_wxT", [C, H, P])
    ws = sb(scope, "s_ws", [C, G])
    bxT = sb(scope, "s_bxT", [C, H])
    bsl = sb(scope, "s_bsl", [1, G])
    brow = sb(scope, "s_brow", [1, HG])
    bfull = sb(scope, "s_bfull", [P, HG])
    wxs = sb(scope, "s_wxs", [P, DH, HG])
    tmp = sb(scope, "s_tmp", [P, H])
    rtmp = sb(scope, "s_rtmp", [P, H])
    real = sb(scope, "s_real", [P, TILES])
    m = sb(scope, "s_m", [P, MW])
    bs = sb(scope, "s_bs", [P, D])
    deg = sb(scope, "s_deg", [P, 2])
    xs = sb(scope, "s_xs", [P, D])
    stats = sb(scope, "s_stats", [P, 6])
    mv = sb(scope, "s_mv", [P, 2])
    dev = sb(scope, "s_dev", [P, 3])
    xn = sb(scope, "s_xn", [P, D])
    xT = sb(scope, "s_xT", [P, DH, P])
    lg = sb(scope, "s_lg", [P, HG])
    top = sb(scope, "s_top", [P, 2, H])
    ex = sb(scope, "s_ex", [P, HG])
    tot = sb(scope, "s_tot", [P, H])
    inv = sb(scope, "s_inv", [P, 2, H])
    sw = sb(scope, "s_sw", [P, HG])
    one_idx = sb(scope, "g_idx", [P, 1], U32)
    row_idx = sb(scope, "g_row_idx", [P, 1], U32)
    dt = sb(scope, "g_dt", [P, 2])
    mask = sb(scope, "g_mask", [P, R])
    diag = sb(scope, "g_diag", [P, P])
    same = sb(scope, "g_same", [P, P])
    below = sb(scope, "g_below", [P, P])
    spill = sb(scope, "g_spill", [P, P])
    trash = sb(scope, "g_trash", [P, 1])
    pick = sb(scope, "g_pick", [P, 4])
    gT = sb(scope, "g_gT", [P, DH, P])
    msg = sb(scope, "g_msg", [P, MW])
    wide = sb(scope, "g_wide", [P, MP])

    consts = sem("a_consts")
    idx_ok = sem("a_idx_ok")
    kd_ok = sem("a_kd_ok")
    acc_zero = sem("a_acc_zero")
    gathered = [[sem(f"a_gathered{b}_{c}") for c in range(CH)] for b in range(2)]
    built = sem("a_built")
    summed = sem("a_summed")
    added = sem("a_added")
    msg_ok = sem("a_msg_ok")
    res_ok = sem("a_res_ok")
    accumulated = sem("a_accumulated")

    g_idx_ok = sem("g_idx_ok")
    g_rows_in = sem("g_rows_in")
    g_dt_ok = sem("g_dt_ok")
    g_mask_ok = sem("g_mask_ok")
    g_diag_ok = sem("g_diag_ok")
    g_dst_ps = sem("g_dst_ps")
    g_same_ok = sem("g_same_ok")
    g_before_ok = sem("g_before_ok")
    g_pick_ok = sem("g_pick_ok")
    g_row_idx_ok = sem("g_row_idx_ok")
    g_turned = sem("g_turned")
    g_gT_ok = sem("g_gT_ok")
    g_part_ps = sem("g_part_ps")
    g_msg_ok = sem("g_msg_ok")
    g_comb_ps = sem("g_comb_ps")
    g_wide_ok = sem("g_wide_ok")
    g_scattered = sem("g_scattered")

    w_in = sem("s_w_in")
    real_ok = sem("s_real_ok")
    tmp_ok = sem("s_tmp_ok")
    wx_ps = sem("s_wx_ps")
    wx_ok = sem("s_wx_ok")
    m_in = sem("s_m_in")
    deg_ok = sem("s_deg_ok")
    xs_ok = sem("s_xs_ok")
    x1_out = sem("s_x1_out")
    stats_ok = sem("s_stats_ok")
    mv_ok = sem("s_mv_ok")
    var_ok = sem("s_var_ok")
    std_ok = sem("s_std_ok")
    rstd_ok = sem("s_rstd_ok")
    xn_ok = sem("s_xn_ok")
    xT_ps = sem("s_xT_ps")
    xT_ok = sem("s_xT_ok")
    lg_ps = sem("s_lg_ps")
    lg_ok = sem("s_lg_ok")
    top_ok = sem("s_top_ok")
    ex_ok = sem("s_ex_ok")
    inv_ok = sem("s_inv_ok")
    sw_ok = sem("s_sw_ok")
    sw_out = sem("s_sw_out")
    tok_ps = sem("s_tok_ps")
    sum_ok = sem("s_sum_ok")
    tok_ok = sem("s_tok_ok")

    def row(a):
        return a.rearrange("(a n) -> a n", a=1)

    def heads(a):
        return a.rearrange("p (h g) -> p h g", h=H)

    def per_head(a, rows=P):
        return a.rearrange("p (h a) -> p h a", a=1).to_broadcast((rows, H, G))

    def behind(eng, semaphore, count):
        if not (isinstance(count, int) and count == 0):
            eng.wait_ge(semaphore, count)

    def load_tile(sp, t):
        behind(sp, xs_ok, t)
        sp.dma_start(m[:, :], sums[bass.ds(t * P, P), 0:MW]).then_inc(m_in, 16)
        sp.dma_start(bs[:, :], base[bass.ds(t * P, P), :]).then_inc(m_in, 16)

    def store_x1(sp, t):
        sp.wait_ge(xs_ok, t + 1)
        sp.dma_start(x1[bass.ds(t * P, P), :], xs[:, :]).then_inc(x1_out, 16)

    def store_slices(sp, t):
        sp.wait_ge(sw_ok, t + 1)
        sp.dma_start(slices[bass.ds(t * P, P), :], sw[:, :]).then_inc(sw_out, 16)

    def tile_dve_early(dve, t, n):
        if n == 0:
            dve.wait_ge(m_in, t * 32 + 32)
            nc.vector.tensor_scalar(deg[:, 0:1], m[:, D:MW], 1.0, None, ALU.max).then_inc(deg_ok, 1)
        if n == 1:
            dve.wait_ge(deg_ok, t * 2 + 1)
            nc.vector.reciprocal(deg[:, 1:2], deg[:, 0:1]).then_inc(deg_ok, 1)
        if n == 2:
            behind(dve, x1_out, t * 16)
            dve.wait_ge(deg_ok, t * 2 + 2)
            nc.vector.scalar_tensor_tensor(out=xs[:, :], in0=m[:, 0:D], scalar=deg[:, 1:2], in1=bs[:, :],
                                           op0=ALU.mult, op1=ALU.add).then_inc(xs_ok, 1)
        if n == 3:
            dve.wait_ge(xs_ok, t + 1)
            nc.vector.bn_stats(stats[:, :], xs[:, :]).then_inc(stats_ok, 1)
        if n == 4:
            dve.wait_ge(stats_ok, t + 1)
            dve.sem_inc(passed, 1)
            nc.vector.bn_aggr(mv[:, :], stats[:, :]).then_inc(mv_ok, 1)
        if n == 5:
            dve.wait_ge(mv_ok, t + 1)
            nc.vector.tensor_scalar(dev[:, 0:1], mv[:, 1:2], EPS, None, ALU.add).then_inc(var_ok, 1)
        if n == 7:
            dve.wait_ge(std_ok, t + 1)
            nc.vector.reciprocal(dev[:, 2:3], dev[:, 1:2]).then_inc(rstd_ok, 1)
        if n == 8:
            behind(dve, tok_ps, t)
            dve.wait_ge(rstd_ok, t + 1)
            nc.vector.tensor_scalar(xn[:, :], xs[:, :], mv[:, 0:1], dev[:, 2:3], ALU.subtract, ALU.mult).then_inc(xn_ok, 1)
        if n == 12:
            behind(dve, ex_ok, t)
            dve.wait_ge(lg_ps, t + 1)
            nc.vector.tensor_tensor(lg[:, :], p_lg[:, :], bfull[:, :], ALU.add).then_inc(lg_ok, 1)
        if n == 13:
            dve.wait_ge(lg_ok, t + 1)
            nc.vector.reduce_max(top[:, 0, :], heads(lg[:, :]), AX_X).then_inc(top_ok, 1)
        if n == 14:
            dve.wait_ge(top_ok, t * 2 + 1)
            nc.vector.tensor_scalar(top[:, 1, :], top[:, 0, :], -1.0, None, ALU.mult).then_inc(top_ok, 1)

    def tile_dve_late(dve, t, n):
        if n == 1:
            dve.wait_ge(ex_ok, t + 1)
            nc.vector.reciprocal(inv[:, 0, :], tot[:, :]).then_inc(inv_ok, 1)
        if n == 2:
            dve.wait_ge(inv_ok, t * 2 + 1)
            nc.vector.tensor_scalar(inv[:, 1, :], inv[:, 0, :], real[:, bass.ds(t, 1)], None, ALU.mult).then_inc(inv_ok, 1)
        if n == 3:
            behind(dve, sw_out, t * 16)
            dve.wait_ge(inv_ok, t * 2 + 2)
            nc.vector.tensor_tensor(heads(sw[:, :]), heads(ex[:, :]), per_head(inv[:, 1, :]), ALU.mult).then_inc(sw_ok, 1)
        if n == 9:
            dve.wait_ge(sum_ok, t + 1)
            dve.wait_ge(tok_ps, t + 1)
            nc.vector.tensor_tensor(tok_sum[:, :], tok_sum[:, :], p_sum, ALU.add).then_inc(sum_ok, 1)

    def tile_dve_all(dve, t):
        for n in range(15):
            tile_dve_early(dve, t, n)
        for n in range(15):
            tile_dve_late(dve, t, n)

    def deviation(act, t):
        act.wait_ge(var_ok, t + 1)
        behind(act, rstd_ok, t)
        nc.scalar.activation(dev[:, 1:2], dev[:, 0:1], ACT.Sqrt).then_inc(std_ok, 1)

    def copy_xT(act, t):
        act.wait_ge(xT_ps, t + 1)
        nc.scalar.activation(xT[:, :, :], p_x[:, 0:D].rearrange("p (h n) -> p h n", h=DH), ACT.Copy).then_inc(xT_ok, 1)

    def exponentials(act, t):
        act.wait_ge(top_ok, t * 2 + 2)
        behind(act, sw_ok, t)
        for h in range(H):
            e = nc.scalar.activation(ex[:, h * G:(h + 1) * G], lg[:, h * G:(h + 1) * G], ACT.Exp,
                                     bias=top[:, 1, h:h + 1], accum_out=tot[:, h:h + 1])
        e.then_inc(ex_ok, 1)

    def tile_act_all(act, t):
        deviation(act, t)
        copy_xT(act, t)
        exponentials(act, t)

    def turn_tile(pe, t):
        pe.wait_ge(sum_ok, t + 1)
        pe.wait_ge(xn_ok, t + 1)
        for h in range(DH):
            e = nc.tensor.transpose(p_x[:, h * P:(h + 1) * P], xn[:, h * P:(h + 1) * P], ident[:, :])
        e.then_inc(xT_ps, 1)

    def logits(pe, t):
        behind(pe, lg_ok, t)
        pe.wait_ge(xT_ok, t + 1)
        for h in range(DH):
            e = nc.tensor.matmul(p_lg[:, :], xT[:, h, :], wxs[:, h, :], start=(h == 0), stop=(h == DH - 1))
        e.then_inc(lg_ps, 1)

    def tokens(pe, t):
        pe.wait_ge(sum_ok, t + 1)
        pe.wait_ge(sw_ok, t + 1)
        for j in range(4):
            nc.tensor.matmul(p_tok[:, j, :], sw[:, j * P:(j + 1) * P], xn[:, :],
                             start=(isinstance(t, int) and t == 0 and j % 2 == 0), stop=False, skip_group_check=True)
        for j in range(4):
            e = nc.tensor.matmul(p_sum[:, j:j + 1], sw[:, j * P:(j + 1) * P], ones[:, 0:1], start=True, stop=True)
        e.then_inc(tok_ps, 1)

    def tile_pe_all(pe, t):
        turn_tile(pe, t)
        logits(pe, t)
        tokens(pe, t)

    def tile_at(i, place):
        if place < LAG - 1:
            return None if isinstance(i, int) and i == 0 else i * TPB + place + TPB + 1 - LAG - TPB
        return None if place == LAG - 1 else i * TPB + place - LAG

    def tile_before(i, place):
        if place:
            return tile_at(i, place - 1)
        return None if isinstance(i, int) and i == 0 else i * TPB + MG - 1 - LAG - TPB

    def general_pool(pool):
        nc.gpsimd.iota(trash[:, :], pattern=[[0, 1]], base=TRASH, channel_multiplier=1,
                       allow_small_or_imprecise_dtypes=True).then_inc(consts, 1)
        nc.gpsimd.memset(wide[:, :], 0.0).then_inc(consts, 1)
        nc.gpsimd.memset(below[:, :], 1.0).then_inc(consts, 1)
        pool.wait_ge(consts, 6)
        nc.gpsimd.affine_select(out=below[:, :], in_=below[:, :], compare_op=ALU.is_gt, fill=0.0, base=0,
                                pattern=[[-1, P]], channel_multiplier=1).then_inc(consts, 1)

        def turn(j, first, last):
            pool.wait_ge(g_idx_ok, j + 1)
            pool.sem_inc(passed, 1)
            pool.indirect_dma_start(out=rows[:, 0, 0, :], out_offset=None, in_=table,
                                    in_offset=bass.IndirectOffsetOnAxis(ap=one_idx[:, 0:1], axis=0)).then_inc(g_rows_in, 16)
            pool.wait_ge(g_wide_ok, j + 1)
            pool.sem_inc(passed, 1)
            pool.wait_ge(g_row_idx_ok, j + 1)
            pool.sem_inc(passed, 1)
            pool.indirect_dma_start(out=sums, out_offset=bass.IndirectOffsetOnAxis(ap=row_idx[:, 0:1], axis=0),
                                    in_=wide[:, :], in_offset=None, compute_op=ALU.add).then_inc(g_scattered, 16)
            pool.wait_ge(g_scattered, j * 16 + 16)
            pool.sem_inc(passed, 1)

        several(pool, CHUNKS, turn)

    def general_act(act):
        def turn(j, first, last):
            if not first:
                act.wait_ge(g_rows_in, j * 16)
                act.sem_inc(passed, 1)
            nc.scalar.activation(one_idx[:, 0:1], meta[:, 0, bass.ds(j, 1)], ACT.Copy).then_inc(g_idx_ok, 1)
            act.wait_ge(g_turned, j + 1)
            if not first:
                act.wait_ge(g_part_ps, j * R)
            nc.scalar.activation(gT[:, :, :], p_chunk[:, 1, 0:D].rearrange("p (h n) -> p h n", h=DH), ACT.Copy).then_inc(g_gT_ok, 1)
            act.wait_ge(g_comb_ps, j + 1)
            if not first:
                act.wait_ge(g_scattered, j * 16)
            nc.scalar.activation(wide[:, 0:MW], p_lg[:, 0:MW], ACT.Copy).then_inc(g_wide_ok, 1)

        act.wait_ge(consts, 7)
        several(act, CHUNKS, turn)
        several(act, TILES, lambda t, first, last: tile_act_all(act, t))

    def general_dve(dve):
        dve.wait_ge(consts, 7)
        nc.vector.memset(msg[:, D:MW], 1.0).then_inc(g_before_ok, 1)

        def turn(j, first, last):
            if not first:
                dve.wait_ge(g_row_idx_ok, j)
                dve.wait_ge(g_mask_ok, j)
                dve.sem_inc(passed, 1)
            nc.vector.tensor_copy(dt[:, :], meta[:, 3:5, bass.ds(j, 1)].rearrange("p a c -> p (a c)")).then_inc(g_dt_ok, 1)
            dve.wait_ge(g_dt_ok, j + 1)
            if not first:
                dve.wait_ge(g_msg_ok, j * R)
            nc.vector.tensor_scalar(mask[:, :], count[:, 0:R], dt[:, 1:2], None, ALU.is_equal).then_inc(g_mask_ok, 1)
            if not first:
                dve.wait_ge(g_dst_ps, j)
            nc.vector.tensor_scalar(diag[:, :], ident[:, :], dt[:, 0:1], None, ALU.mult).then_inc(g_diag_ok, 1)
            dve.wait_ge(g_dst_ps, j + 1)
            if not first:
                dve.wait_ge(g_comb_ps, j)
            nc.vector.tensor_scalar(same[:, :], p_chunk[:, 0, 0:P], dt[:, 0:1], None, ALU.is_equal).then_inc(g_same_ok, 1)
            dve.wait_ge(g_same_ok, j + 1)
            dve.wait_ge(g_before_ok, j + 1)
            nc.vector.tensor_tensor_reduce(spill[:, :], same[:, :], below[:, :], 1.0, 0.0, ALU.mult, ALU.add,
                                           pick[:, 0:1]).then_inc(g_before_ok, 1)
            dve.wait_ge(g_before_ok, j + 2)
            nc.vector.tensor_scalar(pick[:, 1:2], pick[:, 0:1], 0.5, None, ALU.is_lt).then_inc(g_pick_ok, 1)
            nc.vector.tensor_tensor(pick[:, 2:3], dt[:, 0:1], trash[:, :], ALU.subtract).then_inc(g_pick_ok, 1)
            dve.wait_ge(g_pick_ok, j * 3 + 2)
            nc.vector.tensor_tensor(pick[:, 3:4], pick[:, 2:3], pick[:, 1:2], ALU.mult).then_inc(g_pick_ok, 1)
            dve.wait_ge(g_pick_ok, j * 3 + 3)
            if not first:
                dve.wait_ge(g_scattered, j * 16)
            nc.vector.tensor_tensor(row_idx[:, :], pick[:, 3:4], trash[:, :], ALU.add).then_inc(g_row_idx_ok, 1)
            dve.wait_ge(g_mask_ok, j + 1)
            for r in range(R):
                dve.wait_ge(g_part_ps, j * R + r + 1)
                if r == 0:
                    if not first:
                        dve.wait_ge(g_comb_ps, j)
                    nc.vector.tensor_scalar(msg[:, 0:D], p_acc[:, 0, 0:D], mask[:, 0:1], None, ALU.mult).then_inc(g_msg_ok, 1)
                    continue
                dve.wait_ge(g_msg_ok, j * R + r)
                nc.vector.scalar_tensor_tensor(out=msg[:, 0:D], in0=p_acc[:, r % 2, 0:D], scalar=mask[:, r:r + 1],
                                               in1=msg[:, 0:D], op0=ALU.mult, op1=ALU.add).then_inc(g_msg_ok, 1)

        several(dve, CHUNKS, turn)
        several(dve, TILES, lambda t, first, last: tile_dve_all(dve, t))

    def general_pe(pe):
        pe.wait_ge(consts, 7)

        def turn(j, first, last):
            pe.wait_ge(g_diag_ok, j + 1)
            if not first:
                pe.wait_ge(g_same_ok, j)
            nc.tensor.matmul(p_chunk[:, 0, 0:P], ones[:, :], diag[:, :], start=True, stop=True).then_inc(g_dst_ps, 1)
            pe.wait_ge(g_rows_in, j * 16 + 16)
            if not first:
                pe.wait_ge(g_gT_ok, j)
            for h in range(DH):
                t = nc.tensor.transpose(p_chunk[:, 1, h * P:(h + 1) * P], rows[:, 0, 0, h * P:(h + 1) * P], ident[:, :])
            t.then_inc(g_turned, 1)
            pe.wait_ge(g_gT_ok, j + 1)
            for r in range(R):
                if not first or r >= 2:
                    pe.wait_ge(g_msg_ok, j * R + r - 1)
                for h in range(DH):
                    m = nc.tensor.matmul(p_acc[:, r % 2, 0:D], gT[:, h, :], w_sb[:, h, r, :], start=(h == 0), stop=(h == DH - 1))
                m.then_inc(g_part_ps, 1)
            pe.wait_ge(g_msg_ok, j * R + R)
            if not first:
                pe.wait_ge(g_wide_ok, j)
            nc.tensor.matmul(p_lg[:, 0:MW], same[:, :], msg[:, :], start=True, stop=True).then_inc(g_comb_ps, 1)

        several(pe, CHUNKS, turn)
        several(pe, TILES, lambda t, first, last: tile_pe_all(pe, t))

    def general_sp(sp):
        sp.wait_ge(g_scattered, CHUNKS * 16)
        load_tile(sp, 0)

        def turn(t, first, last):
            store_x1(sp, t)
            if not last:
                load_tile(sp, t + 1)
            store_slices(sp, t)

        several(sp, TILES, turn)

    with nc.Block() as block:
        @block.sync
        def _(sp):
            for h in range(DH):
                sp.dma_start(wx[:, h, :], w_x[h * P:(h + 1) * P, :]).then_inc(w_in, 16)
            sp.dma_start(ws[:, :], w_slice).then_inc(w_in, 16)
            for h in range(H):
                sp.dma_start(bxT[:, h:h + 1], b_x[h * C:(h + 1) * C].rearrange("(c a) -> c a", a=1)).then_inc(w_in, 16)
            sp.dma_start(bsl[:, :], row(b_slice)).then_inc(w_in, 16)
            sp.dma_start(tmp[:, :], temp.rearrange("a h b c -> (a b c) h").to_broadcast((P, H))).then_inc(w_in, 16)
            general = sp.value_load(flag[0:1, 0:1], min_val=0, max_val=1)
            with sp.If(general == 0):
                def load_behind(t, step):
                    sp.wait_ge(accumulated, (step - 2) * 16)
                    load_tile(sp, t)

                load_behind(0, LAG)

                def turn(i, first, last):
                    for place in range(MG):
                        t = tile_at(i, place)
                        if t is None:
                            continue
                        store_x1(sp, t)
                        ahead = 2 if place == LAG - 2 else 1
                        load_behind(t + 1, i * MG + place + ahead)
                        store_slices(sp, t)

                several(sp, PREPS, turn)
                for t in range(TILES - LAG + 1, TILES):
                    store_x1(sp, t)
                    if t < TILES - 1:
                        load_behind(t + 1, min(t + 1 - (TILES - LAG + 1) + GROUPS, GROUPS + 2))
                    store_slices(sp, t)
            with sp.Else():
                general_sp(sp)
            sp.wait_ge(x1_out, TILES * 16)
            sp.wait_ge(sw_out, TILES * 16)

        @block.gpsimd
        def _(pool):
            nc.gpsimd.iota(count[:, :], pattern=[[1, P]], base=0, channel_multiplier=0,
                           allow_small_or_imprecise_dtypes=True).then_inc(consts, 1)
            nc.gpsimd.memset(zeros[:, :], 0.0).then_inc(consts, 1)
            nc.gpsimd.memset(ones_bf[:, :], 1.0).then_inc(consts, 1)
            nc.gpsimd.memset(real[:, :], 1.0).then_inc(real_ok, 1)
            pool.wait_ge(real_ok, 1)
            nc.gpsimd.affine_select(out=real[:, :], in_=real[:, :], compare_op=ALU.is_gt, fill=0.0, base=N,
                                    pattern=[[-P, TILES]], channel_multiplier=-1).then_inc(real_ok, 1)
            general = pool.value_load(flag[0:1, 0:1], min_val=0, max_val=1)
            with pool.If(general == 0):
                def accumulate(g, b):
                    start = pool.value_load(start_row[0:1, 1, bass.ds(g * CH, 1)], min_val=0, max_val=NP)
                    pool.wait_ge(res_ok, g + 1)
                    pool.sem_inc(passed, 1)
                    pool.dma_start(sums[bass.ds(start, WIN), 0:MW], res[:, b, :], accum_op=ALU.add).then_inc(accumulated, 16)

                def turn(i, first, last):
                    for place in range(MG):
                        b = place % 2
                        g = i * MG + place
                        pool.wait_ge(idx_ok, g + 1)
                        pool.sem_inc(passed, 1)
                        for c in range(CH):
                            if not (first and place < 2):
                                pool.wait_ge(summed, (g - 2) * CH + c + 1)
                                pool.sem_inc(passed, 1)
                                if c == 5:
                                    accumulate(g - 2, b)
                                if c == CH - 1:
                                    pool.wait_ge(accumulated, (g - 1) * 16)
                                    pool.sem_inc(passed, 1)
                            pool.indirect_dma_start(
                                out=rows[:, b, c, :], out_offset=None, in_=table,
                                in_offset=bass.IndirectOffsetOnAxis(ap=idx[:, b, c:c + 1], axis=0),
                            ).then_inc(gathered[b][c], 16)

                several(pool, PREPS, turn)
                for g in (GROUPS - 2, GROUPS - 1):
                    accumulate(g, g % 2)
                    pool.wait_ge(accumulated, 16 * (g + 1))
            with pool.Else():
                general_pool(pool)

        @block.scalar
        def _(act):
            act.wait_ge(consts, 3)
            general = act.value_load(flag[0:1, 0:1], min_val=0, max_val=1)
            with act.If(general == 0):
                def lists(g, b):
                    nc.scalar.activation(idx[:, b, :], meta[:, 0, bass.ds(g * CH, CH)], ACT.Copy).then_inc(idx_ok, 1)
                    nc.scalar.activation(kd[:, b, :, :], meta[:, 1:3, bass.ds(g * CH, CH)], ACT.Copy).then_inc(kd_ok, 1)

                def clear(g, b):
                    nc.scalar.activation(acc[:, b, :, :].rearrange("p a n -> p (a n)"), zeros[:, :], ACT.Copy).then_inc(acc_zero, 1)

                def collect(g, b, early):
                    if not early:
                        act.wait_ge(accumulated, (g - 1) * 16)
                    act.wait_ge(msg_ok, g + 1)
                    nc.scalar.activation(res[:, b, 0:D], p_acc[:, b, 0:D], ACT.Copy)
                    nc.scalar.activation(res[:, b, D:MW], p_acc[:, b, D:MW], ACT.Copy).then_inc(res_ok, 1)

                for n in range(2):
                    lists(n, n)
                    clear(n, n)

                def turn(i, first, last):
                    for place in range(MG):
                        g = i * MG + place
                        b = place % 2
                        t, before = tile_at(i, place), tile_before(i, place)
                        if before is not None:
                            exponentials(act, before)
                        early = first and place == 0
                        final = last and place == MG - 1
                        if not early and not final:
                            act.wait_ge(summed, g * CH)
                            act.sem_inc(passed, 1)
                            lists(g + 1, 1 - b)
                        if t is not None:
                            deviation(act, t)
                            copy_xT(act, t)
                        if not early:
                            if not final:
                                act.wait_ge(msg_ok, g)
                                clear(g + 1, 1 - b)
                            collect(g - 1, 1 - b, first and place <= 2)

                several(act, PREPS, turn)
                exponentials(act, TILES - LAG)
                collect(GROUPS - 1, 1, False)
                for t in range(TILES - LAG + 1, TILES):
                    tile_act_all(act, t)
            with act.Else():
                general_act(act)

        @block.vector
        def _(dve):
            nc.vector.memset(tok_sum[:, :], 0.0).then_inc(sum_ok, 1)
            dve.wait_ge(consts, 3)
            dve.wait_ge(real_ok, 2)
            dve.wait_ge(w_in, 16 * (DH + H + 3))
            nc.vector.tensor_scalar(tmp[:, :], tmp[:, :], 0.1, 5.0, ALU.max, ALU.min).then_inc(tmp_ok, 1)
            dve.wait_ge(tmp_ok, 1)
            nc.vector.reciprocal(rtmp[:, :], tmp[:, :]).then_inc(tmp_ok, 1)
            dve.wait_ge(tmp_ok, 2)
            for h in range(DH):
                dve.wait_ge(wx_ps, 2 * h + 1)
                nc.vector.tensor_copy(wxT[:, :, :], p_tok[0:C, :, :].rearrange("p a (b n) -> p (a b) n", n=P)).then_inc(wx_ok, 1)
                dve.wait_ge(wx_ps, 2 * h + 2)
                nc.vector.tensor_tensor(heads(wxs[:, h, :]), heads(p_lg[:, :]), per_head(rtmp[:, :]), ALU.mult).then_inc(wx_ok, 1)
            dve.wait_ge(wx_ps, 2 * DH + 1)
            nc.vector.tensor_tensor(heads(brow[:, :]), heads(p_x[0:1, :]), per_head(rtmp[0:1, :], 1), ALU.mult).then_inc(wx_ok, 1)
            dve.wait_ge(wx_ps, 2 * DH + 2)
            nc.vector.tensor_copy(bfull[:, :], p_x[:, :]).then_inc(wx_ok, 1)
            dve.wait_ge(wx_ok, 2 * DH + 2)
            general = dve.value_load(flag[0:1, 0:1], min_val=0, max_val=1)
            with dve.If(general == 0):
                def build(g, b, c, fresh):
                    q = g * CH + c
                    if c == 0:
                        dve.wait_ge(kd_ok, g + 1)
                    if not fresh:
                        dve.wait_ge(summed, q - SR + 1)
                    nc.vector.tensor_scalar(spot[:, c % SR, :], count[:, :], kd[:, b, 0, c:c + 1], None, ALU.is_equal)
                    nc.vector.tensor_scalar(hits[:, c % SR, :], count[:, :], kd[:, b, 1, c:c + 1], None, ALU.is_equal).then_inc(built, 1)

                def add(g, b, c, slot, at, early):
                    q = g * CH + c
                    if c == 0:
                        dve.wait_ge(acc_zero, g + 1)
                    if not (early and c == 0):
                        dve.wait_ge(added, q)
                    dve.wait_ge(summed, q + 1)
                    a = acc[:, b, :, bass.ds(at, LOC)]
                    nc.vector.tensor_tensor(a, a, p_chunk[:, slot, 0:D].rearrange("p (a l) -> p a l", l=LOC), ALU.add).then_inc(added, 1)

                build(0, 0, 0, True)
                build(0, 0, 1, True)

                def turn(i, first, last):
                    for place in range(MG):
                        g = i * MG + place
                        b = place % 2
                        early = first and place == 0
                        t, before = tile_at(i, place), tile_before(i, place)
                        _, at = nc.values_load_multi_w_load_instructions(
                            start_row[0:1, 0, bass.ds(g * CH, CH)], engines=(ENG.DVE,), min_val=0, max_val=WIN - LOC,
                            skip_runtime_bounds_check_because="the offsets are clamped, and the flag is clear")
                        for n in range(CH):
                            c = (n + 2) % CH
                            if n < CH - 2:
                                build(g, b, c, early and c < SR)
                            elif not (last and place == MG - 1):
                                build(g + 1, 1 - b, c, False)
                            if before is not None:
                                tile_dve_late(dve, before, n)
                            if t is not None:
                                tile_dve_early(dve, t, n)
                            add(g, b, n, (place * CH + n) % CR, at[n], early)

                several(dve, PREPS, turn)
                for n in range(CH):
                    tile_dve_late(dve, TILES - LAG, n)
                for t in range(TILES - LAG + 1, TILES):
                    tile_dve_all(dve, t)
            with dve.Else():
                general_dve(dve)
            dve.wait_ge(tok_ps, TILES)
            nc.vector.tensor_copy(tok[:, :, :], p_tok[:, :, :]).then_inc(tok_ok, 1)
            dve.wait_ge(tok_ok, 1)
            dve.wait_ge(sum_ok, TILES + 1)

        @block.tensor
        def _(pe):
            pe.wait_ge(w_in, 16 * (DH + H + 3))
            for h in range(DH):
                if h:
                    pe.wait_ge(wx_ok, 2 * h)
                for n in range(H):
                    e = nc.tensor.transpose(p_tok[0:C, n // 2, (n % 2) * P:(n % 2 + 1) * P], wx[:, h, n * C:(n + 1) * C], ident[:, :])
                e.then_inc(wx_ps, 1)
                pe.wait_ge(wx_ok, 2 * h + 1)
                for n in range(H):
                    e = nc.tensor.matmul(p_lg[:, n * G:(n + 1) * G], wxT[:, n, :], ws[:, :], start=True, stop=True)
                e.then_inc(wx_ps, 1)
            for n in range(H):
                nc.tensor.matmul(p_x[0:1, n * G:(n + 1) * G], bxT[:, n:n + 1], ws[:, :], start=True, stop=False)
                e = nc.tensor.matmul(p_x[0:1, n * G:(n + 1) * G], ones[0:1, 0:1], bsl[:, :], start=False, stop=True)
            e.then_inc(wx_ps, 1)
            pe.wait_ge(wx_ok, 2 * DH + 1)
            nc.tensor.matmul(p_x[:, :], ones[0:1, :], brow[:, :], start=True, stop=True).then_inc(wx_ps, 1)
            pe.wait_ge(wx_ok, 2 * DH + 2)
            pe.wait_ge(consts, 3)
            general = pe.value_load(flag[0:1, 0:1], min_val=0, max_val=1)
            with pe.If(general == 0):
                FIRST, SPAN = 2, 9

                def messages(g, b, c, early):
                    if c == FIRST:
                        pe.wait_ge(added, (g + 1) * CH)
                        if not early:
                            pe.wait_ge(res_ok, g - 1)
                    k = c - FIRST
                    for n in range(k * DH * R // SPAN, (k + 1) * DH * R // SPAN):
                        e = nc.tensor.matmul(p_acc[:, b, 0:D], acc[:, b, n, :], w_sb[:, n // R, n % R, :],
                                             start=(n == 0), stop=(n == DH * R - 1))
                    if k == SPAN - 1:
                        e.then_inc(msg_ok, 1)

                def turn(i, first, last):
                    for place in range(MG):
                        g = i * MG + place
                        b = place % 2
                        early = first and place < 2
                        t, before = tile_at(i, place), tile_before(i, place)
                        for c in range(CH):
                            q = g * CH + c
                            pe.wait_ge(built, q + 1)
                            pe.wait_ge(gathered[b][c], (i * MG + place - b) * 8 + 16)
                            if not (early and b == 0 and c < CR):
                                pe.wait_ge(added, q - CR + 1)
                            if c == 0 and not early:
                                pe.wait_ge(res_ok, g - 1)
                            for h in range(DH):
                                nc.tensor.matmul(p_chunk[:, (place * CH + c) % CR, h * P:(h + 1) * P], rows[:, b, c, h * P:(h + 1) * P],
                                                 spot[:, c % SR, :], start=True, stop=True)
                            nc.tensor.matmul(p_acc[:, b, D:MW], hits[:, c % SR, :], ones_bf[:, :],
                                             start=(c == 0), stop=(c == CH - 1)).then_inc(summed, 1)
                            if FIRST <= c < FIRST + SPAN and not (early and b == 0):
                                messages(g - 1, 1 - b, c, first and place <= 2)
                            if c == 6 and before is not None:
                                tokens(pe, before)
                            if c == 11 and t is not None:
                                turn_tile(pe, t)
                            if c == 13 and t is not None:
                                logits(pe, t)

                several(pe, PREPS, turn)
                for c in range(FIRST, FIRST + SPAN):
                    messages(GROUPS - 1, 1, c, False)
                tokens(pe, TILES - LAG)
                for t in range(TILES - LAG + 1, TILES):
                    tile_pe_all(pe, t)
            with pe.Else():
                general_pe(pe)


def token_stage(nc, scope, sb, ps, sem, w_fx, b_fx, w_q, w_k, w_v, w_out, ident, tok, tok_sum, mix):
    wfx = sb(scope, "t_wfx", [P, DH, HG])
    bfx = sb(scope, "t_bfx", [1, HG])
    wqkv = sb(scope, "t_wqkv", [C, 3, C])
    wo = sb(scope, "t_wo", [C, H, D])
    den = sb(scope, "t_den", [P, 2, 4])
    tn = sb(scope, "t_tn", [P, 4, D + 1])
    tT = sb(scope, "t_tT", [P, DH, HG])
    nrow = sb(scope, "t_nrow", [1, HG])
    tokT = sb(scope, "t_tokT", [C, HG])
    qkv = sb(scope, "t_qkv", [C, 3, HG])
    sc = sb(scope, "t_sc", [G, H, G])
    sm = sb(scope, "t_sm", [G, 3, H])
    aT = sb(scope, "t_aT", [G, H, G])
    vw = sb(scope, "t_vw", [G, H, D])
    p_a = ps(scope, "tp_a", [P, 2, 512])
    p_b = ps(scope, "tp_b", [P, 512])
    p_c = ps(scope, "tp_c", [P, 512])
    p_vw = ps(scope, "tp_vw", [P, 4, 512])
    w_in = sem("t_w_in")
    mm = sem("t_products")
    el = sem("t_elementwise")
    exped = sem("t_exped")

    def per_head(a):
        return a.rearrange("p (h a) -> p h a", a=1).to_broadcast((G, H, G))

    with nc.Block() as block:
        @block.sync
        def _(sp):
            for h in range(DH):
                sp.dma_start(wfx[:, h, :], w_fx[h * P:(h + 1) * P, :]).then_inc(w_in, 16)
            sp.dma_start(bfx[:, :], b_fx.rearrange("(a n) -> a n", a=1)).then_inc(w_in, 16)
            for n, w in enumerate((w_q, w_k, w_v)):
                sp.dma_start(wqkv[:, n, :], w).then_inc(w_in, 16)
            sp.dma_start(wo[:, :, :], w_out.rearrange("(h c) d -> c h d", c=C)).then_inc(w_in, 16)

        @block.vector
        def _(dve):
            nc.vector.tensor_scalar(den[:, 0, :], tok_sum[:, :], 1e-5, None, ALU.add).then_inc(el, 1)
            dve.wait_ge(el, 1)
            nc.vector.reciprocal(den[:, 1, :], den[:, 0, :]).then_inc(el, 1)
            dve.wait_ge(el, 2)
            nc.vector.tensor_tensor(tn[:, :, 0:D], tok[:, :, :], den[:, 1, :].rearrange("p (j a) -> p j a", a=1).to_broadcast((P, 4, D)),
                                    ALU.mult)
            nc.vector.tensor_tensor(tn[:, :, D], tok_sum[:, :], den[:, 1, :], ALU.mult).then_inc(el, 1)
            dve.wait_ge(mm, 1)
            nc.vector.tensor_copy(tT[:, :, :], p_a[:, :, :])
            nc.vector.tensor_copy(nrow[:, :], p_b[0:1, :]).then_inc(el, 1)
            dve.wait_ge(mm, 2)
            nc.vector.tensor_copy(tokT[:, :], p_c[0:C, :]).then_inc(el, 1)
            dve.wait_ge(mm, 3)
            nc.vector.tensor_copy(qkv[:, 0:2, :], p_a[0:C, :, :])
            nc.vector.tensor_copy(qkv[:, 2, :], p_b[0:C, :]).then_inc(el, 1)
            dve.wait_ge(mm, 4)
            nc.vector.tensor_scalar(sc[:, :, :], p_c[0:G, :].rearrange("p (h k) -> p h k", h=H), C ** -0.5, None, ALU.mult).then_inc(el, 1)
            dve.wait_ge(el, 7)
            nc.vector.reduce_max(sm[:, 0, :], sc[:, :, :], AX_X).then_inc(el, 1)
            dve.wait_ge(el, 8)
            nc.vector.tensor_tensor(sc[:, :, :], sc[:, :, :], per_head(sm[:, 0, :]), ALU.subtract).then_inc(el, 1)
            dve.wait_ge(exped, 1)
            nc.vector.reduce_sum(sm[:, 1, :], sc[:, :, :], AX_X).then_inc(el, 1)
            dve.wait_ge(el, 10)
            nc.vector.reciprocal(sm[:, 2, :], sm[:, 1, :]).then_inc(el, 1)
            dve.wait_ge(el, 11)
            nc.vector.tensor_tensor(sc[:, :, :], sc[:, :, :], per_head(sm[:, 2, :]), ALU.mult).then_inc(el, 1)
            dve.wait_ge(mm, 5)
            nc.vector.tensor_copy(vw[:, :, :], p_vw[0:G, :, :].rearrange("p a (b d) -> p (a b) d", d=D)).then_inc(el, 1)
            dve.wait_ge(mm, 6)
            nc.vector.tensor_copy(aT[:, :, :], p_a[0:G, 0, :].rearrange("p (h g) -> p h g", h=H)).then_inc(el, 1)
            dve.wait_ge(mm, 7)
            nc.vector.tensor_copy(mix[:, :, :], p_vw[:, 0:2, :].rearrange("p a (b d) -> p (a b) d", d=D)).then_inc(el, 1)
            dve.wait_ge(el, 15)

        @block.scalar
        def _(act):
            act.wait_ge(el, 9)
            nc.scalar.activation(sc[:, :, :], sc[:, :, :], ACT.Exp).then_inc(exped, 1)

        @block.tensor
        def _(pe):
            pe.wait_ge(el, 3)
            for j in range(4):
                for h in range(DH):
                    nc.tensor.transpose(p_a[:, h, j * P:(j + 1) * P], tn[:, j, h * P:(h + 1) * P], ident[:, :])
                m = nc.tensor.matmul(p_b[0:1, j * P:(j + 1) * P], tn[:, j, D:D + 1], ident[:, :], start=True, stop=True)
            m.then_inc(mm, 1)
            pe.wait_ge(w_in, 16 * (DH + 5))
            pe.wait_ge(el, 4)
            for n in range(H):
                own = slice(n * C, (n + 1) * C)
                for h in range(DH):
                    nc.tensor.matmul(p_c[0:C, own], wfx[:, h, own], tT[:, h, own], start=(h == 0), stop=False)
                m = nc.tensor.matmul(p_c[0:C, own], bfx[:, own], nrow[:, own], start=False, stop=True)
            m.then_inc(mm, 1)
            pe.wait_ge(el, 5)
            for n in range(3):
                m = nc.tensor.matmul(p_a[0:C, n, :] if n < 2 else p_b[0:C, :], wqkv[:, n, :], tokT[:, :], start=True, stop=True)
            m.then_inc(mm, 1)
            pe.wait_ge(el, 6)
            for n in range(H):
                own = slice(n * C, (n + 1) * C)
                m = nc.tensor.matmul(p_c[0:G, own], qkv[:, 0, own], qkv[:, 1, own], start=True, stop=True)
            m.then_inc(mm, 1)
            for n in range(H):
                m = nc.tensor.matmul(p_vw[0:G, n // 2, (n % 2) * D:(n % 2 + 1) * D], qkv[:, 2, n * C:(n + 1) * C], wo[:, n, :], start=True, stop=True)
            m.then_inc(mm, 1)
            pe.wait_ge(el, 12)
            for n in range(H):
                m = nc.tensor.transpose(p_a[0:G, 0, n * G:(n + 1) * G], sc[:, n, :], ident[0:G, 0:G])
            m.then_inc(mm, 1)
            pe.wait_ge(el, 14)
            for n in range(H):
                m = nc.tensor.matmul(p_vw[(n % 2) * G:(n % 2 + 1) * G, n // 4, (n // 2 % 2) * D:(n // 2 % 2 + 1) * D], aT[:, n, :], vw[:, n, :],
                                     start=True, stop=True)
            m.then_inc(mm, 1)


def output_pass(nc, scope, sb, ps, sem, b_out, x1, slices, out, ident, mix):
    U = 7
    sl = sb(scope, "o_sl", [P, U, HG])
    sT = sb(scope, "o_sT", [P, U, 4, P])
    ot = sb(scope, "o_ot", [P, U, D])
    xt = sb(scope, "o_xt", [P, U, D])
    xb = sb(scope, "o_xb", [P, U, D])
    bo = sb(scope, "o_bo", [P, D])
    p_T = ps(scope, "op_T", [P, 3, 512])
    p_o = ps(scope, "op_o", [P, 3, 512])
    sl_in = [sem(f"o_sl_in{k}") for k in range(U)]
    bo_in = sem("o_bo_in")
    xt_in = [sem(f"o_xt_in{k}") for k in range(U)]
    xb_ok = sem("o_xb_ok")
    turned = sem("o_turned")
    sT_ok = sem("o_sT_ok")
    o_ps = sem("o_ps")
    ot_ok = sem("o_ot_ok")
    out_out = [sem(f"o_out{k}") for k in range(U)]

    with nc.Block() as block:
        @block.sync
        def _(sp):
            sp.dma_start(bo[:, :], b_out.rearrange("(a n) -> a n", a=1).to_broadcast((P, D))).then_inc(bo_in, 16)
            for k in range(U):
                sp.dma_start(sl[:, k, :], slices[k * P:(k + 1) * P, :]).then_inc(sl_in[k], 16)
                sp.dma_start(xt[:, k, :], x1[k * P:(k + 1) * P, :]).then_inc(xt_in[k], 16)

            def turn(i, first, last):
                for k in range(U):
                    t = i * U + k
                    if not last:
                        sp.wait_ge(turned, t + 1)
                        sp.dma_start(sl[:, k, :], slices[bass.ds((t + U) * P, P), :]).then_inc(sl_in[k], 16)
                        sp.wait_ge(xb_ok, t + 1)
                        sp.dma_start(xt[:, k, :], x1[bass.ds((t + U) * P, P), :]).then_inc(xt_in[k], 16)
                    sp.wait_ge(ot_ok, t + 1)
                    sp.dma_start(out[bass.ds(t * P, P), :], ot[:, k, :]).then_inc(out_out[k], 16)

            several(sp, TILES // U, turn)
            for k in range(U):
                sp.wait_ge(out_out[k], 16 * (TILES // U))

        @block.gpsimd
        def _(pool):
            pool.wait_ge(bo_in, 16)

            def turn(i, first, last):
                for k in range(U):
                    t = i * U + k
                    if not first:
                        pool.wait_ge(ot_ok, t - U + 1)
                    pool.wait_ge(xt_in[k], i * 16 + 16)
                    nc.gpsimd.tensor_tensor(xb[:, k, :], xt[:, k, :], bo[:, :], ALU.add).then_inc(xb_ok, 1)

            several(pool, TILES // U, turn)

        @block.tensor
        def _(pe):
            def turn_slices(i, k, first):
                t = i * U + k
                pe.wait_ge(sl_in[k], i * 16 + 16)
                if not (first and k < 3):
                    pe.wait_ge(sT_ok, reused(i, k, 3, U))
                for j in range(4):
                    m = nc.tensor.transpose(p_T[:, k % 3, j * P:(j + 1) * P], sl[:, k, j * P:(j + 1) * P], ident[:, :])
                m.then_inc(turned, 1)

            def blend(i, k, first):
                t = i * U + k
                pe.wait_ge(sT_ok, t + 1)
                if not (first and k < 3):
                    pe.wait_ge(ot_ok, reused(i, k, 3, U))
                for j in range(4):
                    m = nc.tensor.matmul(p_o[:, k % 3, 0:D], sT[:, k, j, :], mix[:, j, :], start=(j == 0), stop=(j == 3))
                m.then_inc(o_ps, 1)

            def turn(i, first, last):
                for k in range(U):
                    turn_slices(i, k, first)
                    if k:
                        blend(i, k - 1, first)
                blend(i, U - 1, first)

            several(pe, TILES // U, turn)

        @block.scalar
        def _(act):
            def turn(i, first, last):
                for k in range(U):
                    t = i * U + k
                    act.wait_ge(turned, t + 1)
                    if not first:
                        act.wait_ge(o_ps, t - U + 1)
                    nc.scalar.activation(sT[:, k, :, :], p_T[:, k % 3, :].rearrange("p (j n) -> p j n", j=4), ACT.Copy).then_inc(sT_ok, 1)

            several(act, TILES // U, turn)

        @block.vector
        def _(dve):
            def turn(i, first, last):
                for k in range(U):
                    t = i * U + k
                    if not first:
                        dve.wait_ge(out_out[k], i * 16)
                    dve.wait_ge(o_ps, t + 1)
                    dve.wait_ge(xb_ok, t + 1)
                    nc.vector.tensor_tensor(ot[:, k, :], p_o[:, k % 3, 0:D], xb[:, k, :], ALU.add).then_inc(ot_ok, 1)

            several(dve, TILES // U, turn)


def kernel(x, src, dst, edge_type_8, L0_gnn_weight, L0_gnn_sl_w, L0_gnn_sl_b, L0_ffn_W_fx, L0_ffn_b_fx,
           L0_ffn_W_x, L0_ffn_b_x, L0_ffn_W_slice, L0_ffn_b_slice, L0_ffn_W_q, L0_ffn_W_k, L0_ffn_W_v,
           L0_ffn_W_out, L0_ffn_b_out, L0_ffn_temperature):
    import concourse.bacc as bacc
    from concourse.bass_utils import run_bass_kernel_spmd

    def filled(a, rows, value):
        a = np.ascontiguousarray(a)
        full = np.full((rows,) + a.shape[1:], value, a.dtype)
        full[:a.shape[0]] = a
        return full

    arrays = {
        "x": filled(x, NP, 0),
        "src": filled(src, EP + P, 0),
        "dst": filled(dst, EP + P, NP),
        "typ": filled(edge_type_8, EP + P, PAD_TYPE),
        "w_rel": L0_gnn_weight, "sl_w": L0_gnn_sl_w, "sl_b": L0_gnn_sl_b,
        "w_fx": L0_ffn_W_fx, "b_fx": L0_ffn_b_fx, "w_x": L0_ffn_W_x, "b_x": L0_ffn_b_x,
        "w_slice": L0_ffn_W_slice, "b_slice": L0_ffn_b_slice, "w_q": L0_ffn_W_q, "w_k": L0_ffn_W_k,
        "w_v": L0_ffn_W_v, "w_out": L0_ffn_W_out, "b_out": L0_ffn_b_out, "temp": L0_ffn_temperature,
    }
    nc = bacc.Bacc("TRN2", target_bir_lowering=False, num_devices=1)
    feed, aps = {}, {}
    for name, a in arrays.items():
        a = np.ascontiguousarray(a)
        feed[f"in_{name}"] = a
        aps[name] = nc.dram_tensor(f"in_{name}", a.shape, mybir.dt.from_np(a.dtype), kind="ExternalInput").ap()
    aps["out"] = nc.dram_tensor("out_0", (NP, D), F32, kind="ExternalOutput").ap()
    program(nc, **aps)
    r = run_bass_kernel_spmd(nc, [feed], core_ids=[0])
    return r.results[0]["out_0"][:N]
```

```python
from contextlib import ExitStack

import numpy as np
import concourse.bass as bass
from concourse import mybir

ALU = mybir.AluOpType
ACT = mybir.ActivationFunctionType
AX_X = mybir.AxisListType.X
F32 = mybir.dt.float32
BF16 = mybir.dt.bfloat16
I32 = mybir.dt.int32
U32 = mybir.dt.uint32
ENG = mybir.EngineType

P = 128
N, D, R, E = 12500, 256, 8, 212500
DH = D // P
EPS = 1e-5

TILES = -(-N // P)
NP = TILES * P
CH = 15
WIN = P
LOC = P // R
GROUP = CH * P
MG = 8
MC = MG * CH
GROUPS = -(-E // (GROUP * MG)) * MG
CHUNKS = GROUPS * CH
PREPS = GROUPS // MG
EP = GROUPS * GROUP
TPB = TILES // PREPS
LAG = 5
assert PREPS % 2 == 0 and TPB * PREPS == TILES and MG % 2 == 0 and MG == TPB + 1 and MC % 2 == 0
PAD_TYPE = 64
WORK_GROUPS = -(-E // GROUP)
MG_LAST = WORK_GROUPS - (PREPS - 1) * MG
assert 1 < MG_LAST <= MG
TAIL = [(PREPS - 1, place) for place in range(MG_LAST, MG)] + [(PREPS, place) for place in range(LAG + 1)]
MROWS = NP + 2 * P
TRASH = NP + P
MW = D + 1
MP = 261

LATE_PARTS, LATE = 8, DH * R * WIN
ZERO = (MROWS * MP // P - LATE_PARTS * LATE) // PREPS
assert (ZERO * PREPS + LATE_PARTS * LATE) * P == MROWS * MP

H, C, G = 8, 64, 64
HG = H * G


def heads(a):
    return a.rearrange("p (h g) -> p h g", h=H)


def per_head(a):
    return a.rearrange("p (h a) -> p h a", a=1).to_broadcast((P, H, G))


def several(eng, n, body):
    body(0, True, False)
    with eng.Fori(1, n - 1) as i:
        body(i, False, False)
    body(n - 1, False, True)


def reused(turn, k, ring, per):
    if k >= ring:
        return turn * per + k - ring + 1
    return (turn - 1) * per + k + ring * ((per - 1 - k) // ring) + 1


def program(nc, x, src, dst, typ, w_rel, sl_w, sl_b, w_fx, b_fx, w_x, b_x, w_slice, b_slice,
            w_q, w_k, w_v, w_out, b_out, temp, out):
    table = nc.dram_tensor("table", (NP, D), F32, kind="Internal").ap()
    base = nc.dram_tensor("base", (NP, D), F32, kind="Internal").ap()
    sums = nc.dram_tensor("sums", (MROWS, MP), F32, kind="Internal").ap()
    starts = nc.dram_tensor("starts", (2, CHUNKS), I32, kind="Internal").ap()
    mid = nc.dram_tensor("mid", (NP, HG + D), F32, kind="Internal").ap()

    with ExitStack() as whole:
        def sb(scope, name, shape, dt=F32):
            return scope.enter_context(nc.sbuf_tensor(name, shape, dt))

        def ps(scope, name, shape, dt=F32):
            return scope.enter_context(nc.psum_tensor(name, shape, dt))

        live = []

        def sem(name):
            live.append(nc.alloc_semaphore(name=name))
            return live[-1]

        def release():
            nc.clear_and_free_semaphores(live)
            live.clear()
            nc.all_engine_barrier()

        passed = nc.alloc_semaphore(name="passed")

        ident = sb(whole, "ident", [P, P])
        ones = sb(whole, "ones", [P, P])
        tok = sb(whole, "tok", [P, 4, D])
        tok_sum = sb(whole, "tok_sum", [P, 4])
        mix = sb(whole, "mix", [P, 4, D])
        with ExitStack() as graph:
            meta = sb(graph, "meta", [P, 5, CHUNKS])
            w_sb = sb(graph, "w_sb", [P, DH, R, D])
            start_row = sb(graph, "start_row", [1, 2, CHUNKS], I32)
            flag = sb(graph, "flag", [1, 1], I32)
            bfull = sb(graph, "bfull", [P, HG])
            wxs = sb(graph, "wxs", [P, DH, HG])
            with ExitStack() as scope:
                prepare(nc, scope, sb, ps, sem, passed, x, src, dst, typ, w_rel, sl_w, sl_b, w_x, b_x, w_slice,
                        b_slice, temp, table, base, sums, starts, ident, ones, meta, w_sb, start_row, flag,
                        bfull, wxs)
            release()
            with ExitStack() as scope:
                main_pass(nc, scope, sb, ps, sem, passed, table, base, sums, mid, ident, ones, meta, w_sb,
                          start_row, flag, bfull, wxs, tok, tok_sum)
            release()
        with ExitStack() as scope:
            token_stage(nc, scope, sb, ps, sem, w_fx, b_fx, w_q, w_k, w_v, w_out, ident, tok, tok_sum, mix)
        with ExitStack() as scope:
            output_pass(nc, scope, sb, ps, sem, b_out, mid, out, ident, mix)


def prepare(nc, scope, sb, ps, sem, passed, x, src, dst, typ, w_rel, sl_w, sl_b, w_x, b_x, w_slice, b_slice,
            temp, table, base, sums, starts, ident, ones, meta, w_sb, start_row, flag, bfull, wxs):
    x_t = sb(scope, "p_x", [P, 2, TPB, D])
    hn = sb(scope, "p_hn", [P, TPB, D])
    xb = sb(scope, "p_xb", [P, TPB, D])
    own = sb(scope, "p_own", [P, 2, TPB, D])
    hT = sb(scope, "p_hT", [P, 2, DH, P])
    stats = sb(scope, "p_stats", [P, TPB, 6])
    mv = sb(scope, "p_mv", [P, TPB, 2])
    var = sb(scope, "p_var", [P, TPB])
    std = sb(scope, "p_std", [P, TPB])
    rstd = sb(scope, "p_rstd", [P, TPB])
    slw = sb(scope, "p_slw", [P, DH, D])
    slT = sb(scope, "p_slT", [P, DH, D])
    slb = sb(scope, "p_slb", [P, D])
    zero = sb(scope, "p_zero", [P, ZERO])
    raw = sb(scope, "p_raw", [MC, 4, P], I32)
    rows = sb(scope, "p_rows", [MC, 4, P])
    key = sb(scope, "p_key", [MC, 2, P])
    junk = sb(scope, "p_junk", [MC, P])
    ow = sb(scope, "p_ow", [MC, 4])
    oi = sb(scope, "p_oi", [MC, 2], I32)
    over = sb(scope, "p_over", [MC, 4])
    bad = sb(scope, "p_bad", [MC, 4])
    bad_sum = sb(scope, "p_bad_sum", [MC, 4])
    due = sb(scope, "p_due", [MC, 1])
    bad_row = sb(scope, "p_bad_row", [MC, 1])
    first_of = sb(scope, "p_first_of", [MC, MG, CH])
    wx = sb(scope, "s_wx", [P, DH, HG])
    wxT = sb(scope, "s_wxT", [C, H, P])
    ws = sb(scope, "s_ws", [C, G])
    bxT = sb(scope, "s_bxT", [C, H])
    bsl = sb(scope, "s_bsl", [1, G])
    tmp = sb(scope, "s_tmp", [P, H])
    rtmp = sb(scope, "s_rtmp", [P, H])
    p_hT = ps(scope, "pp_hT", [P, 2, 512])
    p_own = ps(scope, "pp_own", [P, 2, 512])
    p_cols = ps(scope, "pp_cols", [P, 2, 512])
    p_small = ps(scope, "pp_small", [P, 512])

    const_ok = sem("const_ok")
    masks_ok = sem("masks_ok")
    weights_in = sem("weights_in")
    sl_turned = sem("sl_turned")
    sl_ready = sem("sl_ready")
    zero_ok = sem("zero_ok")
    due_ok = sem("due_ok")
    zero_out = sem("zero_out")
    x_in = [[sem(f"x_in{b}_{n}") for n in range(2)] for b in range(2)]
    rel_in = sem("rel_in")
    stats_ok = sem("stats_ok")
    mv_ok = sem("mv_ok")
    var_ok = sem("var_ok")
    std_ok = sem("std_ok")
    rstd_ok = sem("rstd_ok")
    hn_ok = sem("hn_ok")
    xb_ok = sem("xb_ok")
    hT_ps = sem("hT_ps")
    hT_ok = sem("hT_ok")
    own_ps = sem("own_ps")
    own_copied = sem("own_copied")
    own_ok = sem("own_ok")
    table_out = [sem(f"table_out{n}") for n in range(2)]
    base_out = [[sem(f"base_out{b}_{n}") for n in range(2)] for b in range(2)]
    raw_in = sem("raw_in")
    rows_ok = sem("rows_ok")
    base_ps = sem("base_ps")
    base_ok = sem("base_ok")
    w_ok = sem("w_ok")
    off_ok = sem("off_ok")
    key_half = sem("key_half")
    planes_ok = sem("planes_ok")
    bad_ok = sem("bad_ok")
    bad_added = sem("bad_added")
    cols_ps = sem("cols_ps")
    cols_ok = sem("cols_ok")
    starts_out = sem("starts_out")
    row_in = sem("row_in")
    bad_rowed = sem("bad_rowed")
    bad_ps = sem("bad_ps")
    flag_ok = sem("flag_ok")
    w_in = sem("w_in")
    tmp_ok = sem("tmp_ok")
    wx_ps = sem("wx_ps")
    wx_ok = sem("wx_ok")

    def edges(a, turn, shift=0):
        return a[bass.ds(turn * (MC * P) + shift, MC * P)].rearrange("(c p) -> c p", p=P)

    PARTS = ((0, 4), (4, TPB))

    def pairs(body):
        def pair(j, first, last):
            body(2 * j, first, False, j, 0, last)
            body(2 * j + 1, False, last, j, 1, last)
        return pair

    def part_of(k):
        return 0 if k < PARTS[0][1] else 1

    def tiles(a, turn, n):
        k0, k1 = PARTS[n]
        return a[bass.ds(turn * (TPB * P) + k0 * P, (k1 - k0) * P), :].rearrange("(k p) d -> p k d", p=P)

    with nc.Block() as block:
        @block.sync
        def _(sp):
            def load_x(turn, b, n):
                k0, k1 = PARTS[n]
                sp.dma_start(x_t[:, b, k0:k1, :], tiles(x, turn, n)).then_inc(x_in[b][n], 16)

            def load_edges(turn):
                for n, (a, shift) in enumerate(((dst, 0), (typ, 0), (src, 0), (dst, 1))):
                    sp.dma_start(raw[:, n, :], edges(a, turn, shift)).then_inc(raw_in, 16)

            def store_base(turn, b, n):
                k0, k1 = PARTS[n]
                sp.wait_ge(own_ok, turn * TPB + k1)
                sp.dma_start(tiles(base, turn, n), own[:, b, k0:k1, :]).then_inc(base_out[b][n], 16)

            load_x(0, 0, 0)
            load_edges(0)
            load_x(0, 0, 1)
            for h in range(DH):
                sp.dma_start(slw[:, h, :], sl_w[h * P:(h + 1) * P, :]).then_inc(weights_in, 16)
            sp.dma_start(slb[:, :], sl_b.rearrange("(a n) -> a n", a=1).to_broadcast((P, D))).then_inc(weights_in, 16)
            for n in range(2):
                load_x(1, 1, n)
            for h in range(DH):
                sp.dma_start(w_sb[:, h, :, :], w_rel[:, h * P:(h + 1) * P, :].rearrange("r p n -> p r n")).then_inc(rel_in, 16)
            for h in range(DH):
                sp.dma_start(wx[:, h, :], w_x[h * P:(h + 1) * P, :]).then_inc(w_in, 16)
            sp.dma_start(ws[:, :], w_slice).then_inc(w_in, 16)
            for h in range(H):
                sp.dma_start(bxT[:, h:h + 1], b_x[h * C:(h + 1) * C].rearrange("(c a) -> c a", a=1)).then_inc(w_in, 16)
            sp.dma_start(bsl[:, :], b_slice.rearrange("(a n) -> a n", a=1)).then_inc(w_in, 16)
            sp.dma_start(tmp[:, :], temp.rearrange("a h b c -> (a b c) h").to_broadcast((P, H))).then_inc(w_in, 16)
            flat = sums.rearrange("(p a) w -> p (a w)", p=P)
            sp.wait_ge(zero_ok, 1)

            def turn(i, first, last, j, b, final):
                sp.wait_ge(rows_ok, i + 1)
                if not last:
                    load_edges(i + 1)
                sp.wait_ge(off_ok, i * 2 + 2)
                for n in range(2):
                    sp.dma_start(starts[n, bass.ds(i * MC, MC)].rearrange("(c a) -> c a", a=1), oi[:, n:n + 1]).then_inc(starts_out, 16)
                for n, (k0, k1) in enumerate(PARTS):
                    sp.wait_ge(hn_ok, i * TPB + k1)
                    if not final:
                        sp.wait_ge(xb_ok, i * TPB + k1)
                        load_x(i + 2, b, n)
                    sp.dma_start(tiles(table, i, n), hn[:, k0:k1, :]).then_inc(table_out[n], 16)
                    if not first:
                        store_base(i - 1, 1 - b, n)
                sp.dma_start(flat[:, bass.ds(i * ZERO, ZERO)], zero[:, :]).then_inc(zero_out, 16)

            several(sp, PREPS // 2, pairs(turn))
            for n in range(2):
                store_base(PREPS - 1, 1, n)
            sp.wait_ge(starts_out, 32 * PREPS)
            sp.dma_start(start_row[0:1, :, :], starts.rearrange("(o a) c -> o a c", o=1)).then_inc(row_in, 16)
            sp.wait_ge(row_in, 16)
            sp.wait_ge(rel_in, 16 * DH)
            sp.wait_ge(zero_out, 16 * PREPS)
            for n in range(2):
                sp.wait_ge(table_out[n], 16 * PREPS)
                for b in range(2):
                    sp.wait_ge(base_out[b][n], 16 * (PREPS // 2))

        @block.gpsimd
        def _(pool):
            nc.gpsimd.memset(ident[:, :], 0.0)
            nc.gpsimd.memset(first_of[:, :, :], 0.0)
            nc.gpsimd.memset(ones[:, :], 1.0).then_inc(const_ok, 1)
            pool.wait_ge(const_ok, 1)
            nc.gpsimd.affine_select(out=ident[:, :], in_=ident[:, :], compare_op=ALU.not_equal, fill=1.0,
                                    base=0, pattern=[[-1, P]], channel_multiplier=1).then_inc(masks_ok, 1)
            nc.gpsimd.affine_select(out=first_of[:, :, :], in_=first_of[:, :, :], compare_op=ALU.not_equal, fill=1.0,
                                    base=0, pattern=[[-CH, MG], [0, CH]], channel_multiplier=1).then_inc(masks_ok, 1)
            nc.gpsimd.memset(due[:, :], float(-NP)).then_inc(due_ok, 1)
            for n in range(MG):
                for k in range(TPB):
                    turns, g = divmod(k + LAG - 2, MG)
                    if g == n:
                        pool.wait_ge(due_ok, n + 1 - (n > (LAG - 3) % MG))
                        nc.gpsimd.affine_select(out=due[:, :], in_=due[:, :], compare_op=ALU.not_equal,
                                                fill=float(P * (k + 1) - turns * TPB * P), base=-n * CH,
                                                pattern=[[0, 1]], channel_multiplier=1).then_inc(due_ok, 1)
            nc.gpsimd.memset(zero[:, :], 0.0).then_inc(zero_ok, 1)
            pool.wait_ge(weights_in, 16 * (DH + 1))

            def add_x(i, b, k):
                pool.wait_ge(own_copied, i * TPB + k + 1)
                pool.wait_ge(xb_ok, i * TPB + k + 1)
                nc.gpsimd.tensor_tensor(own[:, b, k, :], own[:, b, k, :], xb[:, k, :], ALU.add).then_inc(own_ok, 1)

            def turn(i, first, last, j, b, final):
                for k in range(TPB):
                    if not first:
                        add_x(i - 1, 1 - b, k)
                        pool.wait_ge(own_ok, (i - 1) * TPB + k + 1)
                    pool.wait_ge(x_in[b][part_of(k)], j * 16 + 16)
                    nc.gpsimd.tensor_tensor(xb[:, k, :], x_t[:, b, k, :], slb[:, :], ALU.add).then_inc(xb_ok, 1)

            several(pool, PREPS // 2, pairs(turn))
            for k in range(TPB):
                add_x(PREPS - 1, 1, k)

        @block.vector
        def _(dve):
            nc.vector.memset(bad_sum[:, :], 0.0).then_inc(bad_added, 1)
            dve.wait_ge(due_ok, TPB + 1)
            for h in range(DH):
                dve.wait_ge(sl_turned, h + 1)
                nc.vector.tensor_copy(slT[:, h, :], p_own[:, h, 0:D]).then_inc(sl_ready, 1)

            def convert(i, first):
                dve.wait_ge(raw_in, i * 64 + 64)
                if not first:
                    dve.wait_ge(cols_ps, i)
                    dve.wait_ge(planes_ok, i * 2)
                nc.vector.tensor_copy(rows[:, :, :], raw[:, :, :]).then_inc(rows_ok, 1)

            def order(i, first):
                dve.wait_ge(rows_ok, i + 1)
                if not first:
                    dve.wait_ge(bad_added, i + 1)
                dve.sem_inc(passed, 1)
                nc.vector.tensor_tensor_reduce(junk[:, :], rows[:, 0, :], rows[:, 3, :], 1.0, 0.0, ALU.subtract,
                                               ALU.max, over[:, 0:1]).then_inc(bad_ok, 1)

            def window(i, first):
                dve.wait_ge(base_ps, i + 1)
                if not first:
                    dve.wait_ge(off_ok, i * 2)
                nc.vector.tensor_copy(ow[:, 1:2], p_small[0:MC, 0:1]).then_inc(base_ok, 1)
                dve.wait_ge(base_ok, i + 1)
                nc.vector.tensor_scalar(ow[:, 2:3], ow[:, 1:2], float(WIN - LOC), rows[:, 0, 0:1], ALU.add, ALU.min).then_inc(w_ok, 1)

            def half_key(i):
                nc.vector.scalar_tensor_tensor(out=key[:, 0, :], in0=rows[:, 1, :], scalar=float(LOC), in1=rows[:, 0, :],
                                               op0=ALU.mult, op1=ALU.add).then_inc(key_half, 1)
                nc.vector.tensor_scalar(key[:, 1, :], rows[:, 0, :], ow[:, 1:2], None, ALU.subtract).then_inc(planes_ok, 1)

            def offsets(i, first):
                dve.wait_ge(w_ok, i + 1)
                nc.vector.tensor_scalar(ow[:, 0:1], ow[:, 2:3], ow[:, 1:2], None, ALU.subtract).then_inc(off_ok, 1)
                dve.wait_ge(off_ok, i * 2 + 1)
                if not first:
                    dve.wait_ge(starts_out, i * 32)
                nc.vector.tensor_copy(oi[:, :], ow[:, 0:2]).then_inc(off_ok, 1)

            def full_key(i):
                dve.wait_ge(key_half, i + 1)
                nc.vector.tensor_scalar(key[:, 0, :], key[:, 0, :], ow[:, 2:3], None, ALU.subtract).then_inc(planes_ok, 1)

            def spans(i):
                for n, start in enumerate((rows[:, 0, 0:1], ow[:, 1:2])):
                    nc.vector.tensor_scalar(over[:, n + 1:n + 2], rows[:, 0, P - 1:P], float(N - 1), start,
                                            ALU.min, ALU.subtract).then_inc(bad_ok, 1)
                nc.vector.tensor_scalar(over[:, 3:4], due[:, :], ow[:, 1:2], None, ALU.subtract).then_inc(bad_ok, 1)
                dve.wait_ge(bad_ok, i * 9 + 4)
                nc.vector.tensor_scalar(due[:, :], due[:, :], float(TPB * P), None, ALU.add).then_inc(bad_ok, 1)
                for n, most in enumerate((0, LOC - 1, WIN - 1, 0)):
                    nc.vector.tensor_scalar(bad[:, n:n + 1], over[:, n:n + 1], most + 0.5, None, ALU.is_gt).then_inc(bad_ok, 1)
                dve.wait_ge(bad_ok, i * 9 + 9)
                dve.wait_ge(bad_added, i + 1)
                nc.vector.tensor_tensor(bad_sum[:, :], bad_sum[:, :], bad[:, :], ALU.add).then_inc(bad_added, 1)

            def turn(i, first, last, j, b, final):
                n0 = i * TPB
                convert(i, first)
                if not first:
                    dve.wait_ge(hn_ok, n0)
                for k in range(TPB):
                    dve.wait_ge(x_in[b][part_of(k)], j * 16 + 16)
                    nc.vector.bn_stats(stats[:, k, :], x_t[:, b, k, :]).then_inc(stats_ok, 1)
                order(i, first)
                for k in range(TPB):
                    if k == 0:
                        dve.wait_ge(stats_ok, n0 + TPB)
                        dve.sem_inc(passed, 1)
                    nc.vector.bn_aggr(mv[:, k, :], stats[:, k, :]).then_inc(mv_ok, 1)
                dve.wait_ge(mv_ok, n0 + TPB)
                nc.vector.tensor_scalar(var[:, :], mv[:, :, 1], EPS, None, ALU.add).then_inc(var_ok, 1)
                window(i, first)
                dve.wait_ge(base_ok, i + 1)
                half_key(i)
                offsets(i, first)
                full_key(i)
                dve.wait_ge(std_ok, i + 1)
                nc.vector.reciprocal(rstd[:, :], std[:, :]).then_inc(rstd_ok, 1)
                dve.wait_ge(rstd_ok, i + 1)
                for k in range(TPB):
                    if not first:
                        dve.wait_ge(table_out[part_of(k)], i * 16)
                        dve.wait_ge(hT_ps, (i - 1) * TPB + k + 1)
                    nc.vector.tensor_scalar(hn[:, k, :], x_t[:, b, k, :], mv[:, k, 0:1], rstd[:, k:k + 1],
                                            ALU.subtract, ALU.mult).then_inc(hn_ok, 1)
                spans(i)

            several(dve, PREPS // 2, pairs(turn))
            dve.wait_ge(bad_added, PREPS + 1)
            nc.vector.reduce_sum(bad_row[:, :], bad_sum[:, :], AX_X).then_inc(bad_rowed, 1)
            dve.wait_ge(bad_ps, 1)
            nc.vector.tensor_scalar(flag[:, :], p_small[0:1, 0:1], 0.5, None, ALU.is_gt).then_inc(flag_ok, 1)
            dve.wait_ge(w_in, 16 * (DH + H + 3))
            nc.vector.tensor_scalar(tmp[:, :], tmp[:, :], 0.1, 5.0, ALU.max, ALU.min).then_inc(tmp_ok, 1)
            dve.wait_ge(tmp_ok, 1)
            nc.vector.reciprocal(rtmp[:, :], tmp[:, :]).then_inc(tmp_ok, 1)
            dve.wait_ge(tmp_ok, 2)
            nc.vector.tensor_scalar(rtmp[:, :], rtmp[:, :], -1.0, None, ALU.mult).then_inc(tmp_ok, 1)
            dve.wait_ge(tmp_ok, 3)
            for h in range(DH):
                dve.wait_ge(wx_ps, 2 * h + 1)
                nc.vector.tensor_copy(wxT[:, :, :], p_own[0:C, :, :].rearrange("p a (b n) -> p (a b) n", n=P)).then_inc(wx_ok, 1)
                dve.wait_ge(wx_ps, 2 * h + 2)
                nc.vector.tensor_tensor(heads(wxs[:, h, :]), heads(p_cols[:, 0, :]), per_head(rtmp[:, :]), ALU.mult).then_inc(wx_ok, 1)
            dve.wait_ge(wx_ps, 2 * DH + 1)
            nc.vector.tensor_tensor(heads(bfull[:, :]), heads(p_cols[:, 1, :]), per_head(rtmp[:, :]), ALU.mult).then_inc(wx_ok, 1)
            dve.wait_ge(wx_ok, 2 * DH + 1)

        @block.scalar
        def _(act):
            def deviation(i, first):
                act.wait_ge(var_ok, i + 1)
                if not first:
                    act.wait_ge(rstd_ok, i)
                nc.scalar.activation(std[:, :], var[:, :], ACT.Sqrt).then_inc(std_ok, 1)

            def copy_own(i, j, b, k, fresh):
                act.wait_ge(own_ps, i * TPB + k + 1)
                if not fresh:
                    act.wait_ge(base_out[b][part_of(k)], j * 16)
                nc.scalar.activation(own[:, b, k, :], p_own[:, k % 2, 0:D], ACT.Copy).then_inc(own_copied, 1)

            deviation(0, True)

            def turn(i, first, last, j, b, final):
                fresh = isinstance(j, int) and j == 0
                act.wait_ge(cols_ps, i + 1)
                act.sem_inc(passed, 1)
                nc.scalar.activation(meta[:, 0:4, bass.ds(i * MC, MC)], p_cols[:, 0, :].rearrange("p (a c) -> p a c", a=4)[:, :, 0:MC], ACT.Copy)
                nc.scalar.activation(meta[:, 4, bass.ds(i * MC, MC)], p_cols[:, 1, 0:MC], ACT.Copy).then_inc(cols_ok, 1)
                for k in range(TPB):
                    act.wait_ge(hT_ps, i * TPB + k + 1)
                    if not (first and k < 2):
                        act.wait_ge(own_ps, reused(i, k, 2, TPB))
                    nc.scalar.activation(hT[:, k % 2, :, :], p_hT[:, k % 2, 0:D].rearrange("p (h n) -> p h n", h=DH), ACT.Copy).then_inc(hT_ok, 1)
                    if k:
                        copy_own(i, j, b, k - 1, fresh)
                    if k == 5 and not last:
                        deviation(i + 1, False)
                copy_own(i, j, b, TPB - 1, fresh)

            several(act, PREPS // 2, pairs(turn))

        @block.tensor
        def _(pe):
            pe.wait_ge(masks_ok, 2)
            pe.wait_ge(weights_in, 16 * (DH + 1))
            for h in range(DH):
                for g in range(DH):
                    last = nc.tensor.transpose(p_own[:, h, g * P:(g + 1) * P], slw[:, g, h * P:(h + 1) * P], ident[:, :])
                last.then_inc(sl_turned, 1)
            pe.wait_ge(sl_ready, DH)

            def own_product(i, k, first):
                n = i * TPB + k
                pe.wait_ge(hT_ok, n + 1)
                if not (first and k < 2):
                    pe.wait_ge(own_copied, reused(i, k, 2, TPB))
                for h in range(DH):
                    last = nc.tensor.matmul(p_own[:, k % 2, 0:D], hT[:, k % 2, h, :], slT[:, h, :], start=(h == 0), stop=(h == DH - 1))
                last.then_inc(own_ps, 1)

            def group_starts(i, first):
                pe.wait_ge(rows_ok, i + 1)
                if not first:
                    pe.wait_ge(base_ok, i)
                nc.tensor.matmul(p_small[0:MC, 0:1], first_of[:, :, :].rearrange("p g c -> p (g c)"), rows[:, 0, 0:1],
                                 start=True, stop=True).then_inc(base_ps, 1)

            group_starts(0, True)

            def turn(i, first, last):
                pe.wait_ge(planes_ok, i * 2 + 2)
                if not first:
                    pe.wait_ge(cols_ok, i)
                for n, plane in enumerate((rows[:, 2, :], key[:, 0, :], key[:, 1, :], rows[:, 0, :], rows[:, 1, :])):
                    t = nc.tensor.transpose(p_cols[:, n // 4, (n % 4) * P:(n % 4) * P + MC], plane, ident[0:MC, 0:MC])
                t.then_inc(cols_ps, 1)
                for k in range(TPB):
                    n = i * TPB + k
                    pe.wait_ge(hn_ok, n + 1)
                    if not (first and k < 2):
                        pe.wait_ge(hT_ok, reused(i, k, 2, TPB))
                    for h in range(DH):
                        t = nc.tensor.transpose(p_hT[:, k % 2, h * P:(h + 1) * P], hn[:, k, h * P:(h + 1) * P], ident[:, :])
                    t.then_inc(hT_ps, 1)
                    if k:
                        own_product(i, k - 1, first)
                    if k == 3 and not last:
                        group_starts(i + 1, False)
                own_product(i, TPB - 1, first)

            several(pe, PREPS, turn)
            pe.wait_ge(bad_rowed, 1)
            nc.tensor.matmul(p_small[0:1, 0:1], bad_row[:, :], ones[0:MC, 0:1], start=True, stop=True).then_inc(bad_ps, 1)
            pe.wait_ge(own_copied, PREPS * TPB)
            pe.wait_ge(cols_ok, PREPS)
            pe.wait_ge(w_in, 16 * (DH + H + 3))
            for h in range(DH):
                if h:
                    pe.wait_ge(wx_ok, 2 * h)
                for n in range(H):
                    e = nc.tensor.transpose(p_own[0:C, n // 4, (n % 4) * P:(n % 4 + 1) * P], wx[:, h, n * C:(n + 1) * C], ident[:, :])
                e.then_inc(wx_ps, 1)
                pe.wait_ge(wx_ok, 2 * h + 1)
                for n in range(H):
                    e = nc.tensor.matmul(p_cols[:, 0, n * G:(n + 1) * G], wxT[:, n, :], ws[:, :], start=True, stop=True)
                e.then_inc(wx_ps, 1)
            for n in range(H):
                nc.tensor.matmul(p_cols[:, 1, n * G:(n + 1) * G], bxT[:, n:n + 1].to_broadcast((C, P)), ws[:, :], start=True, stop=False)
                e = nc.tensor.matmul(p_cols[:, 1, n * G:(n + 1) * G], ones[0:1, :], bsl[:, :], start=False, stop=True)
            e.then_inc(wx_ps, 1)


def main_pass(nc, scope, sb, ps, sem, passed, table, base, sums, mid, ident, ones, meta, w_sb,
              start_row, flag, bfull, wxs, tok, tok_sum):
    STEPS = 2 * CH + 1
    SR, CR = 5, 2
    rows = sb(scope, "a_rows", [P, 2, CH, D])
    idx = sb(scope, "a_idx", [P, 2, CH], U32)
    kd = sb(scope, "a_kd", [P, 2, 2, CH])
    spot = sb(scope, "a_spot", [P, SR, P])
    hits = sb(scope, "a_hits", [P, 2, P], BF16)
    acc = sb(scope, "a_acc", [P, 2, DH * R, WIN])
    res = sb(scope, "a_res", [P, 2, MW])
    count = sb(scope, "a_count", [P, P])
    zeros = sb(scope, "a_zeros", [P, DH * R * WIN])
    ones_bf = sb(scope, "a_ones_bf", [P, 1], BF16)
    p_chunk = ps(scope, "ap_chunk", [P, CR, 512])
    p_acc = ps(scope, "ap_acc", [P, 2, 512])
    p_tok = ps(scope, "sp_tok", [P, 4, D])
    p_lg = ps(scope, "sp_lg", [P, HG])
    p_x = ps(scope, "sp_x", [P, 512])
    real = sb(scope, "s_real", [P, TILES])
    m = sb(scope, "s_m", [P, MW])
    bs = sb(scope, "s_bs", [P, D])
    deg = sb(scope, "s_deg", [P, 2])
    xs = sb(scope, "s_xs", [P, D])
    stats = sb(scope, "s_stats", [P, 6])
    mv = sb(scope, "s_mv", [P, 2])
    dev = sb(scope, "s_dev", [P, 3])
    xn = sb(scope, "s_xn", [P, TPB, D])
    xT = sb(scope, "s_xT", [P, DH, P])
    lg = sb(scope, "s_lg", [P, HG])
    least = sb(scope, "s_least", [P, H])
    ex = sb(scope, "s_ex", [P, HG])
    tot = sb(scope, "s_tot", [P, H])
    inv = sb(scope, "s_inv", [P, 2, H])
    sw = sb(scope, "s_sw", [P, HG])
    sw_sum = sb(scope, "s_sw_sum", [P, HG])
    one_idx = sb(scope, "g_idx", [P, 1], U32)
    row_idx = sb(scope, "g_row_idx", [P, 1], U32)
    dt = sb(scope, "g_dt", [P, 2])
    mask = sb(scope, "g_mask", [P, R])
    diag = sb(scope, "g_diag", [P, P])
    same = sb(scope, "g_same", [P, P])
    below = sb(scope, "g_below", [P, P])
    spill = sb(scope, "g_spill", [P, P])
    trash = sb(scope, "g_trash", [P, 1])
    pick = sb(scope, "g_pick", [P, 4])
    gT = sb(scope, "g_gT", [P, DH, P])
    msg = sb(scope, "g_msg", [P, MW])
    wide = sb(scope, "g_wide", [P, MP])

    consts = sem("a_consts")
    zero_out = sem("a_zero_out")
    idx_ok = sem("a_idx_ok")
    kd_ok = sem("a_kd_ok")
    acc_zero = sem("a_acc_zero")
    gathered = [[sem(f"a_gathered{b}_{c}") for c in range(CH)] for b in range(2)]
    built = sem("a_built")
    counted = sem("a_counted")
    deg_ps = sem("a_deg_ps")
    summed = sem("a_summed")
    added = sem("a_added")
    msg_ok = sem("a_msg_ok")
    res_ok = sem("a_res_ok")
    accumulated = sem("a_accumulated")

    g_idx_ok = sem("g_idx_ok")
    g_rows_in = sem("g_rows_in")
    g_dt_ok = sem("g_dt_ok")
    g_mask_ok = sem("g_mask_ok")
    g_diag_ok = sem("g_diag_ok")
    g_dst_ps = sem("g_dst_ps")
    g_same_ok = sem("g_same_ok")
    g_before_ok = sem("g_before_ok")
    g_pick_ok = sem("g_pick_ok")
    g_row_idx_ok = sem("g_row_idx_ok")
    g_turned = sem("g_turned")
    g_gT_ok = sem("g_gT_ok")
    g_part_ps = sem("g_part_ps")
    g_msg_ok = sem("g_msg_ok")
    g_comb_ps = sem("g_comb_ps")
    g_wide_ok = sem("g_wide_ok")
    g_scattered = sem("g_scattered")

    real_ok = sem("s_real_ok")
    m_in = sem("s_m_in")
    deg_ok = sem("s_deg_ok")
    xs_ok = sem("s_xs_ok")
    x1_out = sem("s_x1_out")
    stats_ok = sem("s_stats_ok")
    mv_ok = sem("s_mv_ok")
    var_ok = sem("s_var_ok")
    std_ok = sem("s_std_ok")
    rstd_ok = sem("s_rstd_ok")
    xn_ok = sem("s_xn_ok")
    xT_ps = sem("s_xT_ps")
    xT_ok = sem("s_xT_ok")
    lg_ps = sem("s_lg_ps")
    lg_ok = sem("s_lg_ok")
    least_ok = sem("s_least_ok")
    ex_ok = sem("s_ex_ok")
    inv_ok = sem("s_inv_ok")
    sw_ok = sem("s_sw_ok")
    sw_out = sem("s_sw_out")
    tok_ps = sem("s_tok_ps")
    sum_ok = sem("s_sum_ok")
    tok_ok = sem("s_tok_ok")

    def behind(eng, semaphore, count):
        if not (isinstance(count, int) and count <= 0):
            eng.wait_ge(semaphore, count)

    def load_tile(sp, t):
        behind(sp, xs_ok, t)
        sp.dma_start(m[:, :], sums[bass.ds(t * P, P), 0:MW]).then_inc(m_in, 16)
        sp.dma_start(bs[:, :], base[bass.ds(t * P, P), :]).then_inc(m_in, 16)

    def store_x1(sp, t):
        sp.wait_ge(xs_ok, t + 1)
        sp.sem_inc(passed, 1)
        sp.dma_start(mid[bass.ds(t * P, P), HG:HG + D], xs[:, :]).then_inc(x1_out, 16)

    def store_slices(sp, t):
        sp.wait_ge(sw_ok, t + 1)
        sp.sem_inc(passed, 1)
        sp.dma_start(mid[bass.ds(t * P, P), 0:HG], sw[:, :]).then_inc(sw_out, 16)

    def tile_dve(dve, t, k, n, apart=1):
        if n == 0:
            dve.wait_ge(m_in, t * 32 + 32)
            nc.vector.tensor_scalar(deg[:, 0:1], m[:, D:MW], 1.0, None, ALU.max).then_inc(deg_ok, 1)
        if n == 1:
            dve.wait_ge(deg_ok, t * 2 + 1)
            nc.vector.reciprocal(deg[:, 1:2], deg[:, 0:1]).then_inc(deg_ok, 1)
        if n == 2:
            behind(dve, x1_out, t * 16)
            dve.wait_ge(deg_ok, t * 2 + 2)
            nc.vector.scalar_tensor_tensor(out=xs[:, :], in0=m[:, 0:D], scalar=deg[:, 1:2], in1=bs[:, :],
                                           op0=ALU.mult, op1=ALU.add).then_inc(xs_ok, 1)
        if n == 3:
            dve.wait_ge(xs_ok, t + 1)
            nc.vector.bn_stats(stats[:, :], xs[:, :]).then_inc(stats_ok, 1)
        if n == 4:
            dve.wait_ge(stats_ok, t + 1)
            dve.sem_inc(passed, 1)
            nc.vector.bn_aggr(mv[:, :], stats[:, :]).then_inc(mv_ok, 1)
        if n == 5:
            dve.wait_ge(mv_ok, t + 1)
            nc.vector.tensor_scalar(dev[:, 0:1], mv[:, 1:2], EPS, None, ALU.add).then_inc(var_ok, 1)
        if n == 9:
            dve.wait_ge(std_ok, t + 1)
            nc.vector.reciprocal(dev[:, 2:3], dev[:, 1:2]).then_inc(rstd_ok, 1)
        if n == 10:
            behind(dve, tok_ps, t - apart)
            dve.wait_ge(rstd_ok, t + 1)
            nc.vector.tensor_scalar(xn[:, k, :], xs[:, :], mv[:, 0:1], dev[:, 2:3], ALU.subtract, ALU.mult).then_inc(xn_ok, 1)
        if n == CH + 1:
            behind(dve, ex_ok, t)
            dve.wait_ge(lg_ps, t + 1)
            nc.vector.tensor_tensor(lg[:, :], p_lg[:, :], bfull[:, :], ALU.add).then_inc(lg_ok, 1)
        if n == CH + 2:
            dve.wait_ge(lg_ok, t + 1)
            nc.vector.tensor_reduce(least[:, :], heads(lg[:, :]), AX_X, ALU.min).then_inc(least_ok, 1)
        if n == CH + 7:
            dve.wait_ge(ex_ok, t + 1)
            nc.vector.reciprocal(inv[:, 0, :], tot[:, :]).then_inc(inv_ok, 1)
        if n == CH + 8:
            dve.wait_ge(inv_ok, t * 2 + 1)
            nc.vector.tensor_scalar(inv[:, 1, :], inv[:, 0, :], real[:, bass.ds(t, 1)], None, ALU.mult).then_inc(inv_ok, 1)
        if n == CH + 9:
            behind(dve, sw_out, t * 16)
            behind(dve, tok_ps, t)
            dve.wait_ge(inv_ok, t * 2 + 2)
            nc.vector.tensor_tensor(heads(sw[:, :]), heads(ex[:, :]), per_head(inv[:, 1, :]), ALU.mult).then_inc(sw_ok, 1)
        if n == CH + 11:
            dve.wait_ge(sum_ok, t + 1)
            dve.wait_ge(sw_ok, t + 1)
            nc.vector.tensor_tensor(sw_sum[:, :], sw_sum[:, :], sw[:, :], ALU.add).then_inc(sum_ok, 1)

    def tile_dve_all(dve, t):
        for n in range(STEPS):
            tile_dve(dve, t, 0, n, 0)

    def deviation(act, t):
        act.wait_ge(var_ok, t + 1)
        behind(act, rstd_ok, t)
        nc.scalar.activation(dev[:, 1:2], dev[:, 0:1], ACT.Sqrt).then_inc(std_ok, 1)

    def copy_xT(act, t):
        act.wait_ge(xT_ps, t + 1)
        nc.scalar.activation(xT[:, :, :], p_x[:, 0:D].rearrange("p (h n) -> p h n", h=DH), ACT.Copy).then_inc(xT_ok, 1)

    def exponentials(act, t):
        act.wait_ge(least_ok, t + 1)
        behind(act, sw_ok, t)
        for h in range(H):
            e = nc.scalar.activation(ex[:, h * G:(h + 1) * G], lg[:, h * G:(h + 1) * G], ACT.Exp, scale=-1.0,
                                     bias=least[:, h:h + 1], accum_out=tot[:, h:h + 1])
        e.then_inc(ex_ok, 1)

    def tile_act_all(act, t):
        deviation(act, t)
        copy_xT(act, t)
        exponentials(act, t)

    def tile_pe(pe, t, k, n):
        if n == 11:
            pe.wait_ge(xn_ok, t + 1)
            for h in range(DH):
                e = nc.tensor.transpose(p_x[:, h * P:(h + 1) * P], xn[:, k, h * P:(h + 1) * P], ident[:, :])
            e.then_inc(xT_ps, 1)
        for h in range(DH):
            if n == 13 + h:
                behind(pe, lg_ok, t)
                pe.wait_ge(xT_ok, t + 1)
                e = nc.tensor.matmul(p_lg[:, :], xT[:, h, :], wxs[:, h, :], start=(h == 0), stop=(h == DH - 1))
                if h == DH - 1:
                    e.then_inc(lg_ps, 1)
        if n in (CH + 12, 2 * CH):
            pe.wait_ge(sw_ok, t + 1)
            for j in (0, 1) if n < 2 * CH else (2, 3):
                e = nc.tensor.matmul(p_tok[:, j, :], sw[:, j * P:(j + 1) * P], xn[:, k, :],
                                     start=(isinstance(t, int) and t == 0 and j % 2 == 0), stop=False, skip_group_check=True)
            if n == 2 * CH:
                e.then_inc(tok_ps, 1)

    def tile_pe_all(pe, t):
        for n in range(STEPS):
            tile_pe(pe, t, 0, n)

    def tiles_beside(i, place):
        found = []
        for back in range(3):
            turn, at = (i, place - back) if place >= back else (i - 1, place - back + MG)
            if at == LAG - 1:
                continue
            k = at - LAG if at >= LAG else at - LAG + MG
            if at < LAG:
                turn = turn - 1
            if isinstance(i, int) and i == 0 and (at < LAG or place < back):
                continue
            if isinstance(turn, int) and turn == PREPS:
                continue
            found.append((turn * TPB + k, k, back * CH))
        return found

    def general_pool(pool):
        pool.wait_ge(zero_out, 16 * LATE_PARTS)
        nc.gpsimd.iota(trash[:, :], pattern=[[0, 1]], base=TRASH, channel_multiplier=1,
                       allow_small_or_imprecise_dtypes=True).then_inc(consts, 1)
        nc.gpsimd.memset(wide[:, :], 0.0).then_inc(consts, 1)
        nc.gpsimd.memset(below[:, :], 1.0).then_inc(consts, 1)
        pool.wait_ge(consts, 6)
        nc.gpsimd.affine_select(out=below[:, :], in_=below[:, :], compare_op=ALU.is_gt, fill=0.0, base=0,
                                pattern=[[-1, P]], channel_multiplier=1).then_inc(consts, 1)

        def turn(j, first, last):
            pool.wait_ge(g_idx_ok, j + 1)
            pool.sem_inc(passed, 1)
            pool.indirect_dma_start(out=rows[:, 0, 0, :], out_offset=None, in_=table,
                                    in_offset=bass.IndirectOffsetOnAxis(ap=one_idx[:, 0:1], axis=0)).then_inc(g_rows_in, 16)
            pool.wait_ge(g_wide_ok, j + 1)
            pool.sem_inc(passed, 1)
            pool.wait_ge(g_row_idx_ok, j + 1)
            pool.sem_inc(passed, 1)
            pool.indirect_dma_start(out=sums, out_offset=bass.IndirectOffsetOnAxis(ap=row_idx[:, 0:1], axis=0),
                                    in_=wide[:, :], in_offset=None, compute_op=ALU.add).then_inc(g_scattered, 16)
            pool.wait_ge(g_scattered, j * 16 + 16)
            pool.sem_inc(passed, 1)

        several(pool, CHUNKS, turn)

    def general_act(act):
        def turn(j, first, last):
            if not first:
                act.wait_ge(g_rows_in, j * 16)
                act.sem_inc(passed, 1)
            nc.scalar.activation(one_idx[:, 0:1], meta[:, 0, bass.ds(j, 1)], ACT.Copy).then_inc(g_idx_ok, 1)
            act.wait_ge(g_turned, j + 1)
            if not first:
                act.wait_ge(g_part_ps, j * R)
            nc.scalar.activation(gT[:, :, :], p_chunk[:, 1, 0:D].rearrange("p (h n) -> p h n", h=DH), ACT.Copy).then_inc(g_gT_ok, 1)
            act.wait_ge(g_comb_ps, j + 1)
            if not first:
                act.wait_ge(g_scattered, j * 16)
            nc.scalar.activation(wide[:, 0:MW], p_lg[:, 0:MW], ACT.Copy).then_inc(g_wide_ok, 1)

        act.wait_ge(consts, 7)
        several(act, CHUNKS, turn)
        several(act, TILES, lambda t, first, last: tile_act_all(act, t))

    def general_dve(dve):
        dve.wait_ge(consts, 7)
        nc.vector.memset(msg[:, D:MW], 1.0).then_inc(g_before_ok, 1)

        def turn(j, first, last):
            if not first:
                dve.wait_ge(g_row_idx_ok, j)
                dve.wait_ge(g_mask_ok, j)
                dve.sem_inc(passed, 1)
            nc.vector.tensor_copy(dt[:, :], meta[:, 3:5, bass.ds(j, 1)].rearrange("p a c -> p (a c)")).then_inc(g_dt_ok, 1)
            dve.wait_ge(g_dt_ok, j + 1)
            if not first:
                dve.wait_ge(g_msg_ok, j * R)
            nc.vector.tensor_scalar(mask[:, :], count[:, 0:R], dt[:, 1:2], None, ALU.is_equal).then_inc(g_mask_ok, 1)
            if not first:
                dve.wait_ge(g_dst_ps, j)
            nc.vector.tensor_scalar(diag[:, :], ident[:, :], dt[:, 0:1], None, ALU.mult).then_inc(g_diag_ok, 1)
            dve.wait_ge(g_dst_ps, j + 1)
            if not first:
                dve.wait_ge(g_comb_ps, j)
            nc.vector.tensor_scalar(same[:, :], p_chunk[:, 0, 0:P], dt[:, 0:1], None, ALU.is_equal).then_inc(g_same_ok, 1)
            dve.wait_ge(g_same_ok, j + 1)
            dve.wait_ge(g_before_ok, j + 1)
            nc.vector.tensor_tensor_reduce(spill[:, :], same[:, :], below[:, :], 1.0, 0.0, ALU.mult, ALU.add,
                                           pick[:, 0:1]).then_inc(g_before_ok, 1)
            dve.wait_ge(g_before_ok, j + 2)
            nc.vector.tensor_scalar(pick[:, 1:2], pick[:, 0:1], 0.5, None, ALU.is_lt).then_inc(g_pick_ok, 1)
            nc.vector.tensor_tensor(pick[:, 2:3], dt[:, 0:1], trash[:, :], ALU.subtract).then_inc(g_pick_ok, 1)
            dve.wait_ge(g_pick_ok, j * 3 + 2)
            nc.vector.tensor_tensor(pick[:, 3:4], pick[:, 2:3], pick[:, 1:2], ALU.mult).then_inc(g_pick_ok, 1)
            dve.wait_ge(g_pick_ok, j * 3 + 3)
            if not first:
                dve.wait_ge(g_scattered, j * 16)
            nc.vector.tensor_tensor(row_idx[:, :], pick[:, 3:4], trash[:, :], ALU.add).then_inc(g_row_idx_ok, 1)
            dve.wait_ge(g_mask_ok, j + 1)
            for r in range(R):
                dve.wait_ge(g_part_ps, j * R + r + 1)
                if r == 0:
                    if not first:
                        dve.wait_ge(g_comb_ps, j)
                    nc.vector.tensor_scalar(msg[:, 0:D], p_acc[:, 0, 0:D], mask[:, 0:1], None, ALU.mult).then_inc(g_msg_ok, 1)
                    continue
                dve.wait_ge(g_msg_ok, j * R + r)
                nc.vector.scalar_tensor_tensor(out=msg[:, 0:D], in0=p_acc[:, r % 2, 0:D], scalar=mask[:, r:r + 1],
                                               in1=msg[:, 0:D], op0=ALU.mult, op1=ALU.add).then_inc(g_msg_ok, 1)

        several(dve, CHUNKS, turn)
        several(dve, TILES, lambda t, first, last: tile_dve_all(dve, t))

    def general_pe(pe):
        pe.wait_ge(consts, 7)

        def turn(j, first, last):
            pe.wait_ge(g_diag_ok, j + 1)
            if not first:
                pe.wait_ge(g_same_ok, j)
            nc.tensor.matmul(p_chunk[:, 0, 0:P], ones[:, :], diag[:, :], start=True, stop=True).then_inc(g_dst_ps, 1)
            pe.wait_ge(g_rows_in, j * 16 + 16)
            if not first:
                pe.wait_ge(g_gT_ok, j)
            for h in range(DH):
                t = nc.tensor.transpose(p_chunk[:, 1, h * P:(h + 1) * P], rows[:, 0, 0, h * P:(h + 1) * P], ident[:, :])
            t.then_inc(g_turned, 1)
            pe.wait_ge(g_gT_ok, j + 1)
            for r in range(R):
                if not first or r >= 2:
                    pe.wait_ge(g_msg_ok, j * R + r - 1)
                for h in range(DH):
                    m = nc.tensor.matmul(p_acc[:, r % 2, 0:D], gT[:, h, :], w_sb[:, h, r, :], start=(h == 0), stop=(h == DH - 1))
                m.then_inc(g_part_ps, 1)
            pe.wait_ge(g_msg_ok, j * R + R)
            if not first:
                pe.wait_ge(g_wide_ok, j)
            nc.tensor.matmul(p_lg[:, 0:MW], same[:, :], msg[:, :], start=True, stop=True).then_inc(g_comb_ps, 1)

        several(pe, CHUNKS, turn)
        several(pe, TILES, lambda t, first, last: tile_pe_all(pe, t))

    def zero_sums(sp, n):
        at = ZERO * PREPS + n * LATE
        sp.dma_start(sums.rearrange("(p a) w -> p (a w)", p=P)[:, at:at + LATE], zeros[:, :]).then_inc(zero_out, 16)

    def general_sp(sp):
        for n in range(LATE_PARTS):
            zero_sums(sp, n)
        sp.wait_ge(g_scattered, CHUNKS * 16)
        load_tile(sp, 0)

        def turn(t, first, last):
            store_x1(sp, t)
            if not last:
                load_tile(sp, t + 1)
            store_slices(sp, t)

        several(sp, TILES, turn)

    with nc.Block() as block:
        @block.sync
        def _(sp):
            sp.wait_ge(consts, 1)
            general = sp.value_load(flag[0:1, 0:1], min_val=0, max_val=1)
            with sp.If(general == 0):
                def load_behind(t, step):
                    in_time = step - 2
                    if isinstance(in_time, int):
                        in_time = min(in_time, WORK_GROUPS)
                    sp.wait_ge(accumulated, in_time * 16)
                    load_tile(sp, t)

                for n in range(LATE_PARTS):
                    sp.wait_ge(summed, 3 * n + 1)
                    zero_sums(sp, n)
                load_behind(0, LAG)

                def beside(i, place):
                    for t, k, step in tiles_beside(i, place):
                        if step == 0:
                            store_x1(sp, t)
                            if not (isinstance(t, int) and t == TILES - 1):
                                load_behind(t + 1, i * MG + place + (2 if place == LAG - 2 else 1))
                        if step == CH:
                            store_slices(sp, t)

                def turn(i, first, last):
                    for place in range(MG_LAST if last else MG):
                        beside(i, place)

                several(sp, PREPS, turn)
                for i, place in TAIL:
                    beside(i, place)
            with sp.Else():
                general_sp(sp)
            sp.wait_ge(x1_out, TILES * 16)
            sp.wait_ge(sw_out, TILES * 16)

        @block.gpsimd
        def _(pool):
            nc.gpsimd.memset(zeros[:, :], 0.0).then_inc(consts, 1)
            nc.gpsimd.iota(count[:, :], pattern=[[1, P]], base=0, channel_multiplier=0,
                           allow_small_or_imprecise_dtypes=True).then_inc(consts, 1)
            nc.gpsimd.memset(ones_bf[:, :], 1.0).then_inc(consts, 1)
            nc.gpsimd.memset(real[:, :], 1.0).then_inc(real_ok, 1)
            pool.wait_ge(real_ok, 1)
            nc.gpsimd.affine_select(out=real[:, :], in_=real[:, :], compare_op=ALU.is_gt, fill=0.0, base=N,
                                    pattern=[[-P, TILES]], channel_multiplier=-1).then_inc(real_ok, 1)
            general = pool.value_load(flag[0:1, 0:1], min_val=0, max_val=1)
            with pool.If(general == 0):
                def accumulate(g, b):
                    start = pool.value_load(start_row[0:1, 1, bass.ds(g * CH, 1)], min_val=0, max_val=NP)
                    pool.wait_ge(res_ok, g + 1)
                    pool.sem_inc(passed, 1)
                    pool.dma_start(sums[bass.ds(start, WIN), 0:MW], res[:, b, :], accum_op=ALU.add).then_inc(accumulated, 16)

                def turn(i, first, last):
                    for place in range(MG_LAST if last else MG):
                        b = place % 2
                        g = i * MG + place
                        pool.wait_ge(idx_ok, g + 1)
                        pool.sem_inc(passed, 1)
                        for c in range(CH):
                            if not (first and place < 2):
                                pool.wait_ge(summed, (g - 2) * CH + c + 1)
                                pool.sem_inc(passed, 1)
                                if c == 5:
                                    if first and place == 2:
                                        pool.wait_ge(zero_out, 16 * LATE_PARTS)
                                        pool.sem_inc(passed, 1)
                                    accumulate(g - 2, b)
                                if c == CH - 1:
                                    pool.wait_ge(accumulated, (g - 1) * 16)
                                    pool.sem_inc(passed, 1)
                            pool.indirect_dma_start(
                                out=rows[:, b, c, :], out_offset=None, in_=table,
                                in_offset=bass.IndirectOffsetOnAxis(ap=idx[:, b, c:c + 1], axis=0),
                            ).then_inc(gathered[b][c], 16)

                several(pool, PREPS, turn)
                for g in (WORK_GROUPS - 2, WORK_GROUPS - 1):
                    accumulate(g, g % 2)
                    pool.wait_ge(accumulated, 16 * (g + 1))
            with pool.Else():
                general_pool(pool)

        @block.scalar
        def _(act):
            act.wait_ge(consts, 3)
            general = act.value_load(flag[0:1, 0:1], min_val=0, max_val=1)
            with act.If(general == 0):
                def lists(g, b):
                    nc.scalar.activation(idx[:, b, :], meta[:, 0, bass.ds(g * CH, CH)], ACT.Copy).then_inc(idx_ok, 1)
                    nc.scalar.activation(kd[:, b, :, :], meta[:, 1:3, bass.ds(g * CH, CH)], ACT.Copy).then_inc(kd_ok, 1)

                def clear(g, b):
                    nc.scalar.activation(acc[:, b, :, :].rearrange("p a n -> p (a n)"), zeros[:, :], ACT.Copy).then_inc(acc_zero, 1)

                def collect(g, b, early):
                    if not early:
                        act.wait_ge(accumulated, (g - 1) * 16)
                    act.wait_ge(msg_ok, g + 1)
                    nc.scalar.activation(res[:, b, 0:D], p_acc[:, b, 0:D], ACT.Copy)
                    nc.scalar.activation(res[:, b, D:MW], p_acc[:, b, D:MW], ACT.Copy).then_inc(res_ok, 1)

                for n in range(2):
                    lists(n, n)
                    clear(n, n)

                def beside(i, place, first, last):
                    g = i * MG + place
                    b = place % 2
                    work = tiles_beside(i, place)
                    ahead = not (first and place == 0) and not (last and place == MG_LAST - 1)
                    if ahead:
                        act.wait_ge(summed, g * CH)
                        act.sem_inc(passed, 1)
                        lists(g + 1, 1 - b)
                    for t, k, step in work:
                        if step == CH:
                            exponentials(act, t)
                    for t, k, step in work:
                        if step == 0:
                            deviation(act, t)
                    if not (first and place == 0):
                        collect(g - 1, 1 - b, first and place <= 2)
                    for t, k, step in work:
                        if step == 0:
                            copy_xT(act, t)
                    if ahead:
                        act.wait_ge(msg_ok, g)
                        clear(g + 1, 1 - b)

                def turn(i, first, last):
                    for place in range(MG_LAST if last else MG):
                        beside(i, place, first, last)

                several(act, PREPS, turn)
                for i, place in TAIL:
                    work = tiles_beside(i, place)
                    for t, k, step in work:
                        if step == 0:
                            deviation(act, t)
                            copy_xT(act, t)
                    for t, k, step in work:
                        if step == CH:
                            exponentials(act, t)
                    if i * MG + place == WORK_GROUPS:
                        collect(WORK_GROUPS - 1, (WORK_GROUPS - 1) % 2, False)
            with act.Else():
                general_act(act)

        @block.vector
        def _(dve):
            nc.vector.memset(sw_sum[:, :], 0.0).then_inc(sum_ok, 1)
            dve.wait_ge(consts, 3)
            dve.wait_ge(real_ok, 2)
            general = dve.value_load(flag[0:1, 0:1], min_val=0, max_val=1)
            with dve.If(general == 0):
                def build(g, b, c, fresh, new):
                    q = g * CH + c
                    if c == 0:
                        dve.wait_ge(kd_ok, g + 1)
                    if not fresh:
                        dve.wait_ge(summed, q - SR + 1)
                    nc.vector.tensor_scalar(spot[:, c % SR, :], count[:, :], kd[:, b, 0, c:c + 1], None, ALU.is_equal).then_inc(built, 1)
                    if c == 0:
                        if not new:
                            dve.wait_ge(deg_ps, g - 1)
                        nc.vector.tensor_scalar(hits[:, b, :], count[:, :], kd[:, b, 1, 0:1], None, ALU.is_equal).then_inc(counted, 1)
                    else:
                        dve.wait_ge(counted, q)
                        nc.vector.scalar_tensor_tensor(out=hits[:, b, :], in0=count[:, :], scalar=kd[:, b, 1, c:c + 1], in1=hits[:, b, :],
                                                       op0=ALU.is_equal, op1=ALU.add).then_inc(counted, 1)

                def add(g, b, c, slot, at, early):
                    q = g * CH + c
                    if c == 0:
                        dve.wait_ge(acc_zero, g + 1)
                    if not (early and c == 0):
                        dve.wait_ge(added, q)
                    dve.wait_ge(summed, q + 1)
                    a = acc[:, b, :, bass.ds(at, LOC)]
                    nc.vector.tensor_tensor(a, a, p_chunk[:, slot, 0:D].rearrange("p (a l) -> p a l", l=LOC), ALU.add).then_inc(added, 1)

                build(0, 0, 0, True, True)
                build(0, 0, 1, True, True)

                def turn(i, first, last):
                    for place in range(MG_LAST if last else MG):
                        g = i * MG + place
                        b = place % 2
                        early = first and place == 0
                        work = tiles_beside(i, place)
                        _, at = nc.values_load_multi_w_load_instructions(
                            start_row[0:1, 0, bass.ds(g * CH, CH)], engines=(ENG.DVE,), min_val=0, max_val=WIN - LOC,
                            skip_runtime_bounds_check_because="the offsets are clamped, and the flag is clear")
                        for n in range(CH):
                            c = (n + 2) % CH
                            if n < CH - 2:
                                build(g, b, c, early and c < SR, first and place < 2)
                            elif not (last and place == MG_LAST - 1):
                                build(g + 1, 1 - b, c, False, first and place == 0)
                            for t, k, step in work:
                                tile_dve(dve, t, k, step + n)
                            add(g, b, n, (place * CH + n) % CR, at[n], early)

                several(dve, PREPS, turn)
                for i, place in TAIL:
                    for t, k, step in tiles_beside(i, place):
                        for n in range(CH):
                            tile_dve(dve, t, k, step + n)
            with dve.Else():
                general_dve(dve)
            dve.wait_ge(tok_ps, TILES)
            nc.vector.tensor_copy(tok[:, :, :], p_tok[:, :, :]).then_inc(tok_ok, 1)
            dve.wait_ge(tok_ps, TILES + 1)
            nc.vector.tensor_copy(tok_sum[:, :], p_x[:, 0:4]).then_inc(tok_ok, 1)
            dve.wait_ge(tok_ok, 2)

        @block.tensor
        def _(pe):
            pe.wait_ge(consts, 3)
            general = pe.value_load(flag[0:1, 0:1], min_val=0, max_val=1)
            with pe.If(general == 0):
                FIRST, SPAN = 1, 10

                def messages(g, b, c, early):
                    if c == FIRST:
                        pe.wait_ge(added, (g + 1) * CH)
                        if not early:
                            pe.wait_ge(res_ok, g - 1)
                        pe.wait_ge(counted, (g + 1) * CH)
                        nc.tensor.matmul(p_acc[:, b, D:MW], hits[:, b, :], ones_bf[:, :], start=True, stop=True).then_inc(deg_ps, 1)
                    k = c - FIRST
                    for n in range(k * DH * R // SPAN, (k + 1) * DH * R // SPAN):
                        e = nc.tensor.matmul(p_acc[:, b, 0:D], acc[:, b, n, :], w_sb[:, n // R, n % R, :],
                                             start=(n == 0), stop=(n == DH * R - 1))
                    if k == SPAN - 1:
                        e.then_inc(msg_ok, 1)

                def turn(i, first, last):
                    for place in range(MG_LAST if last else MG):
                        g = i * MG + place
                        b = place % 2
                        early = first and place < 2
                        work = tiles_beside(i, place)
                        for c in range(CH):
                            q = g * CH + c
                            pe.wait_ge(built, q + 1)
                            pe.wait_ge(gathered[b][c], (i * MG + place - b) * 8 + 16)
                            if not (early and b == 0 and c < CR):
                                pe.wait_ge(added, q - CR + 1)
                            for h in range(DH):
                                m = nc.tensor.matmul(p_chunk[:, (place * CH + c) % CR, h * P:(h + 1) * P], rows[:, b, c, h * P:(h + 1) * P],
                                                     spot[:, c % SR, :], start=True, stop=True)
                            m.then_inc(summed, 1)
                            if FIRST <= c < FIRST + SPAN and not (early and b == 0):
                                messages(g - 1, 1 - b, c, first and place <= 2)
                            for t, k, step in work:
                                tile_pe(pe, t, k, step + c)

                several(pe, PREPS, turn)
                for i, place in TAIL:
                    for back in (2, 0, 1):
                        for t, k, step in tiles_beside(i, place):
                            if step == back * CH:
                                for c in range(CH):
                                    tile_pe(pe, t, k, step + c)
                        if back == 0 and i * MG + place == WORK_GROUPS:
                            for c in range(FIRST, FIRST + SPAN):
                                messages(WORK_GROUPS - 1, (WORK_GROUPS - 1) % 2, c, False)
            with pe.Else():
                general_pe(pe)
            pe.wait_ge(sum_ok, TILES + 1)
            for j in range(4):
                e = nc.tensor.matmul(p_x[:, j:j + 1], sw_sum[:, j * P:(j + 1) * P], ones[:, 0:1], start=True, stop=True)
            e.then_inc(tok_ps, 1)


def token_stage(nc, scope, sb, ps, sem, w_fx, b_fx, w_q, w_k, w_v, w_out, ident, tok, tok_sum, mix):
    wfx = sb(scope, "t_wfx", [P, DH, HG])
    bfx = sb(scope, "t_bfx", [1, HG])
    wqkv = sb(scope, "t_wqkv", [C, 3, C])
    wo = sb(scope, "t_wo", [C, H, D])
    den = sb(scope, "t_den", [P, 2, 4])
    tn = sb(scope, "t_tn", [P, 4, D + 1])
    tT = sb(scope, "t_tT", [P, DH, HG])
    nrow = sb(scope, "t_nrow", [1, HG])
    tokT = sb(scope, "t_tokT", [C, HG])
    qkv = sb(scope, "t_qkv", [C, 3, HG])
    sc = sb(scope, "t_sc", [G, H, G])
    sm = sb(scope, "t_sm", [G, 3, H])
    aT = sb(scope, "t_aT", [G, H, G])
    vw = sb(scope, "t_vw", [G, H, D])
    p_a = ps(scope, "tp_a", [P, 2, 512])
    p_b = ps(scope, "tp_b", [P, 512])
    p_c = ps(scope, "tp_c", [P, 512])
    p_vw = ps(scope, "tp_vw", [P, 4, 512])
    w_in = sem("t_w_in")
    mm = sem("t_products")
    el = sem("t_elementwise")
    exped = sem("t_exped")

    def per_head(a):
        return a.rearrange("p (h a) -> p h a", a=1).to_broadcast((G, H, G))

    with nc.Block() as block:
        @block.sync
        def _(sp):
            for h in range(DH):
                sp.dma_start(wfx[:, h, :], w_fx[h * P:(h + 1) * P, :]).then_inc(w_in, 16)
            sp.dma_start(bfx[:, :], b_fx.rearrange("(a n) -> a n", a=1)).then_inc(w_in, 16)
            for n, w in enumerate((w_q, w_k, w_v)):
                sp.dma_start(wqkv[:, n, :], w).then_inc(w_in, 16)
            sp.dma_start(wo[:, :, :], w_out.rearrange("(h c) d -> c h d", c=C)).then_inc(w_in, 16)

        @block.vector
        def _(dve):
            nc.vector.tensor_scalar(den[:, 0, :], tok_sum[:, :], 1e-5, None, ALU.add).then_inc(el, 1)
            dve.wait_ge(el, 1)
            nc.vector.reciprocal(den[:, 1, :], den[:, 0, :]).then_inc(el, 1)
            dve.wait_ge(el, 2)
            nc.vector.tensor_tensor(tn[:, :, 0:D], tok[:, :, :], den[:, 1, :].rearrange("p (j a) -> p j a", a=1).to_broadcast((P, 4, D)),
                                    ALU.mult)
            nc.vector.tensor_tensor(tn[:, :, D], tok_sum[:, :], den[:, 1, :], ALU.mult).then_inc(el, 1)
            dve.wait_ge(mm, 1)
            nc.vector.tensor_copy(tT[:, :, :], p_a[:, :, :])
            nc.vector.tensor_copy(nrow[:, :], p_b[0:1, :]).then_inc(el, 1)
            dve.wait_ge(mm, 2)
            nc.vector.tensor_copy(tokT[:, :], p_c[0:C, :]).then_inc(el, 1)
            dve.wait_ge(mm, 3)
            nc.vector.tensor_copy(qkv[:, 0:2, :], p_a[0:C, :, :])
            nc.vector.tensor_copy(qkv[:, 2, :], p_b[0:C, :]).then_inc(el, 1)
            dve.wait_ge(mm, 4)
            nc.vector.tensor_scalar(sc[:, :, :], p_c[0:G, :].rearrange("p (h k) -> p h k", h=H), C ** -0.5, None, ALU.mult).then_inc(el, 1)
            dve.wait_ge(el, 7)
            nc.vector.reduce_max(sm[:, 0, :], sc[:, :, :], AX_X).then_inc(el, 1)
            dve.wait_ge(el, 8)
            nc.vector.tensor_tensor(sc[:, :, :], sc[:, :, :], per_head(sm[:, 0, :]), ALU.subtract).then_inc(el, 1)
            dve.wait_ge(exped, 1)
            nc.vector.reduce_sum(sm[:, 1, :], sc[:, :, :], AX_X).then_inc(el, 1)
            dve.wait_ge(el, 10)
            nc.vector.reciprocal(sm[:, 2, :], sm[:, 1, :]).then_inc(el, 1)
            dve.wait_ge(el, 11)
            nc.vector.tensor_tensor(sc[:, :, :], sc[:, :, :], per_head(sm[:, 2, :]), ALU.mult).then_inc(el, 1)
            dve.wait_ge(mm, 5)
            nc.vector.tensor_copy(vw[:, :, :], p_vw[0:G, :, :].rearrange("p a (b d) -> p (a b) d", d=D)).then_inc(el, 1)
            dve.wait_ge(mm, 6)
            nc.vector.tensor_copy(aT[:, :, :], p_a[0:G, 0, :].rearrange("p (h g) -> p h g", h=H)).then_inc(el, 1)
            dve.wait_ge(mm, 7)
            nc.vector.tensor_copy(mix[:, :, :], p_vw[:, 0:2, :].rearrange("p a (b d) -> p (a b) d", d=D)).then_inc(el, 1)
            dve.wait_ge(el, 15)

        @block.scalar
        def _(act):
            act.wait_ge(el, 9)
            nc.scalar.activation(sc[:, :, :], sc[:, :, :], ACT.Exp).then_inc(exped, 1)

        @block.tensor
        def _(pe):
            pe.wait_ge(el, 3)
            for j in range(4):
                for h in range(DH):
                    nc.tensor.transpose(p_a[:, h, j * P:(j + 1) * P], tn[:, j, h * P:(h + 1) * P], ident[:, :])
                m = nc.tensor.matmul(p_b[0:1, j * P:(j + 1) * P], tn[:, j, D:D + 1], ident[:, :], start=True, stop=True)
            m.then_inc(mm, 1)
            pe.wait_ge(w_in, 16 * (DH + 5))
            pe.wait_ge(el, 4)
            for n in range(H):
                own = slice(n * C, (n + 1) * C)
                for h in range(DH):
                    nc.tensor.matmul(p_c[0:C, own], wfx[:, h, own], tT[:, h, own], start=(h == 0), stop=False)
                m = nc.tensor.matmul(p_c[0:C, own], bfx[:, own], nrow[:, own], start=False, stop=True)
            m.then_inc(mm, 1)
            pe.wait_ge(el, 5)
            for n in range(3):
                m = nc.tensor.matmul(p_a[0:C, n, :] if n < 2 else p_b[0:C, :], wqkv[:, n, :], tokT[:, :], start=True, stop=True)
            m.then_inc(mm, 1)
            pe.wait_ge(el, 6)
            for n in range(H):
                own = slice(n * C, (n + 1) * C)
                m = nc.tensor.matmul(p_c[0:G, own], qkv[:, 0, own], qkv[:, 1, own], start=True, stop=True)
            m.then_inc(mm, 1)
            for n in range(H):
                m = nc.tensor.matmul(p_vw[0:G, n // 2, (n % 2) * D:(n % 2 + 1) * D], qkv[:, 2, n * C:(n + 1) * C], wo[:, n, :], start=True, stop=True)
            m.then_inc(mm, 1)
            pe.wait_ge(el, 12)
            for n in range(H):
                m = nc.tensor.transpose(p_a[0:G, 0, n * G:(n + 1) * G], sc[:, n, :], ident[0:G, 0:G])
            m.then_inc(mm, 1)
            pe.wait_ge(el, 14)
            for n in range(H):
                m = nc.tensor.matmul(p_vw[(n % 2) * G:(n % 2 + 1) * G, n // 4, (n // 2 % 2) * D:(n // 2 % 2 + 1) * D], aT[:, n, :], vw[:, n, :],
                                     start=True, stop=True)
            m.then_inc(mm, 1)


def output_pass(nc, scope, sb, ps, sem, b_out, mid, out, ident, mix):
    U, RING = 7, 4
    sl = sb(scope, "o_sl", [P, U, HG + D])
    sT = sb(scope, "o_sT", [P, U, 4, P])
    ot = sb(scope, "o_ot", [P, U, D])
    xb = sb(scope, "o_xb", [P, U, D])
    bo = sb(scope, "o_bo", [P, D])
    p_T = ps(scope, "op_T", [P, RING, 512])
    p_o = ps(scope, "op_o", [P, RING, 512])
    sl_in = [sem(f"o_sl_in{k}") for k in range(U)]
    bo_in = sem("o_bo_in")
    xb_ok = sem("o_xb_ok")
    turned = sem("o_turned")
    sT_ok = sem("o_sT_ok")
    o_ps = sem("o_ps")
    ot_ok = sem("o_ot_ok")
    out_out = [sem(f"o_out{k}") for k in range(U)]

    with nc.Block() as block:
        @block.sync
        def _(sp):
            sp.dma_start(bo[:, :], b_out.rearrange("(a n) -> a n", a=1).to_broadcast((P, D))).then_inc(bo_in, 16)
            for k in range(U):
                sp.dma_start(sl[:, k, :], mid[k * P:(k + 1) * P, :]).then_inc(sl_in[k], 16)

            def turn(i, first, last):
                for k in range(U):
                    t = i * U + k
                    if not last:
                        sp.wait_ge(xb_ok, t + 1)
                        sp.dma_start(sl[:, k, :], mid[bass.ds((t + U) * P, P), :]).then_inc(sl_in[k], 16)
                    sp.wait_ge(ot_ok, t + 1)
                    sp.dma_start(out[bass.ds(t * P, P), :], ot[:, k, :]).then_inc(out_out[k], 16)

            several(sp, TILES // U, turn)
            for k in range(U):
                sp.wait_ge(out_out[k], 16 * (TILES // U))

        @block.gpsimd
        def _(pool):
            pool.wait_ge(bo_in, 16)

            def turn(i, first, last):
                for k in range(U):
                    t = i * U + k
                    if not first:
                        pool.wait_ge(ot_ok, t - U + 1)
                    pool.wait_ge(turned, t + 1)
                    nc.gpsimd.tensor_tensor(xb[:, k, :], sl[:, k, HG:HG + D], bo[:, :], ALU.add).then_inc(xb_ok, 1)

            several(pool, TILES // U, turn)

        @block.tensor
        def _(pe):
            def turn_slices(i, k, first):
                t = i * U + k
                pe.wait_ge(sl_in[k], i * 16 + 16)
                if not (first and k < RING):
                    pe.wait_ge(sT_ok, reused(i, k, RING, U))
                for j in range(4):
                    m = nc.tensor.transpose(p_T[:, k % RING, j * P:(j + 1) * P], sl[:, k, j * P:(j + 1) * P], ident[:, :])
                m.then_inc(turned, 1)

            def blend(i, k, first):
                t = i * U + k
                pe.wait_ge(sT_ok, t + 1)
                if not (first and k < RING):
                    pe.wait_ge(ot_ok, reused(i, k, RING, U))
                for j in range(4):
                    m = nc.tensor.matmul(p_o[:, k % RING, 0:D], sT[:, k, j, :], mix[:, j, :], start=(j == 0), stop=(j == 3))
                m.then_inc(o_ps, 1)

            def turn(i, first, last):
                for k in range(U):
                    turn_slices(i, k, first)
                    if k:
                        blend(i, k - 1, first)
                    elif not first:
                        blend(i - 1, U - 1, False)

            several(pe, TILES // U, turn)
            blend(TILES // U - 1, U - 1, False)

        @block.scalar
        def _(act):
            def turn(i, first, last):
                for k in range(U):
                    t = i * U + k
                    act.wait_ge(turned, t + 1)
                    if not first:
                        act.wait_ge(o_ps, t - U + 1)
                    nc.scalar.activation(sT[:, k, :, :], p_T[:, k % RING, :].rearrange("p (j n) -> p j n", j=4), ACT.Copy).then_inc(sT_ok, 1)

            several(act, TILES // U, turn)

        @block.vector
        def _(dve):
            def turn(i, first, last):
                for k in range(U):
                    t = i * U + k
                    if not first:
                        dve.wait_ge(out_out[k], i * 16)
                    dve.wait_ge(o_ps, t + 1)
                    dve.wait_ge(xb_ok, t + 1)
                    nc.vector.tensor_tensor(ot[:, k, :], p_o[:, k % RING, 0:D], xb[:, k, :], ALU.add).then_inc(ot_ok, 1)

            several(dve, TILES // U, turn)


def kernel(x, src, dst, edge_type_8, L0_gnn_weight, L0_gnn_sl_w, L0_gnn_sl_b, L0_ffn_W_fx, L0_ffn_b_fx,
           L0_ffn_W_x, L0_ffn_b_x, L0_ffn_W_slice, L0_ffn_b_slice, L0_ffn_W_q, L0_ffn_W_k, L0_ffn_W_v,
           L0_ffn_W_out, L0_ffn_b_out, L0_ffn_temperature):
    import concourse.bacc as bacc
    from concourse.bass_utils import run_bass_kernel_spmd

    def filled(a, rows, value):
        a = np.ascontiguousarray(a)
        full = np.full((rows,) + a.shape[1:], value, a.dtype)
        full[:a.shape[0]] = a
        return full

    arrays = {
        "x": filled(x, NP, 0),
        "src": filled(src, EP + P, 0),
        "dst": filled(dst, EP + P, NP),
        "typ": filled(edge_type_8, EP + P, PAD_TYPE),
        "w_rel": L0_gnn_weight, "sl_w": L0_gnn_sl_w, "sl_b": L0_gnn_sl_b,
        "w_fx": L0_ffn_W_fx, "b_fx": L0_ffn_b_fx, "w_x": L0_ffn_W_x, "b_x": L0_ffn_b_x,
        "w_slice": L0_ffn_W_slice, "b_slice": L0_ffn_b_slice, "w_q": L0_ffn_W_q, "w_k": L0_ffn_W_k,
        "w_v": L0_ffn_W_v, "w_out": L0_ffn_W_out, "b_out": L0_ffn_b_out, "temp": L0_ffn_temperature,
    }
    nc = bacc.Bacc("TRN2", target_bir_lowering=False, num_devices=1)
    feed, aps = {}, {}
    for name, a in arrays.items():
        a = np.ascontiguousarray(a)
        feed[f"in_{name}"] = a
        aps[name] = nc.dram_tensor(f"in_{name}", a.shape, mybir.dt.from_np(a.dtype), kind="ExternalInput").ap()
    aps["out"] = nc.dram_tensor("out_0", (NP, D), F32, kind="ExternalOutput").ap()
    program(nc, **aps)
    r = run_bass_kernel_spmd(nc, [feed], core_ids=[0])
    return r.results[0]["out_0"][:N]
```
